# Optimizing a Trainium2 kernel written in Bass

```python
import numpy as np
import jax
import jax.numpy as jnp

def _softmax(x, axis=-1):
    return jax.nn.softmax(x, axis=axis)

def _gelu(x):
    return jax.nn.gelu(x, approximate=True)

def _silu(x):
    return jax.nn.silu(x)

def _sigmoid(x):
    return jax.nn.sigmoid(x)

def _layernorm(x, axis=-1, eps=1e-05):
    m = jnp.mean(x, axis=axis, keepdims=True)
    v = jnp.var(x, axis=axis, keepdims=True)
    return (x - m) / jnp.sqrt(v + eps)

def _scatter_add(tgt, idx, src, axis=0):
    return tgt.at[idx].add(src)

def _segment_sum(src, seg, n):
    return jax.ops.segment_sum(src, seg, n)
kernel_name = 'mk_adaln_d2_jaxref_r8_9ef1ff'

def setup_inputs(seed: int=0):
    np.random.seed(seed)
    _w = jnp.asarray

    def _L0_attn_setup():
        import jax, jax.numpy as jnp
        import numpy as np
        DIM = 128
        HEADS = 16
        DIM_HEAD = DIM // HEADS
        LATENT = DIM // 4
        SCALE = DIM_HEAD ** (-0.5)
        key = jax.random.key(seed)
        ks = jax.random.split(key, 8)
        B, S = (2, 256)
        init = lambda k, shape, fan_in: jax.random.normal(k, shape, jnp.float32) * fan_in ** (-0.5)
        return {'x': jax.random.normal(ks[0], (B, S, DIM), jnp.float32), 'Wq': init(ks[1], (DIM, DIM), DIM), 'bq': jnp.zeros((DIM,), jnp.float32), 'Wl': init(ks[2], (DIM, LATENT), DIM), 'bl': jnp.zeros((LATENT,), jnp.float32), 'Wk': init(ks[3], (LATENT, DIM), LATENT), 'bk': jnp.zeros((DIM,), jnp.float32), 'Wv': init(ks[4], (LATENT, DIM), LATENT), 'bv': jnp.zeros((DIM,), jnp.float32), 'Wo': init(ks[5], (DIM, DIM), DIM), 'bo': jnp.zeros((DIM,), jnp.float32)}
    _L0_attn_in = _L0_attn_setup()

    def _L0_ffn_setup():
        import jax, jax.numpy as jnp
        import numpy as np
        B, S, D, F, E, K = (4, 256, 128, 512, 8, 2)
        key = jax.random.key(seed)
        ks = jax.random.split(key, 8)
        x = jax.random.normal(ks[0], (B, S, D), dtype=jnp.float32)
        router_w = jax.random.normal(ks[1], (E, D), dtype=jnp.float32) * 0.02
        w1_w = jax.random.normal(ks[2], (E, F, D), dtype=jnp.float32) * 0.02
        w1_b = jax.random.normal(ks[3], (E, F), dtype=jnp.float32) * 0.02
        w2_w = jax.random.normal(ks[4], (E, D, F), dtype=jnp.float32) * 0.02
        w2_b = jax.random.normal(ks[5], (E, D), dtype=jnp.float32) * 0.02
        wg_w = jax.random.normal(ks[6], (E, F, D), dtype=jnp.float32) * 0.02
        wg_b = jax.random.normal(ks[7], (E, F), dtype=jnp.float32) * 0.02
        return {'x': x, 'router_w': router_w, 'w1_w': w1_w, 'w1_b': w1_b, 'w2_w': w2_w, 'w2_b': w2_b, 'wg_w': wg_w, 'wg_b': wg_b}
    _L0_ffn_in = _L0_ffn_setup()
    _L0_c = _w((lambda *s: np.random.randn(*s).astype(np.float32) * 0.05)(2, 128))
    _L0_wmod = _w((lambda *s: np.random.randn(*s).astype(np.float32) * 0.05)(128, 6 * 128) * 128 ** (-0.5))

    def _L1_attn_setup():
        import jax, jax.numpy as jnp
        import numpy as np
        NUM_HEADS = 16
        D_MODEL = 128
        HEAD_DIM = D_MODEL // NUM_HEADS
        EPS = 1e-06

        def _feature_map(x):
            return jax.nn.elu(x) + 1.0
        key = jax.random.key(seed)
        ks = jax.random.split(key, 9)
        B, S, D = (4, 1024, D_MODEL)
        scale = 1.0 / np.sqrt(D)
        inputs_q = jax.random.normal(ks[0], (B, S, D), dtype=jnp.float32)
        Wq = jax.random.normal(ks[1], (D, D), dtype=jnp.float32) * scale
        Wk = jax.random.normal(ks[2], (D, D), dtype=jnp.float32) * scale
        Wv = jax.random.normal(ks[3], (D, D), dtype=jnp.float32) * scale
        Wo = jax.random.normal(ks[4], (D, D), dtype=jnp.float32) * scale
        bq = jnp.zeros((D,), jnp.float32)
        bk = jnp.zeros((D,), jnp.float32)
        bv = jnp.zeros((D,), jnp.float32)
        bo = jnp.zeros((D,), jnp.float32)
        return {'inputs_q': inputs_q, 'Wq': Wq, 'bq': bq, 'Wk': Wk, 'bk': bk, 'Wv': Wv, 'bv': bv, 'Wo': Wo, 'bo': bo}
    _L1_attn_in = _L1_attn_setup()

    def _L1_ffn_setup():
        import jax, jax.numpy as jnp
        import numpy as np
        D_MODEL = 128
        N_EXPERTS = 8
        TOP_K = 2
        HIDDEN = 4 * D_MODEL
        key = jax.random.key(seed)
        ks = jax.random.split(key, 6)
        B, S = (2, 256)
        x = jax.random.normal(ks[0], (B, S, D_MODEL), dtype=jnp.float32)
        shared_w1 = jax.random.normal(ks[1], (HIDDEN, D_MODEL), dtype=jnp.float32) * 0.02
        shared_w2 = jax.random.normal(ks[2], (D_MODEL, HIDDEN), dtype=jnp.float32) * 0.02
        experts_w1 = jax.random.normal(ks[3], (N_EXPERTS, HIDDEN, D_MODEL), dtype=jnp.float32) * 0.02
        experts_w2 = jax.random.normal(ks[4], (N_EXPERTS, D_MODEL, HIDDEN), dtype=jnp.float32) * 0.02
        gate_w = jax.random.normal(ks[5], (N_EXPERTS, D_MODEL), dtype=jnp.float32) * 0.02
        return {'x': x, 'shared_w1': shared_w1, 'shared_w2': shared_w2, 'experts_w1': experts_w1, 'experts_w2': experts_w2, 'gate_w': gate_w}
    _L1_ffn_in = _L1_ffn_setup()
    _L1_c = _w((lambda *s: np.random.randn(*s).astype(np.float32) * 0.05)(2, 128))
    _L1_wmod = _w((lambda *s: np.random.randn(*s).astype(np.float32) * 0.05)(128, 6 * 128) * 128 ** (-0.5))
    _d = {'L0_attn_x': _L0_attn_in['x'], 'L0_attn_Wq': _L0_attn_in['Wq'], 'L0_attn_bq': _L0_attn_in['bq'], 'L0_attn_Wl': _L0_attn_in['Wl'], 'L0_attn_bl': _L0_attn_in['bl'], 'L0_attn_Wk': _L0_attn_in['Wk'], 'L0_attn_bk': _L0_attn_in['bk'], 'L0_attn_Wv': _L0_attn_in['Wv'], 'L0_attn_bv': _L0_attn_in['bv'], 'L0_attn_Wo': _L0_attn_in['Wo'], 'L0_attn_bo': _L0_attn_in['bo'], 'L0_ffn_router_w': _L0_ffn_in['router_w'], 'L0_ffn_w1_w': _L0_ffn_in['w1_w'], 'L0_ffn_w1_b': _L0_ffn_in['w1_b'], 'L0_ffn_w2_w': _L0_ffn_in['w2_w'], 'L0_ffn_w2_b': _L0_ffn_in['w2_b'], 'L0_ffn_wg_w': _L0_ffn_in['wg_w'], 'L0_ffn_wg_b': _L0_ffn_in['wg_b'], 'L0_c': _L0_c, 'L0_wmod': _L0_wmod, 'L1_attn_Wq': _L1_attn_in['Wq'], 'L1_attn_bq': _L1_attn_in['bq'], 'L1_attn_Wk': _L1_attn_in['Wk'], 'L1_attn_bk': _L1_attn_in['bk'], 'L1_attn_Wv': _L1_attn_in['Wv'], 'L1_attn_bv': _L1_attn_in['bv'], 'L1_attn_Wo': _L1_attn_in['Wo'], 'L1_attn_bo': _L1_attn_in['bo'], 'L1_ffn_shared_w1': _L1_ffn_in['shared_w1'], 'L1_ffn_shared_w2': _L1_ffn_in['shared_w2'], 'L1_ffn_experts_w1': _L1_ffn_in['experts_w1'], 'L1_ffn_experts_w2': _L1_ffn_in['experts_w2'], 'L1_ffn_gate_w': _L1_ffn_in['gate_w'], 'L1_c': _L1_c, 'L1_wmod': _L1_wmod}
    _x0 = _d['L0_attn_x']
    _d['L0_attn_x'] = jax.random.normal(jax.random.fold_in(jax.random.key(seed), 1), (2, 1024, 128), dtype=_x0.dtype)
    del _x0
    return _d

def reference(L0_attn_x, L0_attn_Wq, L0_attn_bq, L0_attn_Wl, L0_attn_bl, L0_attn_Wk, L0_attn_bk, L0_attn_Wv, L0_attn_bv, L0_attn_Wo, L0_attn_bo, L0_ffn_router_w, L0_ffn_w1_w, L0_ffn_w1_b, L0_ffn_w2_w, L0_ffn_w2_b, L0_ffn_wg_w, L0_ffn_wg_b, L0_c, L0_wmod, L1_attn_Wq, L1_attn_bq, L1_attn_Wk, L1_attn_bk, L1_attn_Wv, L1_attn_bv, L1_attn_Wo, L1_attn_bo, L1_ffn_shared_w1, L1_ffn_shared_w2, L1_ffn_experts_w1, L1_ffn_experts_w2, L1_ffn_gate_w, L1_c, L1_wmod):

    def _L0_attn_ref(x, Wq, bq, Wl, bl, Wk, bk, Wv, bv, Wo, bo):
        import jax, jax.numpy as jnp
        import numpy as np
        DIM = 128
        HEADS = 16
        DIM_HEAD = DIM // HEADS
        LATENT = DIM // 4
        SCALE = DIM_HEAD ** (-0.5)
        B, S, D = x.shape
        H, Dh = (HEADS, DIM_HEAD)
        q = (x @ Wq + bq).reshape(B, S, H, Dh)
        latent = x @ Wl + bl
        k = (latent @ Wk + bk).reshape(B, S, H, Dh)
        v = (latent @ Wv + bv).reshape(B, S, H, Dh)
        scores = jnp.einsum('bihd,bjhd->bhij', q, k) * SCALE
        attn = jax.nn.softmax(scores, axis=-1)
        out = jnp.einsum('bhij,bjhd->bihd', attn, v).reshape(B, S, D)
        out = out @ Wo + bo
        return out

    def _L0_ffn_ref(x, router_w, w1_w, w1_b, w2_w, w2_b, wg_w, wg_b):
        import jax, jax.numpy as jnp
        import numpy as np
        B, S, D, F, E, K = (4, 256, 128, 512, 8, 2)
        probs = jax.nn.softmax(jnp.einsum('bsd,ed->bse', x, router_w), axis=-1)
        token_probs, probs_idx = jax.lax.top_k(probs, K)
        gates = jnp.sum(token_probs[..., None] * jax.nn.one_hot(probs_idx, E, dtype=x.dtype), axis=-2)
        gates_e = jnp.moveaxis(gates, -1, 0)

        def body(acc, params):
            w1w, w1b, w2w, w2b, wgw, wgb, g = params
            y = jax.nn.gelu(jnp.einsum('bsd,fd->bsf', x, wgw) + wgb, approximate=False)
            h = y * (jnp.einsum('bsd,fd->bsf', x, w1w) + w1b)
            out = jnp.einsum('bsf,df->bsd', h, w2w) + w2b
            return (acc + out * g[..., None], None)
        acc0 = jnp.zeros_like(x)
        out, _ = jax.lax.scan(body, acc0, (w1_w, w1_b, w2_w, w2_b, wg_w, wg_b, gates_e))
        return out

    def _L1_attn_ref(inputs_q, Wq, bq, Wk, bk, Wv, bv, Wo, bo):
        import jax, jax.numpy as jnp
        import numpy as np
        NUM_HEADS = 16
        D_MODEL = 128
        HEAD_DIM = D_MODEL // NUM_HEADS
        EPS = 1e-06

        def _feature_map(x):
            return jax.nn.elu(x) + 1.0
        B, S, D = inputs_q.shape
        H, Dh = (NUM_HEADS, HEAD_DIM)
        q = (inputs_q @ Wq + bq).reshape(B, S, H, Dh)
        k = (inputs_q @ Wk + bk).reshape(B, S, H, Dh)
        v = (inputs_q @ Wv + bv).reshape(B, S, H, Dh)
        q = _feature_map(q)
        k = _feature_map(k)
        kv = jnp.einsum('bkhd,bkhm->bhdm', k, v)
        out = jnp.einsum('bqhd,bhdm->bqhm', q, kv)
        normalizer = jnp.einsum('bqhd,bkhd->bqh', q, k)
        normalizer = jnp.maximum(normalizer, EPS)
        out = out / normalizer[..., None]
        out = out.reshape(B, S, D)
        return out @ Wo + bo

    def _L1_ffn_ref(x, shared_w1, shared_w2, experts_w1, experts_w2, gate_w):
        import jax, jax.numpy as jnp
        import numpy as np
        D_MODEL = 128
        N_EXPERTS = 8
        TOP_K = 2
        HIDDEN = 4 * D_MODEL
        B, S, D = x.shape
        T = B * S
        x_flat = x.reshape(T, D)
        shared = jnp.einsum('td,dh->th', x_flat, shared_w1.T)
        shared = jnp.einsum('th,hd->td', jax.nn.silu(shared), shared_w2.T)
        gate_logits = x_flat @ gate_w.T
        top_k_gates, top_k_idx = jax.lax.top_k(gate_logits, TOP_K)
        top_k_gates = jax.nn.softmax(top_k_gates, axis=1)
        gates = jnp.zeros((T, N_EXPERTS), dtype=x.dtype)
        gates = gates.at[jnp.arange(T)[:, None], top_k_idx].set(top_k_gates)
        h = jnp.einsum('td,ehd->teh', x_flat, experts_w1)
        expert_out = jnp.einsum('teh,edh->ted', jax.nn.silu(h), experts_w2)
        selected = jnp.einsum('ted,te->td', expert_out, gates)
        return (shared + selected).reshape(B, S, D)
    x = L0_attn_x
    mod = (_silu(L0_c) @ L0_wmod).reshape(L0_c.shape[0], 6, 1, -1)
    sa, ca, ga, sb, cb, gb = (mod[:, 0], mod[:, 1], mod[:, 2], mod[:, 3], mod[:, 4], mod[:, 5])
    ga = (2 * (ga >= 0) - 1) * jnp.maximum(jnp.abs(ga), 0.25)
    gb = (2 * (gb >= 0) - 1) * jnp.maximum(jnp.abs(gb), 0.25)
    h = _layernorm(x, axis=-1) * (1 + ca) + sa
    x = x + ga * _L0_attn_ref(h, L0_attn_Wq, L0_attn_bq, L0_attn_Wl, L0_attn_bl, L0_attn_Wk, L0_attn_bk, L0_attn_Wv, L0_attn_bv, L0_attn_Wo, L0_attn_bo)
    h = _layernorm(x, axis=-1) * (1 + cb) + sb
    x = x + gb * _L0_ffn_ref(h, L0_ffn_router_w, L0_ffn_w1_w, L0_ffn_w1_b, L0_ffn_w2_w, L0_ffn_w2_b, L0_ffn_wg_w, L0_ffn_wg_b)
    mod = (_silu(L1_c) @ L1_wmod).reshape(L1_c.shape[0], 6, 1, -1)
    sa, ca, ga, sb, cb, gb = (mod[:, 0], mod[:, 1], mod[:, 2], mod[:, 3], mod[:, 4], mod[:, 5])
    ga = (2 * (ga >= 0) - 1) * jnp.maximum(jnp.abs(ga), 0.25)
    gb = (2 * (gb >= 0) - 1) * jnp.maximum(jnp.abs(gb), 0.25)
    h = _layernorm(x, axis=-1) * (1 + ca) + sa
    x = x + ga * _L1_attn_ref(h, L1_attn_Wq, L1_attn_bq, L1_attn_Wk, L1_attn_bk, L1_attn_Wv, L1_attn_bv, L1_attn_Wo, L1_attn_bo)
    h = _layernorm(x, axis=-1) * (1 + cb) + sb
    x = x + gb * _L1_ffn_ref(h, L1_ffn_shared_w1, L1_ffn_shared_w2, L1_ffn_experts_w1, L1_ffn_experts_w2, L1_ffn_gate_w)
    return x

_drawn_inputs = setup_inputs


def setup_inputs(seed=0):
    import zlib

    import numpy as np

    out = dict(_drawn_inputs(seed))
    spreads = {'L0_attn_bq': (0.0, 0.8),
     'L0_attn_bl': (0.0, 0.33),
     'L0_attn_bk': (0.0, 0.8),
     'L0_attn_bv': (0.0, 0.363),
     'L0_attn_bo': (0.0, 0.314),
     'L1_attn_bq': (0.0, 0.8),
     'L1_attn_bk': (0.0, 0.8),
     'L1_attn_bv': (0.0, 0.296),
     'L1_attn_bo': (0.0, 0.342)}
    factors = {'L0_ffn_router_w': 8.0,
     'L0_ffn_w1_w': 8.0,
     'L0_ffn_w1_b': 8.0,
     'L0_ffn_w2_w': 8.0,
     'L0_ffn_w2_b': 8.0,
     'L0_ffn_wg_w': 8.0,
     'L0_ffn_wg_b': 8.0,
     'L1_attn_Wq': 8.0,
     'L1_attn_Wk': 8.0,
     'L1_attn_Wv': 3.37,
     'L1_ffn_shared_w1': 4.168,
     'L1_ffn_shared_w2': 3.977,
     'L1_ffn_experts_w1': 6.174,
     'L1_ffn_experts_w2': 6.124,
     'L1_ffn_gate_w': 7.131}
    for name, (base, spread) in spreads.items():
        noise = np.random.default_rng([zlib.crc32(name.encode()), seed]).standard_normal(out[name].shape)
        drawn = base * np.exp(spread * noise) if base else spread * noise
        out[name] = jnp.asarray(drawn.astype(out[name].dtype))
    for name, factor in factors.items():
        out[name] = (out[name] * factor).astype(out[name].dtype)
    return out
```

```python
from contextlib import ExitStack

import numpy as np

import concourse.bass as bass
from concourse import mybir

F32 = mybir.dt.float32
BF16 = mybir.dt.bfloat16
ALU = mybir.AluOpType
ACT = mybir.ActivationFunctionType
AX = mybir.AxisListType

P = 128
B, S = 2, 1024
T = B * S
NT = T // P
BT = S // P
HEADS, DH = 16, 8
HG = 4
GB = HEADS // HG
NG = B * GB
LAT = 32
E, FF = 8, 512
FC = FF // P
HALF = 512
NH = T // HALF
PIECES = 3
KR = PIECES * PIECES * DH
KM = KR + PIECES
SCALE = float(DH) ** -0.5
EPS_LN = 1e-5
EPS_NORM = 1e-6
BIG = 1e30
SAFE_SCORE = 60.0

C_ID, C_BLOCK, C_SEL, C_IOTA = 0, 128, 256, 384
C_HEAD = C_IOTA + BT * E
C_END = C_HEAD + HEADS
(V_BQ0, V_BK0, V_BL0, V_BQ1, V_CT) = (0, 1, 2, 3, 4)
V_EPS = V_CT + 2 * B
V_END = V_EPS + 1
R_BV0, R_BKV1, R_BO1 = 0, 128, 384
R_END = 512
(A_WQ0, A_WL0, A_RT0, A_WQ1, A_WKV1, A_WO1, A_RT1) = (0, 128, 160, 168, 296, 552, 680)
A_END = 688
W0_W = 3 * FF + 2 * FC
W1_W = 2 * FF


def build(nc, x_in, consts_in, vecs_in, rows_in, attnw_in, lowrank_in, wo0_in, wmod_in, w2b_in, exp0_in,
          shared1_in, exp1_in, out):
    q_scr = nc.dram_tensor("q_pieces", [NG, KM, HG * S], BF16, kind="Internal").ap()
    k_scr = nc.dram_tensor("k_pieces", [NG, KM, HG * S], BF16, kind="Internal").ap()

    with ExitStack() as ctx:
        def sb(name, shape, dt=F32):
            return ctx.enter_context(nc.sbuf_tensor(name, shape, dt))

        def ps(name, shape):
            return ctx.enter_context(nc.psum_tensor(name, shape, F32))

        def sem(name):
            return ctx.enter_context(nc.semaphore(name))

        SAB = [ps("bank01", [P, 2 * HALF]), ps("bank23", [P, 2 * HALF])]
        B4, B5, B6, B7 = (ps(f"bank{i}", [P, HALF]) for i in (4, 5, 6, 7))

        consts = sb("consts", [P, C_END])
        ident = consts[:, C_ID:C_ID + P]
        block_mask = consts[:, C_BLOCK:C_BLOCK + P]
        den_sel = consts[:, C_SEL:C_SEL + P]
        iota = consts[:, C_IOTA:C_IOTA + BT * E].rearrange("p (t e) -> p t e", e=E)
        vecs = sb("vecs", [P, V_END])
        rows = sb("rows", [P, R_END])
        attnw = sb("attnw", [P, A_END])
        lowrank = sb("lowrank", [LAT, 2 * P])
        wo0 = sb("wo0", [P, GB, P])
        wo0g = sb("wo0g", [P, B, GB, P])
        wo1g = sb("wo1g", [P, B, P])
        bo1g = sb("bo1g", [P, B, P])
        wmod = sb("wmod", [P, 2, 6 * P])
        w2b = sb("w2b", [E, P])
        silu_c = sb("silu_c", [P, 2 * B])
        silu_cb = sb("silu_cb", [P, 2 * B, P])
        modc = sb("modc", [P, 2, 6, B])
        gmod = sb("gmod", [P, 2, 2, B, P])

        norms = sb("norms", [HEADS, B, 2, 2])
        norm_s = sb("norm_s", [HEADS, 4])
        worst = sb("worst", [1, 2])
        need_max = sb("need_max", [1, 1], mybir.dt.int32)

        X = sb("X", [P, NT, P])
        hT = sb("hT", [P, T])
        XN = sb("XN", [P, BT, P])
        GT = sb("GT", [P, E + 1, NT])
        stats = sb("stats", [P, BT, 6])
        mv = sb("mv", [P, BT, 2])
        sd = sb("sd", [P, BT])
        rstd = sb("rstd", [P, BT])
        latT = sb("latT", [LAT, S])
        V_all = sb("V_all", [P, NG, BT, HG, DH])
        Vg = sb("Vg", [P, 2, BT, HG, 32])
        Kb = sb("Kb", [P, 2, HG * S], BF16)
        Qb = sb("Qb", [P, 2, HG * S], BF16)
        PV_sb = sb("PV_sb", [P, 2, HALF])
        den_r = sb("den_r", [P, HALF])
        mx = sb("mx", [P, 2, HG * BT])
        mneg = sb("mneg", [HG * BT, P])
        mres = sb("mres", [HG * BT, P])
        m3 = sb("m3", [HG * BT, 2, PIECES, P], BF16)
        gate_w = sb("gate_w", [P, 12, BT, E])
        gate_s = sb("gate_s", [P, 8, BT])
        gT = sb("gT", [E, S])
        Wb = [sb(f"Wb{i}", [P, W0_W]) for i in range(2)]
        Wsh = sb("Wsh", [P, W1_W])

        R1 = sb("R1", [P, 10240])
        qk32 = R1[:, 0:4 * S].rearrange("p (b n t) -> p b n t", b=B, n=2)
        pieces = R1[:, 4 * S:10 * S].bitcast(BF16).rearrange("p (b n j t) -> p b n j t", b=B, n=2, j=PIECES)
        At = R1[:, 0:NG * S].rearrange("p (g t) -> p g t", g=NG)
        ZQ, TQ, QF, OT = (R1[:, i * S:(i + 1) * S] for i in range(4))
        TK = R1[:, 4 * S:5 * S].rearrange("p (i d) -> p i d", i=BT)
        KF = R1[:, 5 * S:6 * S].rearrange("p (i d) -> p i d", i=BT)
        NRM = R1[:, 6 * S:7 * S]
        KVW = 2 * P + 4
        KVt = R1[:, 7 * S:7 * S + BT * KVW].rearrange("p (i d) -> p i d", i=BT)
        KVB = R1[:, 9 * S + 512:9 * S + 512 + 2 * P]
        R2 = sb("R2", [P, 8192])
        PR = R2[:, :].rearrange("p (n h t) -> p n h t", n=4, h=HG)
        H = R2[:, 0:2 * FC * HALF].rearrange("p (n f t) -> p n f t", n=2, f=FC)
        Y = R2[:, 2 * FC * HALF:2 * FC * HALF + 2 * HALF].rearrange("p (n t) -> p n t", n=2)
        ACC = R2[:, 5120:5120 + NT * P].rearrange("p (i d) -> p i d", d=P)
        gsign = R2[:, 5120:5120 + 2 * 2 * B * P]
        SQ = R2[:, 6144:8192].rearrange("p (n t) -> p n t", n=2)
        zero_one = R2[:, 0:4096].bitcast(BF16).rearrange("p (n t) -> p n t", n=2)

        s_x, s_small, s_wts = sem("x_loaded"), sem("small_loaded"), sem("wts_loaded")
        s_w = [sem("expert_even_loaded"), sem("expert_odd_loaded")]
        s_wsh = sem("shared_loaded")
        s_dve, s_act, s_pool = sem("dve_chain"), sem("act_chain"), sem("pool_chain")
        s_silu, s_scb, s_modmm, s_mod = sem("silu_c_ready"), sem("silu_cb_ready"), sem("mod_products"), sem("mod_ready")
        s_var, s_sd, s_xn, s_tr, s_ht = (sem(n) for n in ("var_ready", "sd_ready", "xn_ready", "xn_turned", "ht_ready"))
        s_lat, s_latsb, s_qmm, s_kmm, s_vmm = (sem(n) for n in ("lat_mm", "lat_ready", "q_mm", "k_mm", "v_mm"))
        s_qk, s_v, s_pc = sem("qk_evacuated"), sem("v_ready"), sem("pieces_ready")
        s_sq, s_nb, s_nr, s_nt, s_ntr, s_flag = (sem(n) for n in (
            "squares_ready", "norms_summed", "norms_taken", "norm_bound", "norm_bound_turned", "need_max_ready"))
        s_zo, s_scr = sem("zero_one_ready"), sem("pieces_stored")
        s_scr2 = [sem("max_rows_even_stored"), sem("max_rows_odd_stored")]
        s_kq = [sem("kq_even_loaded"), sem("kq_odd_loaded")]
        s_mm, s_mred, s_mtr, s_mev, s_m3, s_m3c = (sem(n) for n in ("max_scores", "max_taken", "max_turned", "max_evac", "max_split", "max_split_chain"))
        s_kqm = [sem("max_kq_even_loaded"), sem("max_kq_odd_loaded")]
        s_vz, s_vg = sem("vg_padding_ready"), sem("vg_ready")
        s_st, s_ex, s_pv, s_pve, s_den, s_denr, s_at = (sem(n) for n in (
            "scores_ready", "probs_ready", "pv_done", "pv_evacuated", "den_spread", "den_recip", "attn_normed"))
        s_wog, s_wo, s_res = sem("wo_scaled"), sem("wo_done"), sem("mixture_added")
        s_lg, s_gx, s_ge, s_gate, s_gtr, s_gts, s_b2 = (sem(n) for n in (
            "logits_ready", "gate_exp_in", "gate_exp_out", "gates_ready", "gates_turned", "gates_t_ready", "bias2_ready"))
        s_acc0 = sem("acc_started")
        s_gm = [sem(f"gate_mm{i}") for i in range(2)]
        s_um = sem("up_mm")
        s_y = [sem(f"act_out{i}") for i in range(2)]
        s_h = sem("hidden_ready")
        s_o = [sem(f"down_mm{i}") for i in range(2)]
        s_ac = [sem(f"acc_done{i}") for i in range(2)]
        s_q1, s_kv1, s_tq, s_eq, s_qf, s_kf, s_kvm, s_kvb, s_nn, s_ot = (sem(n) for n in (
            "q1_mm", "kv1_mm", "t1_ready", "e1_ready", "qf_ready", "kf_ready", "kv_sum", "kv_masked", "num_norm", "ot_ready"))
        s_out = sem("out_stored")

        SMALL = 5
        WTS = 3
        ATT_UNITS = 2 * BT

        block = ctx.enter_context(nc.Block())

        @block.sync
        def _(sp):
            sp.dma_start(vecs[:, :], vecs_in).then_inc(s_small, 16)
            sp.dma_start(wmod[:, :, :], wmod_in).then_inc(s_small, 16)
            sp.dma_start(consts[:, :], consts_in).then_inc(s_small, 16)
            sp.dma_start(rows[:, :], rows_in).then_inc(s_small, 16)
            sp.dma_start(w2b[:, :], w2b_in).then_inc(s_small, 16)
            for b in range(B):
                sp.dma_start(X[:, b * BT:(b + 1) * BT, :], x_in[b].rearrange("(i p) d -> p i d", p=P)).then_inc(s_x, 16)
            sp.dma_start(attnw[:, :], attnw_in).then_inc(s_wts, 16)
            sp.dma_start(lowrank[:, :], lowrank_in).then_inc(s_wts, 16)
            sp.dma_start(wo0[:, :, :], wo0_in).then_inc(s_wts, 16)
            for k in range(2):
                sp.dma_start(Wb[k][:, :], exp0_in[k]).then_inc(s_w[k], 16)
            sp.dma_start(Wsh[:, :], shared1_in).then_inc(s_wsh, 16)
            sp.wait_ge(s_zo, 2)
            sp.dma_start(q_scr[:, KR:KM, :], zero_one[0:NG * PIECES, 0, :]).then_inc(s_scr, 16)
            sp.dma_start(k_scr[:, KR:KM, :], zero_one[0:NG * PIECES, 1, :]).then_inc(s_scr, 16)
            for b in range(B):
                for n, scr in enumerate((q_scr, k_scr)):
                    sp.wait_ge(s_pc, 2 * b + n + 1)
                    for piece in range(PIECES):
                        for rep in range(PIECES):
                            r = (rep * PIECES + piece if n == 0 else piece * PIECES + rep) * DH
                            sp.dma_start(scr[b * GB:(b + 1) * GB, r:r + DH, :].rearrange("g d (h t) -> g (d h) t", h=HG),
                                         pieces[:, b, n, piece, :]).then_inc(s_scr, 16)
            stores = 2 + B * 2 * PIECES * PIECES
            sp.wait_ge(s_scr, 16 * stores)

            sp.wait_ge(s_flag, 1)
            flag = sp.value_load(need_max[0:1, 0:1], min_val=0, max_val=1)
            with sp.If(flag != 0):
                for k in range(2):
                    sp.dma_start(Kb[0:KR, k, :], k_scr[k, 0:KR, :]).then_inc(s_kqm[k], 16)
                    sp.dma_start(Qb[0:KR, k, :], q_scr[k, 0:KR, :]).then_inc(s_kqm[k], 16)
                with sp.Fori(1, NG // 2) as i:
                    for k in range(2):
                        sp.wait_ge(s_mm, (i * 2 + (k - 1)) * (HG * BT))
                        sp.dma_start(Kb[0:KR, k, :], k_scr[bass.ds(i * 2 + k, 1), 0:KR, :].rearrange("g r t -> (g r) t")).then_inc(s_kqm[k], 16)
                        sp.dma_start(Qb[0:KR, k, :], q_scr[bass.ds(i * 2 + k, 1), 0:KR, :].rearrange("g r t -> (g r) t")).then_inc(s_kqm[k], 16)
                for k in range(2):
                    sp.wait_ge(s_scr2[k], 16 * (NG // 2 + 1))
                sp.wait_ge(s_mm, NG * HG * BT)
            for k in range(2):
                sp.dma_start(Kb[0:KM, k, :], k_scr[k, :, :]).then_inc(s_kq[k], 16)
                sp.dma_start(Qb[0:KM, k, :], q_scr[k, :, :]).then_inc(s_kq[k], 16)
            with sp.Fori(1, NG // 2) as i:
                for k in range(2):
                    sp.wait_ge(s_st, (i * 2 + (k - 1)) * (2 * ATT_UNITS))
                    sp.dma_start(Kb[0:KM, k, :], k_scr[bass.ds(i * 2 + k, 1), :, :].rearrange("g r t -> (g r) t")).then_inc(s_kq[k], 16)
                    sp.dma_start(Qb[0:KM, k, :], q_scr[bass.ds(i * 2 + k, 1), :, :].rearrange("g r t -> (g r) t")).then_inc(s_kq[k], 16)
            with sp.Fori(1, E // 2) as i:
                for k in range(2):
                    sp.wait_ge(s_o[0], (i * 2 + (k - 1)) * NH + 2)
                    sp.dma_start(Wb[k][:, :], exp0_in[bass.ds(i * 2 + k, 1)].rearrange("e p w -> (e p) w")).then_inc(s_w[k], 16)
            for k in range(2):
                sp.wait_ge(s_o[0], (E - 1 + k) * NH + 2)
                sp.dma_start(Wb[k][:, 0:W1_W], exp1_in[k]).then_inc(s_w[k], 16)
            with sp.Fori(1, E // 2) as i:
                for k in range(2):
                    sp.wait_ge(s_o[1], (i * 2 + k) * NH + 2)
                    sp.dma_start(Wb[k][:, 0:W1_W], exp1_in[bass.ds(i * 2 + k, 1)].rearrange("e p w -> (e p) w")).then_inc(s_w[k], 16)
            for b in range(B):
                sp.wait_ge(s_res, B + b + 1)
                sp.dma_start(out[b].rearrange("(i p) d -> p i d", p=P), X[:, b * BT:(b + 1) * BT, :]).then_inc(s_out, 16)
            sp.wait_ge(s_out, 16 * B)

        @block.gpsimd
        def _(pool):
            pool.memset(zero_one[0:NG * PIECES, 0, :], 0.0).then_inc(s_zo, 1)
            pool.memset(zero_one[0:NG * PIECES, 1, :], 1.0).then_inc(s_zo, 1)
            pool.memset(Vg[:, :, :, :, :], 0.0).then_inc(s_vz, 1)
            pool.wait_ge(s_vz, 1)
            pool.memset(Vg[:, :, :, :, DH:DH + 1], 1.0).then_inc(s_vz, 1)
            pool.wait_ge(s_vz, 2)
            pool.wait_ge(s_v, B * 2)
            pool.sem_inc(s_pv, 4)
            for k in range(2):
                pool.tensor_copy(Vg[:, k, :, :, 0:DH], V_all[:, k, :, :, :]).then_inc(s_vg, 1)
            with pool.Fori(1, NG // 2) as i:
                for k in range(2):
                    pool.wait_ge(s_pv, (i * 2 + (k - 1)) * ATT_UNITS + 4)
                    pool.tensor_copy(Vg[:, k, :, :, 0:DH],
                                     V_all[:, bass.ds(i * 2 + k, 1), :, :, :].rearrange("p g i h d -> p (g i) h d")).then_inc(s_vg, 1)

        @block.scalar
        def _(act):
            act.wait_ge(s_small, 16 * SMALL)
            act.activation(silu_c[:, :], vecs[:, V_CT:V_EPS], ACT.Silu).then_inc(s_silu, 1)

            def spread(v):
                act.wait_ge(s_var, v + 1)
                act.activation(sd[:, :], mv[:, :, 1], ACT.Sqrt, bias=vecs[:, V_EPS:V_END]).then_inc(s_sd, 1)

            for b in range(B):
                spread(b)
                for half in range(2):
                    act.wait_ge(s_lat, 2 * b + half + 1)
                    if b and not half:
                        act.wait_ge(s_vmm, 2)
                    act.activation(latT[:, half * HALF:(half + 1) * HALF], (B4, B5)[half][0:LAT, :], ACT.Identity,
                                   bias=vecs[0:LAT, V_BL0:V_BL0 + 1]).then_inc(s_latsb, 1)
                for n in range(2):
                    act.wait_ge(s_qk, 2 * b + n + 1)
                    if b:
                        act.wait_ge(s_nb, 2 * n + 2)
                    act.activation(SQ[:, n, :], SAB[n][:, :], ACT.Square,
                                   bias=vecs[:, V_BQ0 + n:V_BQ0 + n + 1]).then_inc(s_sq, 1)

            act.wait_ge(s_flag, 1)
            flag = act.value_load(need_max[0:1, 0:1], min_val=0, max_val=1)
            with act.If(flag != 0):
                for k in range(2):
                    act.sem_inc(s_scr2[k], 16)
                with act.Fori(0, NG // 2) as i:
                    for k in range(2):
                        act.wait_ge(s_m3, i * 2 + k + 1)
                        act.dma_start(q_scr[bass.ds(i * 2 + k, 1), KR:KM, :].rearrange("g r (x t) -> (g x) r t", t=P),
                                      m3[:, k, :, :]).then_inc(s_scr2[k], 16)

            act.sem_inc(s_ex, 2)
            with act.Fori(0, NG // 2) as i:
                for v in range(2 * ATT_UNITS):
                    n = i * (2 * ATT_UNITS) + v
                    for pair in range(2):
                        act.wait_ge(s_st, n * 2 + (pair + 1))
                        act.wait_ge(s_pv, n + 1)
                        act.activation(PR[:, v % 4, 2 * pair:2 * pair + 2, :], SAB[pair][:, :].rearrange("p (h t) -> p h t", h=2),
                                       ACT.Exp, scale=SCALE).then_inc(s_ex, 1)

            def gate_exp(layer, b):
                j = layer * B + b
                act.wait_ge(s_gx, j + 1)
                if layer == 0:
                    act.activation(gate_w[:, 1], gate_w[:, 0], ACT.Exp).then_inc(s_ge, 1)
                else:
                    act.activation(gate_s[:, 5], gate_s[:, 4], ACT.Exp).then_inc(s_ge, 1)

            def hidden(layer, base, buf, v):
                wb = Wsh if buf == 2 else Wb[buf]
                for f in range(FC):
                    act.wait_ge(s_gm[layer], base * FC + (v * FC + f + 1))
                    if layer == 0:
                        act.wait_ge(s_h, base * FC + (v * FC + f + 1))
                        act.activation(Y[:, f % 2, :], SAB[0][:, (f % 2) * HALF:(f % 2 + 1) * HALF], ACT.Gelu,
                                       bias=wb[:, 3 * FF + f:3 * FF + f + 1]).then_inc(s_y[0], 1)
                    else:
                        if f == 0:
                            act.wait_ge(s_o[1], base + (v + 1))
                        act.activation(H[:, v % 2, f, :], SAB[0][:, (f % 2) * HALF:(f % 2 + 1) * HALF],
                                       ACT.Silu).then_inc(s_y[1], 1)

            for b in range(B):
                spread(B + b)
            for b in range(B):
                gate_exp(0, b)
            act.sem_inc(s_y[0], 2)
            with act.Fori(0, E // 2) as i:
                for v in range(2 * NH):
                    hidden(0, i * (2 * NH), v // NH, v)

            for b in range(B):
                spread(2 * B + b)
                act.wait_ge(s_tq, 2 * b + 1)
                act.activation(TQ, TQ, ACT.Exp).then_inc(s_eq, 1)
                act.wait_ge(s_tq, 2 * b + 2)
                act.activation(TK, TK, ACT.Exp).then_inc(s_eq, 1)
            for b in range(B):
                spread(3 * B + b)
            for b in range(B):
                gate_exp(1, b)
            act.sem_inc(s_y[1], 2)
            for v in range(NH):
                hidden(1, 0, 2, v)
            with act.Fori(0, E // 2) as i:
                for v in range(2 * NH):
                    hidden(1, i * (2 * NH) + NH, v // NH, v)

        @block.vector
        def _(dve):
            count = [0]

            def link(ins):
                count[0] += 1
                ins.then_inc(s_dve, 1)
                dve.wait_ge(s_dve, count[0])

            tt, ts, stt, copy = dve.tensor_tensor, dve.tensor_scalar, dve.scalar_tensor_tensor, dve.tensor_copy

            dve.wait_ge(s_silu, 1)
            copy(silu_cb[:, :, :], silu_c[:, :].unsqueeze(2).to_broadcast([P, 2 * B, P])).then_inc(s_scb, 1)
            dve.wait_ge(s_modmm, 1)
            link(copy(modc[:, :, :, :], B4[:, 0:2 * 6 * B].rearrange("p (l c b) -> p l c b", l=2, c=6)))
            for c in (1, 4):
                link(ts(modc[:, :, c, :], modc[:, :, c, :], 1.0, None, ALU.add))
            gm = gmod[:, :, :, :, :].rearrange("p l k b d -> p (l k b d)")
            link(ts(gsign, SAB[0][:, :], 0.0, None, ALU.is_ge))
            link(ts(gsign, gsign, 2.0, -1.0, ALU.mult, ALU.add))
            link(copy(gm, SAB[0][:, :]))
            link(stt(out=gm, in0=gm, scalar=-1.0, in1=gm, op0=ALU.mult, op1=ALU.max))
            stt(out=gm, in0=gm, scalar=0.25, in1=gsign, op0=ALU.max, op1=ALU.mult).then_inc(s_mod, 1)
            dve.wait_ge(s_mod, 1)
            dve.wait_ge(s_wts, 16 * WTS)
            for b in range(B):
                tt(wo0g[:, b], wo0[:, :, :], gmod[:, 0, 0, b, :].unsqueeze(1).to_broadcast([P, GB, P]), ALU.mult).then_inc(s_wog, 1)
                tt(wo1g[:, b], attnw[:, A_WO1:A_WO1 + P], gmod[:, 1, 0, b, :], ALU.mult).then_inc(s_wog, 1)
                link(tt(bo1g[:, b], rows[:, R_BO1:R_BO1 + P], gmod[:, 1, 0, b, :], ALU.mult))

            def layer_norm(v):
                step, b = divmod(v, B)
                if step == 0:
                    dve.wait_ge(s_x, 16 * (b + 1))
                xb = [X[:, b * BT + i, :] for i in range(BT)]
                for i in range(BT):
                    last = dve.bn_stats(stats[:, i, :], xb[i])
                link(last)
                for i in range(BT):
                    last = dve.bn_aggr(mv[:, i, :], stats[:, i, :])
                last.then_inc(s_var, 1)
                dve.wait_ge(s_sd, v + 1)
                link(dve.reciprocal(rstd[:, :], sd[:, :]))
                if v:
                    dve.wait_ge(s_tr, v)
                for i in range(BT):
                    last = ts(XN[:, i, :], xb[i], mv[:, i, 0:1], rstd[:, i:i + 1], ALU.subtract, ALU.mult)
                last.then_inc(s_xn, 1)
                layer, c = divmod(step, 2)
                dve.wait_ge(s_tr, v + 1)
                for half in range(2):
                    last = ts(hT[:, b * S + half * HALF:b * S + (half + 1) * HALF], (B6, B7)[half][:, :],
                              modc[:, layer, 3 * c + 1, b:b + 1], modc[:, layer, 3 * c, b:b + 1], ALU.mult, ALU.add)
                last.then_inc(s_ht, 1)

            for b in range(B):
                layer_norm(b)
                dve.wait_ge(s_qmm, b + 1)
                ts(qk32[:, b, 0, :], SAB[0][:, :], vecs[:, V_BQ0:V_BQ0 + 1], None, ALU.add).then_inc(s_qk, 1)
                dve.wait_ge(s_kmm, b + 1)
                ts(qk32[:, b, 1, :], SAB[1][:, :], vecs[:, V_BK0:V_BK0 + 1], None, ALU.add).then_inc(s_qk, 1)
                for half in range(2):
                    dve.wait_ge(s_vmm, 2 * b + half + 1)
                    for i in range(BT // 2):
                        last = tt(V_all[:, b * GB:(b + 1) * GB, half * BT // 2 + i, :, :],
                                  (B4, B5)[half][:, i * P:(i + 1) * P].rearrange("p (g h d) -> p g h d", g=GB, h=HG),
                                  rows[:, R_BV0:R_BV0 + P].rearrange("p (g h d) -> p g h d", g=GB, h=HG), ALU.add)
                    last.then_inc(s_v, 1)
                for n in range(2):
                    dve.wait_ge(s_qk, 2 * b + n + 1)
                    z = qk32[:, b, n, :]
                    link(copy(pieces[:, b, n, 0, :], z))
                    link(tt(z, z, pieces[:, b, n, 0, :], ALU.subtract))
                    link(copy(pieces[:, b, n, 1, :], z))
                    link(tt(z, z, pieces[:, b, n, 1, :], ALU.subtract))
                    copy(pieces[:, b, n, 2, :], z).then_inc(s_pc, 1)
                for n in range(2):
                    for half in range(2):
                        dve.wait_ge(s_nb, (2 * b + n) * 2 + half + 1)
                        dve.tensor_reduce(norms[:, b, n, half:half + 1], (B6, B7)[half][0:HEADS, :], AX.X,
                                          ALU.max).then_inc(s_nr, 1)
            dve.wait_ge(s_nr, 4 * B)
            link(dve.tensor_reduce(norm_s[:, :], norms[:, :, :, :].rearrange("p b n h -> p (b n) h"), AX.X, ALU.max))
            for b in range(B):
                last = tt(norms[:, b, 0, 0:1], norm_s[:, 2 * b:2 * b + 1], norm_s[:, 2 * b + 1:2 * b + 2], ALU.mult)
            link(last)
            tt(norm_s[:, 0:1], norms[:, 0, 0, 0:1], norms[:, 1, 0, 0:1], ALU.max).then_inc(s_nt, 1)
            dve.wait_ge(s_ntr, 1)
            link(dve.tensor_reduce(worst[:, 0:1], B6[0:1, 0:HEADS], AX.X, ALU.max))
            link(ts(worst[:, 1:2], worst[:, 0:1], (SAFE_SCORE / SCALE) ** 2, None, ALU.is_le))
            ts(need_max[:, :], worst[:, 1:2], -1.0, 1.0, ALU.mult, ALU.add).then_inc(s_flag, 1)

            dve.wait_ge(s_flag, 1)
            flag = dve.value_load(need_max[0:1, 0:1], min_val=0, max_val=1)
            with dve.If(flag != 0):
                dve.sem_inc(s_mred, 2)
                with dve.Fori(0, NG // 2) as i:
                    for k in range(2):
                        g = i * 2 + k
                        for item in range(HG * BT):
                            dve.wait_ge(s_mm, g * (HG * BT) + (item + 1))
                            dve.tensor_reduce(mx[:, k, item:item + 1], SAB[item % 2][:, :], AX.X, ALU.max).then_inc(s_mred, 1)
                        dve.wait_ge(s_mtr, g + 1)
                        ts(mneg[:, :], B4[0:HG * BT, 0:P], -1.0, None, ALU.mult).then_inc(s_m3c, 1)
                        dve.wait_ge(s_m3c, g * 5 + 1)
                        dve.wait_ge(s_scr2[k], i * 16 + 16)
                        copy(m3[:, k, 0, :], mneg[:, :]).then_inc(s_m3c, 1)
                        dve.wait_ge(s_m3c, g * 5 + 2)
                        tt(mneg[:, :], mneg[:, :], m3[:, k, 0, :], ALU.subtract).then_inc(s_m3c, 1)
                        dve.wait_ge(s_m3c, g * 5 + 3)
                        copy(m3[:, k, 1, :], mneg[:, :]).then_inc(s_m3c, 1)
                        dve.wait_ge(s_m3c, g * 5 + 4)
                        tt(mneg[:, :], mneg[:, :], m3[:, k, 1, :], ALU.subtract).then_inc(s_m3c, 1)
                        dve.wait_ge(s_m3c, g * 5 + 5)
                        copy(m3[:, k, 2, :], mneg[:, :]).then_inc(s_m3, 1)

            dve.sem_inc(s_pve, 2)
            dve.sem_inc(s_denr, 1)
            with dve.Fori(0, NG // 2) as i:
                for k in range(2):
                    g = i * 2 + k
                    for qh in range(2):
                        r = g * 2 + qh
                        dve.wait_ge(s_pv, r * BT + (BT + 4))
                        copy(PV_sb[:, qh, :], (B4, B5)[qh][:, :]).then_inc(s_pve, 1)
                        dve.wait_ge(s_den, r + 1)
                        dve.reciprocal(den_r[:, :], B6[:, :]).then_inc(s_denr, 1)
                        dve.wait_ge(s_denr, r + 2)
                        tt(At[:, bass.ds(g, 1), qh * HALF:(qh + 1) * HALF].rearrange("p g t -> p (g t)"),
                           PV_sb[:, qh, :], den_r[:, :], ALU.mult).then_inc(s_at, 1)

            def residual(j, banks, bias=None):
                b = j % B
                dve.wait_ge(s_wo, j + 1)
                for half in range(2):
                    x = X[:, b * BT + half * BT // 2:b * BT + (half + 1) * BT // 2, :]
                    last = tt(x, x, banks[half].rearrange("p (i d) -> p i d", d=P), ALU.add)
                if bias is not None:
                    link(last)
                    x = X[:, b * BT:(b + 1) * BT, :]
                    last = tt(x, x, bias.unsqueeze(1).to_broadcast([P, BT, P]), ALU.add)
                link(last)

            residual(0, (B4[:, :], B5[:, :]))
            residual(1, (SAB[1][:, 0:HALF], SAB[1][:, HALF:2 * HALF]))

            def wide(col):
                return col.unsqueeze(2).to_broadcast([P, BT, E])

            def gates(layer, b):
                j = layer * B + b
                w = [gate_w[:, i] for i in range(12)]
                s = [gate_s[:, i] for i in range(8)]
                dve.wait_ge(s_lg, j + 1)
                logits = SAB[0][:, b * HALF:b * HALF + BT * E].rearrange("p (t e) -> p t e", e=E)
                if layer == 0:
                    link(dve.tensor_reduce(s[0], logits, AX.X, ALU.max))
                    tt(w[0], logits, wide(s[0]), ALU.subtract).then_inc(s_gx, 1)
                    dve.wait_ge(s_ge, j + 1)
                    link(dve.tensor_reduce(s[1], w[1], AX.X, ALU.add))
                    link(dve.reciprocal(s[2], s[1]))
                    link(tt(w[3], w[1], wide(s[2]), ALU.mult))
                else:
                    link(copy(w[3], logits))
                link(dve.tensor_reduce(s[3], w[3], AX.X, ALU.max))
                link(tt(w[4], w[3], wide(s[3]), ALU.not_equal))
                link(stt(out=w[4], in0=w[4], scalar=100.0, in1=iota, op0=ALU.mult, op1=ALU.add))
                link(dve.tensor_reduce(s[6], w[4], AX.X, ALU.min))
                link(tt(w[5], iota, wide(s[6]), ALU.is_equal))
                link(stt(out=w[6], in0=w[5], scalar=-BIG, in1=w[3], op0=ALU.mult, op1=ALU.add))
                link(dve.tensor_reduce(s[7], w[6], AX.X, ALU.max))
                link(tt(w[7], w[6], wide(s[7]), ALU.not_equal))
                link(stt(out=w[7], in0=w[7], scalar=100.0, in1=iota, op0=ALU.mult, op1=ALU.add))
                link(dve.tensor_reduce(s[6], w[7], AX.X, ALU.min))
                link(tt(w[8], iota, wide(s[6]), ALU.is_equal))
                g1, g2 = s[3], s[7]
                if layer == 1:
                    tt(s[4], s[7], s[3], ALU.subtract).then_inc(s_gx, 1)
                    dve.wait_ge(s_ge, j + 1)
                    link(ts(s[0], s[5], 1.0, None, ALU.add))
                    link(dve.reciprocal(s[1], s[0]))
                    link(tt(s[2], s[5], s[1], ALU.mult))
                    g1, g2 = s[1], s[2]
                link(tt(w[9], w[5], wide(g1), ALU.mult))
                link(tt(w[10], w[8], wide(g2), ALU.mult))
                tt(GT[:, layer:layer + E, b * BT:(b + 1) * BT].rearrange("p e t -> p t e"), w[9], w[10],
                   ALU.add).then_inc(s_gate, 1)
                dve.wait_ge(s_gate, j + 1)

            def hidden(base, buf, v):
                wb = Wb[buf]
                dve.wait_ge(s_o[0], base + (v + 1))
                for f in range(FC):
                    n = base * FC + (v * FC + f + 1)
                    dve.wait_ge(s_um, n)
                    dve.wait_ge(s_y[0], n + 2)
                    stt(out=H[:, v % 2, f, :], in0=SAB[1][:, (f % 2) * HALF:(f % 2 + 1) * HALF],
                        scalar=wb[:, 3 * FF + FC + f:3 * FF + FC + f + 1], in1=Y[:, f % 2, :],
                        op0=ALU.add, op1=ALU.mult).then_inc(s_h, 1)

            def accumulate(layer, base, e, v):
                dve.wait_ge(s_o[layer], base + (v + 3))
                n = v % NH
                for t in range(HALF // P):
                    i = n * (HALF // P) + t
                    gate = (GT[:, e, i:i + 1] if isinstance(e, int) else
                            GT[:, bass.ds(e, 1), i:i + 1].rearrange("p e t -> p (e t)"))
                    last = stt(out=ACC[:, i, :], in0=(B4, B5)[v % 2][:, t * P:(t + 1) * P],
                               scalar=gate, in1=ACC[:, i, :], op0=ALU.mult, op1=ALU.add)
                last.then_inc(s_ac[layer], 1)

            def add_mixture(layer):
                for b in range(B):
                    a, x = ACC[:, b * BT:(b + 1) * BT, :], X[:, b * BT:(b + 1) * BT, :]
                    link(tt(a, a, gmod[:, layer, 1, b, :].unsqueeze(1).to_broadcast([P, BT, P]), ALU.mult))
                    tt(x, x, a, ALU.add).then_inc(s_res, 1)
                    dve.wait_ge(s_res, layer * B + b + 1)

            for b in range(B):
                layer_norm(B + b)
            for b in range(B):
                gates(0, b)
                dve.wait_ge(s_gtr, b + 1)
                copy(gT[:, :], SAB[1][0:E, :]).then_inc(s_gts, 1)
                dve.wait_ge(s_b2, b + 1)
                for half in range(2):
                    last = copy(ACC[:, b * BT + half * BT // 2:b * BT + (half + 1) * BT // 2, :],
                                (B4, B5)[half][:, :].rearrange("p (i d) -> p i d", d=P))
                last.then_inc(s_acc0, 1)
            dve.sem_inc(s_h, 2)
            dve.sem_inc(s_ac[0], 2)
            with dve.Fori(0, E // 2) as i:
                for v in range(2 * NH):
                    hidden(i * (2 * NH), v // NH, v)
                    if v:
                        accumulate(0, i * (2 * NH), i * 2 + (v - 1) // NH, v - 1)
                accumulate(0, i * (2 * NH), i * 2 + 1, 2 * NH - 1)
            dve.wait_ge(s_ac[0], E * NH + 2)
            add_mixture(0)

            link(dve.memset(KVt[:, :, 2 * P:2 * P + 1], 1.0))
            for b in range(B):
                layer_norm(2 * B + b)
                if b:
                    dve.wait_ge(s_wo, B + b)
                dve.wait_ge(s_q1, b + 1)
                link(ts(ZQ, SAB[0][:, :], vecs[:, V_BQ1:V_BQ1 + 1], None, ALU.add))
                ts(TQ, ZQ, 0.0, None, ALU.min).then_inc(s_tq, 1)
                dve.wait_ge(s_kv1, b + 1)
                for src, i0, ni in ((SAB[1], 0, 4), (B4, 4, 2), (B5, 6, 2)):
                    last = tt(KVt[:, i0:i0 + ni, 0:2 * P], src[:, :].rearrange("p (i d) -> p i d", d=2 * P),
                              rows[:, R_BKV1:R_BKV1 + 2 * P].unsqueeze(1).to_broadcast([P, ni, 2 * P]), ALU.add)
                link(last)
                ts(TK, KVt[:, :, 0:P], 0.0, None, ALU.min).then_inc(s_tq, 1)
                dve.wait_ge(s_eq, 2 * b + 1)
                stt(out=QF, in0=ZQ, scalar=0.0, in1=TQ, op0=ALU.max, op1=ALU.add).then_inc(s_qf, 1)
                dve.wait_ge(s_eq, 2 * b + 2)
                stt(out=KF, in0=KVt[:, :, 0:P], scalar=0.0, in1=TK, op0=ALU.max, op1=ALU.add).then_inc(s_kf, 1)
                dve.wait_ge(s_kvm, b + 1)
                tt(KVB[:, 0:P], B6[:, 0:P], block_mask, ALU.mult)
                ts(KVB[:, P:2 * P], block_mask, B6[:, P:P + 1], None, ALU.mult).then_inc(s_kvb, 1)
                dve.wait_ge(s_nn, b + 1)
                link(ts(NRM, SAB[1][:, :], EPS_NORM, None, ALU.max))
                link(dve.reciprocal(NRM, NRM))
                tt(OT, SAB[0][:, :], NRM, ALU.mult).then_inc(s_ot, 1)
                residual(B + b, (B4[:, :], B5[:, :]), bo1g[:, b, :])

            for b in range(B):
                layer_norm(3 * B + b)
            link(dve.memset(GT[:, 0, :], 1.0))
            link(dve.memset(ACC[:, :, :], 0.0))
            for b in range(B):
                gates(1, b)
            dve.sem_inc(s_ac[1], 2)
            for v in range(NH):
                accumulate(1, 0, 0, v)
            with dve.Fori(0, E // 2) as i:
                for v in range(2 * NH):
                    accumulate(1, i * (2 * NH) + NH, i * 2 + (1 + v // NH), v)
            dve.wait_ge(s_ac[1], (E + 1) * NH + 2)
            add_mixture(1)

        @block.tensor
        def _(pe):
            mm = pe.matmul
            pe.wait_ge(s_small, 16 * SMALL)
            pe.wait_ge(s_silu, 1)
            for l in range(2):
                for c in range(6):
                    o = (l * 6 + c) * B
                    mm(B4[:, o:o + B], wmod[:, l, c * P:(c + 1) * P], silu_c[:, l * B:(l + 1) * B], start=True, stop=True)
            pe.wait_ge(s_scb, 1)
            for l in range(2):
                for kind in range(2):
                    for b in range(B):
                        o = ((l * 2 + kind) * B + b) * P
                        last = mm(SAB[0][:, o:o + P], silu_cb[:, l * B + b, :], wmod[:, l, (3 * kind + 2) * P:(3 * kind + 3) * P],
                                  start=True, stop=True)
            last.then_inc(s_modmm, 1)

            def turn(v):
                pe.wait_ge(s_xn, v + 1)
                if v == 1:
                    pe.wait_ge(s_nr, 4)
                if v:
                    pe.wait_ge(s_ht, v)
                for i in range(BT):
                    last = pe.transpose((B6, B7)[i // 4][:, (i % 4) * P:(i % 4 + 1) * P], XN[:, i, :], ident)
                last.then_inc(s_tr, 1)
                pe.wait_ge(s_ht, v + 1)

            pe.wait_ge(s_wts, 16 * WTS)
            pe.wait_ge(s_mod, 1)
            for b in range(B):
                turn(b)
                if b:
                    pe.wait_ge(s_v, 2 * b)
                    pe.wait_ge(s_nr, 4 * b)
                for half in range(2):
                    h = hT[:, b * S + half * HALF:b * S + (half + 1) * HALF]
                    mm((B4, B5)[half][0:LAT, :], attnw[:, A_WL0:A_WL0 + LAT], h, start=True, stop=True).then_inc(s_lat, 1)
                if b:
                    pe.wait_ge(s_qk, 2 * b)
                    pe.wait_ge(s_sq, 2 * b)
                for half in range(2):
                    h = hT[:, b * S + half * HALF:b * S + (half + 1) * HALF]
                    last = mm(SAB[0][:, half * HALF:(half + 1) * HALF], attnw[:, A_WQ0:A_WQ0 + P], h, start=True, stop=True)
                last.then_inc(s_qmm, 1)
                pe.wait_ge(s_latsb, 2 * b + 2)
                for half in range(2):
                    last = mm(SAB[1][:, half * HALF:(half + 1) * HALF], lowrank[:, 0:P],
                              latT[:, half * HALF:(half + 1) * HALF], start=True, stop=True)
                last.then_inc(s_kmm, 1)
                for half in range(2):
                    for i in range(BT // 2):
                        t = half * BT // 2 + i
                        last = mm((B4, B5)[half][:, i * P:(i + 1) * P], latT[:, t * P:(t + 1) * P], lowrank[:, P:2 * P],
                                  start=True, stop=True)
                    last.then_inc(s_vmm, 1)
                for n in range(2):
                    pe.wait_ge(s_sq, 2 * b + n + 1)
                    for half in range(2):
                        if n:
                            pe.wait_ge(s_nr, 4 * b + half + 1)
                        mm((B6, B7)[half][0:HEADS, :], consts[:, C_HEAD:C_HEAD + HEADS], SQ[:, n, half * HALF:(half + 1) * HALF],
                           start=True, stop=True).then_inc(s_nb, 1)
            pe.wait_ge(s_nt, 1)
            pe.transpose(B6[0:1, 0:HEADS], norm_s[:, 0:1], ident[0:HEADS, 0:HEADS]).then_inc(s_ntr, 1)

            pe.wait_ge(s_qk, 2 * B)
            pe.wait_ge(s_sq, 2 * B)
            pe.wait_ge(s_v, 2 * B)
            pe.wait_ge(s_flag, 1)
            flag = pe.value_load(need_max[0:1, 0:1], min_val=0, max_val=1)
            with pe.If(flag != 0):
                with pe.Fori(0, NG // 2) as i:
                    for k in range(2):
                        g = i * 2 + k
                        pe.wait_ge(s_kqm[k], i * 32 + 32)
                        for item in range(HG * BT):
                            h, qt = divmod(item, BT)
                            pe.wait_ge(s_mred, g * (HG * BT) + (item + 1))
                            for half in range(2):
                                last = mm(SAB[item % 2][:, half * HALF:(half + 1) * HALF],
                                          Qb[0:KR, k, h * S + qt * P:h * S + (qt + 1) * P],
                                          Kb[0:KR, k, h * S + half * HALF:h * S + (half + 1) * HALF], start=True, stop=True)
                            last.then_inc(s_mm, 1)
                        pe.wait_ge(s_mred, g * (HG * BT) + (HG * BT + 2))
                        pe.transpose(B4[0:HG * BT, 0:P], mx[:, k, :], ident).then_inc(s_mtr, 1)

            with pe.Fori(0, NG // 2) as i:
                def spread_den(r):
                    pe.wait_ge(s_pve, i * 4 + (r + 3))
                    pe.wait_ge(s_denr, i * 4 + (r + 1))
                    mm(B6[:, :], den_sel, PV_sb[:, r % 2, :], start=True, stop=True).then_inc(s_den, 1)

                for v in range(2 * ATT_UNITS + 1):
                    if v < 2 * ATT_UNITS:
                        k, qh, kt = v // ATT_UNITS, v // BT % 2, v % BT
                        if v % ATT_UNITS == 0:
                            pe.wait_ge(s_kq[k], i * 32 + 32)
                        for pair in range(2):
                            pe.wait_ge(s_ex, i * (4 * ATT_UNITS) + (2 * v + pair + 1))
                            for h in (2 * pair, 2 * pair + 1):
                                last = mm(SAB[pair][:, (h % 2) * HALF:(h % 2 + 1) * HALF],
                                          Kb[0:KM, k, h * S + kt * P:h * S + (kt + 1) * P],
                                          Qb[0:KM, k, h * S + qh * HALF:h * S + (qh + 1) * HALF], start=True, stop=True)
                            last.then_inc(s_st, 1)
                    if v:
                        u = v - 1
                        k, qh, kt = u // ATT_UNITS, u // BT % 2, u % BT
                        if u % ATT_UNITS == 0:
                            pe.wait_ge(s_vg, i * 2 + (k + 1))
                        if kt == 0:
                            pe.wait_ge(s_pve, i * 4 + (u // BT + 1))
                        pe.wait_ge(s_ex, i * (4 * ATT_UNITS) + (2 * u + 4))
                        for h in range(HG):
                            last = mm((B4, B5)[qh][32 * h:32 * h + 32, :], Vg[:, k, kt, h, :], PR[:, u % 4, h, :],
                                      start=(kt == 0), stop=(kt == BT - 1))
                        last.then_inc(s_pv, 1)
                        if kt == 1 and u >= BT:
                            spread_den(u // BT - 1)
                spread_den(2 * ATT_UNITS // BT - 1)

            pe.wait_ge(s_wog, 2 * B)
            for b in range(B):
                pe.wait_ge(s_at, 2 * GB * (b + 1))
                for t in range(BT):
                    bank = ((B4, B5) if b == 0 else (SAB[1][:, 0:HALF], SAB[1][:, HALF:2 * HALF]))[t // 4]
                    for g in range(GB):
                        last = mm(bank[:, (t % 4) * P:(t % 4 + 1) * P], At[:, b * GB + g, t * P:(t + 1) * P],
                                  wo0g[:, b, g, :], start=(g == 0), stop=(g == GB - 1))
                last.then_inc(s_wo, 1)

            def router(layer, b):
                for t in range(BT):
                    o = b * HALF + t * E
                    c = (A_RT0, A_RT1)[layer]
                    last = mm(SAB[0][:, o:o + E], hT[:, (b * BT + t) * P:(b * BT + t + 1) * P], attnw[:, c:c + E],
                              start=True, stop=True)
                last.then_inc(s_lg, 1)

            for b in range(B):
                turn(B + b)
                router(0, b)
            for b in range(B):
                pe.wait_ge(s_gate, b + 1)
                if b:
                    pe.wait_ge(s_gts, b)
                for t in range(BT):
                    last = pe.transpose(SAB[1][0:E, t * P:(t + 1) * P], GT[:, 0:E, b * BT + t], ident)
                last.then_inc(s_gtr, 1)
                pe.wait_ge(s_gts, b + 1)
                if b:
                    pe.wait_ge(s_acc0, b)
                for t in range(BT):
                    last = mm((B4, B5)[t // 4][:, (t % 4) * P:(t % 4 + 1) * P], gT[:, t * P:(t + 1) * P], w2b[:, :],
                              start=True, stop=True)
                last.then_inc(s_b2, 1)

            def up(layer, base, buf, v, f):
                wb = Wsh if buf == 2 else Wb[buf]
                h = hT[:, (v % NH) * HALF:(v % NH + 1) * HALF]
                n = base * FC + (v * FC + f + 1)
                pe.wait_ge(s_y[layer], n)
                mm(SAB[0][:, (f % 2) * HALF:(f % 2 + 1) * HALF], wb[:, f * P:(f + 1) * P], h,
                   start=True, stop=True).then_inc(s_gm[layer], 1)
                if layer == 0:
                    pe.wait_ge(s_h, n)
                    mm(SAB[1][:, (f % 2) * HALF:(f % 2 + 1) * HALF], wb[:, FF + f * P:FF + (f + 1) * P], h,
                       start=True, stop=True).then_inc(s_um, 1)

            def down(layer, base, buf, v, t):
                wb = Wsh if buf == 2 else Wb[buf]
                w0 = (2 * FF, FF)[layer]
                if t == 0:
                    pe.wait_ge((s_h, s_y[1])[layer], base * FC + (v * FC + FC + 2))
                    pe.wait_ge(s_ac[layer], base + (v + 1))
                for f in range(FC):
                    last = mm((B4, B5)[v % 2][:, t * P:(t + 1) * P], H[:, v % 2, f, t * P:(t + 1) * P],
                              wb[:, w0 + f * P:w0 + (f + 1) * P], start=(f == 0), stop=(f == FC - 1))
                if t == HALF // P - 1:
                    last.then_inc(s_o[layer], 1)

            def experts(layer, base, bufs, first_wait):
                n = len(bufs) * NH
                for v in range(n + 1):
                    if v < n and v % NH == 0:
                        first_wait(bufs[v // NH])
                    for j in range(FC):
                        if v < n:
                            up(layer, base, bufs[v // NH], v, j)
                        if v:
                            down(layer, base, bufs[(v - 1) // NH], v - 1, j)

            pe.wait_ge(s_acc0, B)
            pe.sem_inc(s_o[0], 2)
            with pe.Fori(0, E // 2) as i:
                experts(0, i * (2 * NH), (0, 1), lambda k: pe.wait_ge(s_w[k], i * 16 + 16))

            for b in range(B):
                if b:
                    pe.wait_ge(s_kvb, b)
                turn(2 * B + b)
                if b:
                    pe.wait_ge(s_ot, b)
                for half in range(2):
                    last = mm(SAB[0][:, half * HALF:(half + 1) * HALF], attnw[:, A_WQ1:A_WQ1 + P],
                              hT[:, b * S + half * HALF:b * S + (half + 1) * HALF], start=True, stop=True)
                last.then_inc(s_q1, 1)
                for t in range(BT):
                    dst = SAB[1][:, t * 2 * P:(t + 1) * 2 * P] if t < 4 else (B4, B5)[(t - 4) // 2][:, (t % 2) * 2 * P:(t % 2 + 1) * 2 * P]
                    last = mm(dst, hT[:, b * S + t * P:b * S + (t + 1) * P], attnw[:, A_WKV1:A_WKV1 + 2 * P],
                              start=True, stop=True)
                last.then_inc(s_kv1, 1)
                pe.wait_ge(s_kf, b + 1)
                for t in range(BT):
                    last = mm(B6[:, 0:P + 1], KF[:, t, :], KVt[:, t, P:2 * P + 1], start=(t == 0), stop=(t == BT - 1))
                last.then_inc(s_kvm, 1)
                pe.wait_ge(s_kvb, b + 1)
                pe.wait_ge(s_qf, b + 1)
                for n in range(2):
                    for half in range(2):
                        last = mm(SAB[n][:, half * HALF:(half + 1) * HALF], KVB[:, n * P:(n + 1) * P],
                                  QF[:, half * HALF:(half + 1) * HALF], start=True, stop=True)
                last.then_inc(s_nn, 1)
                pe.wait_ge(s_ot, b + 1)
                for t in range(BT):
                    last = mm((B4, B5)[t // 4][:, (t % 4) * P:(t % 4 + 1) * P], OT[:, t * P:(t + 1) * P], wo1g[:, b, :],
                              start=True, stop=True)
                last.then_inc(s_wo, 1)

            for b in range(B):
                turn(3 * B + b)
                router(1, b)
            pe.wait_ge(s_gate, 2 * B)
            pe.sem_inc(s_o[1], 2)
            experts(1, 0, (2,), lambda k: pe.wait_ge(s_wsh, 16))
            with pe.Fori(0, E // 2) as i:
                experts(1, i * (2 * NH) + NH, (0, 1), lambda k: pe.wait_ge(s_w[k], i * 16 + (E // 2 + 1) * 16))


def kernel(**inputs):
    import concourse.bacc as bacc
    from concourse.bass_utils import run_bass_kernel_spmd

    a = {k: np.asarray(v) for k, v in inputs.items()}
    f32 = np.float32

    consts = np.zeros((P, C_END), f32)
    consts[:, C_ID:C_ID + P] = np.eye(P)
    consts[:, C_BLOCK:C_BLOCK + P] = np.kron(np.eye(HEADS), np.ones((DH, DH)))
    for h in range(HG):
        consts[32 * h + DH, C_SEL + 32 * h:C_SEL + 32 * h + 32] = 1
    consts[:, C_IOTA:C_HEAD] = np.tile(np.arange(E), BT)

    consts[np.arange(P), C_HEAD + np.arange(P) // (HG * DH) * HG + np.arange(P) % HG] = 1
    def turned(w):
        return w.reshape(w.shape[:-1] + (GB, HG, DH)).swapaxes(-1, -2).reshape(w.shape)

    vecs = np.zeros((P, V_END), f32)
    vecs[:, V_BQ0] = turned(a["L0_attn_bq"])
    vecs[:, V_BK0] = turned(a["L0_attn_bk"])
    vecs[0:LAT, V_BL0] = a["L0_attn_bl"]
    vecs[:, V_BQ1] = a["L1_attn_bq"]
    vecs[:, V_CT:V_CT + B] = a["L0_c"].T
    vecs[:, V_CT + B:V_CT + 2 * B] = a["L1_c"].T
    vecs[:, V_EPS] = EPS_LN
    rows = np.concatenate([a["L0_attn_bv"], a["L1_attn_bk"], a["L1_attn_bv"], a["L1_attn_bo"]])
    rows = np.ascontiguousarray(np.broadcast_to(rows, (P, R_END)))
    attnw = np.concatenate([turned(a["L0_attn_Wq"]), a["L0_attn_Wl"], a["L0_ffn_router_w"].T, a["L1_attn_Wq"],
                            a["L1_attn_Wk"], a["L1_attn_Wv"], a["L1_attn_Wo"], a["L1_ffn_gate_w"].T], axis=1)
    lowrank = np.concatenate([turned(a["L0_attn_Wk"]), a["L0_attn_Wv"]], axis=1)
    wo0 = np.zeros((P, GB, P), f32)
    wo = a["L0_attn_Wo"].reshape(GB, HG, DH, P)
    for h in range(HG):
        wo0[32 * h:32 * h + DH] = wo[:, h].transpose(1, 0, 2)
    wo0[DH, 0] = a["L0_attn_bo"]
    wmod = np.stack([a["L0_wmod"], a["L1_wmod"]], axis=1)

    def up(w):
        return w.transpose(0, 2, 1)

    def down(w):
        return w.transpose(0, 2, 1).reshape(-1, FC, P, P).transpose(0, 2, 1, 3).reshape(-1, P, FF)

    def bias(w):
        return w.reshape(-1, FC, P).transpose(0, 2, 1)

    exp0 = np.concatenate([up(a["L0_ffn_wg_w"]), up(a["L0_ffn_w1_w"]), down(a["L0_ffn_w2_w"]),
                           bias(a["L0_ffn_wg_b"]), bias(a["L0_ffn_w1_b"])], axis=2)
    exp1 = np.concatenate([up(a["L1_ffn_experts_w1"]), down(a["L1_ffn_experts_w2"])], axis=2)
    shared1 = np.concatenate([up(a["L1_ffn_shared_w1"][None]), down(a["L1_ffn_shared_w2"][None])], axis=2)[0]

    arrays, args = {}, []
    nc = bacc.Bacc("TRN2", target_bir_lowering=False, num_devices=1)
    for name, x in (("x", a["L0_attn_x"]), ("consts", consts), ("vecs", vecs), ("rows", rows), ("attnw", attnw),
                    ("lowrank", lowrank), ("wo0", wo0), ("wmod", wmod), ("w2b", a["L0_ffn_w2_b"]), ("exp0", exp0),
                    ("shared1", shared1), ("exp1", exp1)):
        arrays[name + "_dram"] = np.ascontiguousarray(x)
        args.append(nc.dram_tensor(name + "_dram", x.shape, mybir.dt.from_np(x.dtype), kind="ExternalInput").ap())
    out = nc.dram_tensor("out_dram", (B, S, P), F32, kind="ExternalOutput").ap()
    build(nc, *args, out)
    r = run_bass_kernel_spmd(nc, [arrays], core_ids=[0])
    return r.results[0]["out_dram"]
```

```python
from contextlib import ExitStack

import numpy as np

import concourse.bass as bass
from concourse import mybir

F32 = mybir.dt.float32
BF16 = mybir.dt.bfloat16
I32 = mybir.dt.int32
ALU = mybir.AluOpType
ACT = mybir.ActivationFunctionType
AX = mybir.AxisListType

P = 128
B, S = 2, 1024
T = B * S
NT = T // P
BT = S // P
HEADS, DH = 16, 8
HG = 4
GB = HEADS // HG
NG = B * GB
LAT = 32
E, FF = 8, 512
FC = FF // P
HALF = 512
NH = T // HALF
PIECES = 3
KR = PIECES * PIECES * DH
KM = KR + PIECES
SCALE = float(DH) ** -0.5
EPS_LN = 1e-5
EPS_NORM = 1e-6
BIG = 1e30
TOP = 2
MT = (TOP * T + E * (P - 1)) // P
RING = 3
assert MT % RING == 0
SAFE_SCORE = 60.0

C_ID, C_BLOCK, C_SEL, C_IOTA = 0, 128, 256, 384
C_HEAD = C_IOTA + NT * E
C_TRI = C_HEAD + HEADS
C_ONES = C_TRI + P
C_ROW = C_ONES + P
C_STEP = C_ROW + P
C_BEFORE = C_STEP + NT
C_PAIR = C_BEFORE + E * E
C_SPARE = C_PAIR + 2 * NT
C_PART = C_SPARE + MT
C_END = C_PART + 1
(V_BQ0, V_BK0, V_BL0, V_BQ1, V_CT) = (0, 1, 2, 3, 4)
V_EPS = V_CT + 2 * B
V_END = V_EPS + 1
R_BV0, R_BKV1, R_BO1 = 0, 128, 384
R_END = 512
(A_WQ0, A_WL0, A_RT0, A_WQ1, A_WKV1, A_WO1, A_RT1) = (0, 128, 160, 168, 296, 552, 680)
A_END = 688
W1_W = 2 * FF


def build(nc, x_in, consts_in, vecs_in, rows_in, attnw_in, lowrank_in, wo0_in, wmod_in, w2b_in, hb_in, up0_in,
          down0_in, shared1_in, exp1_in, out):
    q_scr = nc.dram_tensor("q_pieces", [NG, KM, HG * S], BF16, kind="Internal").ap()
    k_scr = nc.dram_tensor("k_pieces", [NG, KM, HG * S], BF16, kind="Internal").ap()

    hb_scr = nc.dram_tensor("hidden_bias_pieces", [PIECES, E * 2 * FF], BF16, kind="Internal").ap()
    h_scr = nc.dram_tensor("mixture_in", [T, P], F32, kind="Internal").ap()
    y_scr = [nc.dram_tensor(f"mixture_out{l}", [TOP * T + MT * P, P], F32, kind="Internal").ap() for l in range(2)]

    with ExitStack() as ctx:
        def sb(name, shape, dt=F32):
            return ctx.enter_context(nc.sbuf_tensor(name, shape, dt))

        def ps(name, shape):
            return ctx.enter_context(nc.psum_tensor(name, shape, F32))

        def sem(name):
            return ctx.enter_context(nc.semaphore(name))

        SAB = [ps("bank01", [P, 2 * HALF]), ps("bank23", [P, 2 * HALF])]
        B4, B5, B6, B7 = (ps(f"bank{i}", [P, HALF]) for i in (4, 5, 6, 7))

        consts = sb("consts", [P, C_END])
        ident = consts[:, C_ID:C_ID + P]
        block_mask = consts[:, C_BLOCK:C_BLOCK + P]
        den_sel = consts[:, C_SEL:C_SEL + P]
        iota = consts[:, C_IOTA:C_HEAD].rearrange("p (t e) -> p t e", e=E)
        vecs = sb("vecs", [P, V_END])
        rows = sb("rows", [P, R_END])
        attnw = sb("attnw", [P, A_END])
        lowrank = sb("lowrank", [LAT, 2 * P])
        wo0 = sb("wo0", [P, GB, P])
        wo0g = sb("wo0g", [P, B, GB, P])
        wo1g = sb("wo1g", [P, B, P])
        bo1g = sb("bo1g", [P, B, P])
        w2b = sb("w2b", [E, P])
        ones3 = sb("ones3", [PIECES, P], BF16)[:, :]
        silu_c = sb("silu_c", [P, 2 * B])
        modc = sb("modc", [P, 2, 6, B])
        gmod = sb("gmod", [P, 2, 4, B, P])

        norms = sb("norms", [HEADS, B, 2, 2])
        norm_s = sb("norm_s", [HEADS, 4])
        worst = sb("worst", [1, 2])
        need_max = sb("need_max", [1, 1], mybir.dt.int32)

        X = sb("X", [P, NT, P])
        hT = sb("hT", [P, T])
        XN = sb("XN", [P, B, BT, P])
        GT = sb("GT", [P, E, NT])
        stats = sb("stats", [P, BT, 6])
        mv = sb("mv", [P, BT, 2])
        sd = sb("sd", [P, BT])
        rstd = sb("rstd", [P, BT])
        latT = sb("latT", [LAT, S])
        R5 = sb("R5", [P, E * FF])
        V_all = R5[:, 0:NG * BT * HG * DH].rearrange("p (g i h d) -> p g i h d", g=NG, i=BT, h=HG)
        Vg = R5[:, E * FF // 2:E * FF].rearrange("p (n i h d) -> p n i h d", n=2, i=BT, h=HG)
        W0dn = R5[:, :].rearrange("p (e w) -> p e w", e=E)
        R3 = sb("R3", [P, E * 2 * FF])
        Kb = R3[:, 0:HG * S].bitcast(BF16).rearrange("p (n t) -> p n t", n=2)
        Qb = R3[:, HG * S:2 * HG * S].bitcast(BF16).rearrange("p (n t) -> p n t", n=2)
        W0up = R3[:, :].rearrange("p (e w) -> p e w", e=E)
        mx = sb("mx", [P, 2, HG * BT])
        mneg = sb("mneg", [HG * BT, P])
        m3 = sb("m3", [HG * BT, 2, PIECES, P], BF16)
        gate_w = sb("gate_w", [P, 12, NT, E])
        gate_s = sb("gate_s", [P, 10, NT])
        gsel = sb("gsel", [P, TOP, NT])
        seen = sb("seen", [P, NT + 1, E])
        exp_s = sb("exp_s", [P, 3, E])
        slot = sb("slot", [P, 4, TOP, NT])
        slot_i = sb("slot_i", [P, 3, TOP, NT], I32)
        dst = sb("dst", [P, 3, MT])
        dst_i = sb("dst_i", [P, MT], I32)
        tok_i = sb("tok_i", [P, MT], I32)
        tile_w = sb("tile_w", [1, MT, E])
        tile_e = sb("tile_e", [1, MT])
        tile_i = sb("tile_i", [1, MT], I32)
        gT = latT[0:E, :]
        Wsh = sb("Wsh", [P, W1_W])

        R1 = sb("R1", [P, 10240])
        wmod = R1[:, 0:12 * P].rearrange("p (l w) -> p l w", l=2)
        silu_cb = R1[:, 12 * P:(12 + 2 * B) * P].rearrange("p (n d) -> p n d", d=P)
        ACC = R1[:, E * W1_W:E * W1_W + T].rearrange("p (i d) -> p i d", d=P)
        qk32 = R1[:, 0:4 * S].rearrange("p (b n t) -> p b n t", b=B, n=2)
        pieces = R1[:, 4 * S:10 * S].bitcast(BF16).rearrange("p (b n j t) -> p b n j t", b=B, n=2, j=PIECES)
        At = R1[:, 0:NG * S].rearrange("p (g t) -> p g t", g=NG)
        W1 = R1[:, 0:E * W1_W].rearrange("p (e w) -> p e w", e=E)
        R2 = sb("R2", [P, 8192])
        PR = R2[:, :].rearrange("p (n h t) -> p n h t", n=4, h=HG)
        BR = R2[0:PIECES, 0:E * FF].bitcast(BF16).rearrange("p (e w) -> p e w", e=E)
        H = R2[:, 0:2 * FC * HALF].rearrange("p (n f t) -> p n f t", n=2, f=FC)
        is_lane = R2[:, 4096:6144].bitcast(BF16).rearrange("p (n m) -> p n m", m=P)
        is_tile = R2[:, 6144:6144 + TOP * NT * MT // 2].bitcast(BF16).rearrange("p (n j) -> p n j", j=MT)
        in_tile = R2[:, 6144 + TOP * NT * MT // 2:6144 + 3 * TOP * NT * MT // 2].bitcast(BF16)\
            .rearrange("p (n w j) -> p n w j", w=2, j=MT)
        Yt = R2[:, 4096:8192].rearrange("p (c i d) -> p c i d", c=TOP, i=NT)
        ZQ, TQ, QF = (R2[:, i * S:(i + 1) * S] for i in range(3))
        NRM, OT = ZQ, TQ
        TK = R2[:, 3 * S:4 * S].rearrange("p (i d) -> p i d", i=BT)
        KF = R2[:, 4 * S:5 * S].rearrange("p (i d) -> p i d", i=BT)
        KVW = 2 * P + 4
        KVt = R2[:, 5 * S:5 * S + BT * KVW].rearrange("p (i d) -> p i d", i=BT)
        KVB = R2[:, 5 * S + BT * KVW:5 * S + BT * KVW + 2 * P]
        gsign = R2[:, 5120:5120 + 2 * 2 * B * P]
        R4 = sb("R4", [P, 2560 + RING * P])
        hb32 = R4[0:E, 0:2 * FF]
        hb_pieces = R4[0:E, 2 * FF:5 * FF].bitcast(BF16).rearrange("p (j w) -> p j w", j=PIECES)
        PV_sb = R4[:, 0:2 * HALF].rearrange("p (n t) -> p n t", n=2)
        den_r = R4[:, 2 * HALF:3 * HALF]
        act_out, hid, hidT = (R4[:, i * FF:(i + 1) * FF] for i in range(3))
        XgT = R4[:, 1536:1536 + RING * P].rearrange("p (n d) -> p n d", n=RING)
        Yg = R4[:, 1536 + RING * P:1536 + 2 * RING * P].rearrange("p (n d) -> p n d", n=RING)
        Xg = R4[:, 2560:2560 + RING * P].rearrange("p (n d) -> p n d", n=RING)
        SQ = R2[:, 6144:8192].rearrange("p (n t) -> p n t", n=2)
        zero_one = R2[:, 0:4096].bitcast(BF16).rearrange("p (n t) -> p n t", n=2)

        s_x, s_small, s_wts = sem("x_loaded"), sem("small_loaded"), sem("wts_loaded")
        s_w0d, s_w0u, s_w1, s_br = (sem(n) for n in ("down0_loaded", "up0_loaded", "experts1_loaded", "bias_rows_loaded"))
        s_hb, s_hbs = sem("bias_pieces_ready"), sem("bias_pieces_stored")
        s_hst = sem("mixture_in_stored")
        s_wsh = sem("shared_loaded")
        s_dve, s_act, s_pool = sem("dve_chain"), sem("act_chain"), sem("pool_chain")
        s_silu, s_scb, s_modmm, s_mod = sem("silu_c_ready"), sem("silu_cb_ready"), sem("mod_products"), sem("mod_ready")
        s_var, s_sd, s_xn, s_tr, s_ht = (sem(n) for n in ("var_ready", "sd_ready", "xn_ready", "xn_turned", "ht_ready"))
        s_lat, s_latsb, s_qmm, s_kmm, s_vmm = (sem(n) for n in ("lat_mm", "lat_ready", "q_mm", "k_mm", "v_mm"))
        s_qk, s_v, s_pc = sem("qk_evacuated"), sem("v_ready"), sem("pieces_ready")
        s_sq, s_nb, s_nr, s_nt, s_ntr, s_flag = (sem(n) for n in (
            "squares_ready", "norms_summed", "norms_taken", "norm_bound", "norm_bound_turned", "need_max_ready"))
        s_zo, s_scr = sem("zero_one_ready"), sem("pieces_stored")
        s_scr2 = [sem("max_rows_even_stored"), sem("max_rows_odd_stored")]
        s_kq = [sem("kq_even_loaded"), sem("kq_odd_loaded")]
        s_mm, s_mred, s_mtr, s_mev, s_m3, s_m3c = (sem(n) for n in ("max_scores", "max_taken", "max_turned", "max_evac", "max_split", "max_split_chain"))
        s_kqm = [sem("max_kq_even_loaded"), sem("max_kq_odd_loaded")]
        s_vz, s_vg, s_ones = sem("vg_padding_ready"), sem("vg_ready"), sem("ones_ready")
        s_st, s_ex, s_pv, s_pve, s_den, s_denr, s_at = (sem(n) for n in (
            "scores_ready", "probs_ready", "pv_done", "pv_evacuated", "den_spread", "den_recip", "attn_normed"))
        s_wog, s_wo, s_res = sem("wo_scaled"), sem("wo_done"), sem("mixture_added")
        s_lg, s_gx, s_ge, s_gate, s_gtr, s_gts, s_b2 = (sem(n) for n in (
            "logits_ready", "gate_exp_in", "gate_exp_out", "gates_ready", "gates_turned", "gates_t_ready", "bias2_ready"))
        s_acc0 = sem("acc_started")
        s_gm, s_y, s_o, s_ac = (sem(n) for n in ("shared_up", "shared_silu", "shared_down", "shared_taken"))
        s_ch, s_cnt, s_oh, s_im, s_idx = (sem(n) for n in (
            "choices_ready", "pairs_counted", "slot_tables_ready", "slots_inverted", "indices_ready"))

        def both(name):
            return [sem(f"{name}{l}") for l in range(2)]

        s_xg = [[sem(f"gathered{l}_{v}") for v in range(RING)] for l in range(2)]
        s_sc = [[sem(f"scattered{l}_{v}") for v in range(RING)] for l in range(2)]
        s_xt, s_xte, s_g, s_u, s_ga, s_hh, s_hr, s_hre, s_dn, s_ys = (both(n) for n in (
            "tile_turned", "tile_t_ready", "tile_gate_mm", "tile_up_mm", "tile_act", "tile_hidden", "tile_hidden_turned",
            "tile_hidden_t", "tile_down_mm", "tile_out"))
        s_yt = [sem(f"mixture_out_loaded_{b}") for b in range(B)]
        s_q1, s_kv1, s_tq, s_eq, s_qf, s_kf, s_kvm, s_kvb, s_nn, s_ot = (sem(n) for n in (
            "q1_mm", "kv1_mm", "t1_ready", "e1_ready", "qf_ready", "kf_ready", "kv_sum", "kv_masked", "num_norm", "ot_ready"))
        s_out = sem("out_stored")

        SMALL = 6
        WTS = 3
        ATT_UNITS = 2 * BT

        block = ctx.enter_context(nc.Block())

        @block.sync
        def _(sp):
            sp.dma_start(vecs[:, :], vecs_in).then_inc(s_small, 16)
            sp.dma_start(wmod[:, :, :], wmod_in).then_inc(s_small, 16)
            sp.dma_start(consts[:, :], consts_in).then_inc(s_small, 16)
            sp.dma_start(rows[:, :], rows_in).then_inc(s_small, 16)
            sp.dma_start(w2b[:, :], w2b_in).then_inc(s_small, 16)
            sp.dma_start(hb32, hb_in).then_inc(s_small, 16)
            for b in range(B):
                sp.dma_start(X[:, b * BT:(b + 1) * BT, :], x_in[b].rearrange("(i p) d -> p i d", p=P)).then_inc(s_x, 16)
            sp.dma_start(attnw[:, :], attnw_in).then_inc(s_wts, 16)
            sp.dma_start(lowrank[:, :], lowrank_in).then_inc(s_wts, 16)
            sp.dma_start(wo0[:, :, :], wo0_in).then_inc(s_wts, 16)
            sp.dma_start(Wsh[:, :], shared1_in).then_inc(s_wsh, 16)
            sp.wait_ge(s_zo, 2)
            sp.dma_start(q_scr[:, KR:KM, :], zero_one[0:NG * PIECES, 0, :]).then_inc(s_scr, 16)
            sp.dma_start(k_scr[:, KR:KM, :], zero_one[0:NG * PIECES, 1, :]).then_inc(s_scr, 16)
            for b in range(B):
                for n, scr in enumerate((q_scr, k_scr)):
                    sp.wait_ge(s_pc, 2 * b + n + 1)
                    for piece in range(PIECES):
                        for rep in range(PIECES):
                            r = (rep * PIECES + piece if n == 0 else piece * PIECES + rep) * DH
                            sp.dma_start(scr[b * GB:(b + 1) * GB, r:r + DH, :].rearrange("g d (h t) -> g (d h) t", h=HG),
                                         pieces[:, b, n, piece, :]).then_inc(s_scr, 16)
            sp.wait_ge(s_hb, 1)
            sp.dma_start(hb_scr.rearrange("j (e w) -> e j w", e=E), hb_pieces).then_inc(s_hbs, 16)
            stores = 2 + B * 2 * PIECES * PIECES
            sp.wait_ge(s_scr, 16 * stores)

            sp.wait_ge(s_flag, 1)
            flag = sp.value_load(need_max[0:1, 0:1], min_val=0, max_val=1)
            with sp.If(flag != 0):
                for k in range(2):
                    sp.dma_start(Kb[0:KR, k, :], k_scr[k, 0:KR, :]).then_inc(s_kqm[k], 16)
                    sp.dma_start(Qb[0:KR, k, :], q_scr[k, 0:KR, :]).then_inc(s_kqm[k], 16)
                with sp.Fori(1, NG // 2) as i:
                    for k in range(2):
                        sp.wait_ge(s_mm, (i * 2 + (k - 1)) * (HG * BT))
                        sp.dma_start(Kb[0:KR, k, :], k_scr[bass.ds(i * 2 + k, 1), 0:KR, :].rearrange("g r t -> (g r) t")).then_inc(s_kqm[k], 16)
                        sp.dma_start(Qb[0:KR, k, :], q_scr[bass.ds(i * 2 + k, 1), 0:KR, :].rearrange("g r t -> (g r) t")).then_inc(s_kqm[k], 16)
                for k in range(2):
                    sp.wait_ge(s_scr2[k], 16 * (NG // 2 + 1))
                sp.wait_ge(s_mm, NG * HG * BT)
            for k in range(2):
                sp.dma_start(Kb[0:KM, k, :], k_scr[k, :, :]).then_inc(s_kq[k], 16)
                sp.dma_start(Qb[0:KM, k, :], q_scr[k, :, :]).then_inc(s_kq[k], 16)
            with sp.Fori(1, NG // 2) as i:
                for k in range(2):
                    sp.wait_ge(s_st, (i * 2 + (k - 1)) * (2 * ATT_UNITS))
                    sp.dma_start(Kb[0:KM, k, :], k_scr[bass.ds(i * 2 + k, 1), :, :].rearrange("g r t -> (g r) t")).then_inc(s_kq[k], 16)
                    sp.dma_start(Qb[0:KM, k, :], q_scr[bass.ds(i * 2 + k, 1), :, :].rearrange("g r t -> (g r) t")).then_inc(s_kq[k], 16)
            sp.wait_ge(s_st, NG * 2 * ATT_UNITS)
            for e in range(0, E, 2):
                sp.dma_start(W0up[:, e:e + 2, :], up0_in[:, e:e + 2, :]).then_inc(s_w0u, 16)
            sp.wait_ge(s_pv, NG * ATT_UNITS + 4)
            sp.dma_start(W0dn, down0_in).then_inc(s_w0d, 16)
            sp.wait_ge(s_hbs, 16)
            sp.dma_start(BR, hb_scr.rearrange("j (e w) -> j e w", e=E)).then_inc(s_br, 16)

            def mixture_io(layer):
                for b in range(B):
                    sp.wait_ge(s_xn, (2 * layer + 1) * B + b + 1)
                    sp.dma_start(h_scr[b * S:(b + 1) * S, :].rearrange("(i p) d -> p i d", p=P),
                                 XN[:, b]).then_inc(s_hst, 16)
                if layer == 0:
                    sp.wait_ge(s_wo, B)
                    for e in range(0, E, 2):
                        sp.dma_start(W1[:, e:e + 2, :], exp1_in[:, e:e + 2, :]).then_inc(s_w1, 16)
                for v in range(RING):
                    sp.wait_ge(s_sc[layer][v], 16 * (MT // RING))
                for b in range(B):
                    for c in range(TOP):
                        sp.dma_start(Yt[:, c, b * BT:(b + 1) * BT, :],
                                     y_scr[layer][c * T + b * S:c * T + (b + 1) * S, :].rearrange("(i p) d -> p i d", p=P))\
                          .then_inc(s_yt[b], 16)

            mixture_io(0)
            mixture_io(1)
            for b in range(B):
                sp.wait_ge(s_res, B + b + 1)
                sp.dma_start(out[b].rearrange("(i p) d -> p i d", p=P), X[:, b * BT:(b + 1) * BT, :]).then_inc(s_out, 16)
            sp.wait_ge(s_out, 16 * B)

        @block.gpsimd
        def _(pool):
            pool.memset(zero_one[0:NG * PIECES, 0, :], 0.0).then_inc(s_zo, 1)
            pool.memset(zero_one[0:NG * PIECES, 1, :], 1.0).then_inc(s_zo, 1)
            pool.memset(ones3, 1.0).then_inc(s_ones, 1)
            pool.memset(Vg[:, :, :, :, :], 0.0).then_inc(s_vz, 1)
            pool.wait_ge(s_vz, 1)
            pool.memset(Vg[:, :, :, :, DH:DH + 1], 1.0).then_inc(s_vz, 1)
            pool.wait_ge(s_vz, 2)
            pool.wait_ge(s_small, 16 * SMALL)
            for j in range(PIECES):
                ins = pool.tensor_copy(hb_pieces[:, j, :], hb32)
                if j == PIECES - 1:
                    ins.then_inc(s_hb, 1)
                    break
                ins.then_inc(s_pool, 1)
                pool.wait_ge(s_pool, 2 * j + 1)
                pool.tensor_tensor(hb32, hb32, hb_pieces[:, j, :], ALU.subtract).then_inc(s_pool, 1)
                pool.wait_ge(s_pool, 2 * j + 2)
            pool.wait_ge(s_v, B * 2)
            pool.sem_inc(s_pv, 4)
            for k in range(2):
                pool.tensor_copy(Vg[:, k, :, :, 0:DH], V_all[:, k, :, :, :]).then_inc(s_vg, 1)
            with pool.Fori(1, NG // 2) as i:
                for k in range(2):
                    pool.wait_ge(s_pv, (i * 2 + (k - 1)) * ATT_UNITS + 4)
                    pool.tensor_copy(Vg[:, k, :, :, 0:DH],
                                     V_all[:, bass.ds(i * 2 + k, 1), :, :, :].rearrange("p g i h d -> p (g i) h d")).then_inc(s_vg, 1)

            for layer in range(2):
                def gather(j):
                    pool.indirect_dma_start(Xg[:, j % RING, :], None, h_scr,
                                            bass.IndirectOffsetOnAxis(tok_i[:, j:j + 1], 0)).then_inc(s_xg[layer][j % RING], 16)

                pool.wait_ge(s_idx, layer + 1)
                pool.wait_ge(s_hst, 16 * B * (layer + 1))
                for j in range(RING):
                    gather(j)
                for j in range(MT):
                    if j + RING < MT:
                        pool.wait_ge(s_xt[layer], j + 1)
                        gather(j + RING)
                    pool.wait_ge(s_ys[layer], j + 2)
                    pool.indirect_dma_start(y_scr[layer], bass.IndirectOffsetOnAxis(dst_i[:, j:j + 1], 0),
                                            Yg[:, j % RING, :], None).then_inc(s_sc[layer][j % RING], 16)

        @block.scalar
        def _(act):
            act.wait_ge(s_small, 16 * SMALL)
            act.activation(silu_c[:, :], vecs[:, V_CT:V_EPS], ACT.Silu).then_inc(s_silu, 1)

            def spread(v):
                act.wait_ge(s_var, v + 1)
                act.activation(sd[:, :], mv[:, :, 1], ACT.Sqrt, bias=vecs[:, V_EPS:V_END]).then_inc(s_sd, 1)

            for b in range(B):
                spread(b)
                for half in range(2):
                    act.wait_ge(s_lat, 2 * b + half + 1)
                    if b and not half:
                        act.wait_ge(s_vmm, 2)
                    act.activation(latT[:, half * HALF:(half + 1) * HALF], (B4, B5)[half][0:LAT, :], ACT.Identity,
                                   bias=vecs[0:LAT, V_BL0:V_BL0 + 1]).then_inc(s_latsb, 1)
                for n in range(2):
                    act.wait_ge(s_qk, 2 * b + n + 1)
                    if b:
                        act.wait_ge(s_nb, 2 * n + 2)
                    act.activation(SQ[:, n, :], SAB[n][:, :], ACT.Square,
                                   bias=vecs[:, V_BQ0 + n:V_BQ0 + n + 1]).then_inc(s_sq, 1)

            act.wait_ge(s_flag, 1)
            flag = act.value_load(need_max[0:1, 0:1], min_val=0, max_val=1)
            with act.If(flag != 0):
                for k in range(2):
                    act.sem_inc(s_scr2[k], 16)
                with act.Fori(0, NG // 2) as i:
                    for k in range(2):
                        act.wait_ge(s_m3, i * 2 + k + 1)
                        act.dma_start(q_scr[bass.ds(i * 2 + k, 1), KR:KM, :].rearrange("g r (x t) -> (g x) r t", t=P),
                                      m3[:, k, :, :]).then_inc(s_scr2[k], 16)

            act.sem_inc(s_ex, 2)
            with act.Fori(0, NG // 2) as i:
                for v in range(2 * ATT_UNITS):
                    n = i * (2 * ATT_UNITS) + v
                    for pair in range(2):
                        act.wait_ge(s_st, n * 2 + (pair + 1))
                        act.wait_ge(s_pv, n + 1)
                        act.activation(PR[:, v % 4, 2 * pair:2 * pair + 2, :], SAB[pair][:, :].rearrange("p (h t) -> p h t", h=2),
                                       ACT.Exp, scale=SCALE).then_inc(s_ex, 1)

            def gate_exp(layer):
                act.wait_ge(s_gx, layer + 1)
                if layer == 0:
                    act.activation(gate_w[:, 1], gate_w[:, 0], ACT.Exp).then_inc(s_ge, 1)
                else:
                    act.activation(gate_s[:, 5], gate_s[:, 4], ACT.Exp).then_inc(s_ge, 1)

            def expert_tiles(layer):
                with act.Fori(0, MT) as j:
                    act.wait_ge(s_g[layer], j + 1)
                    if layer == 0:
                        act.activation(act_out, SAB[0][:, 0:HALF], ACT.Gelu).then_inc(s_ga[0], 1)
                    else:
                        act.activation(hid, SAB[0][:, 0:HALF], ACT.Silu).then_inc(s_hh[1], 1)
                    act.wait_ge(s_hr[layer], j + 1)
                    act.activation(hidT, SAB[1][:, 0:HALF], ACT.Copy).then_inc(s_hre[layer], 1)

            for b in range(B):
                spread(B + b)
            gate_exp(0)
            expert_tiles(0)

            for b in range(B):
                spread(2 * B + b)
                act.wait_ge(s_tq, 2 * b + 1)
                act.activation(TQ, TQ, ACT.Exp).then_inc(s_eq, 1)
                act.wait_ge(s_tq, 2 * b + 2)
                act.activation(TK, TK, ACT.Exp).then_inc(s_eq, 1)
            for b in range(B):
                spread(3 * B + b)
            gate_exp(1)
            act.sem_inc(s_y, 2)
            for v in range(NH):
                for f in range(FC):
                    act.wait_ge(s_gm, v * FC + f + 1)
                    if f == 0 and v >= 2:
                        act.wait_ge(s_o, v - 1)
                    act.activation(H[:, v % 2, f, :], SAB[0][:, (f % 2) * HALF:(f % 2 + 1) * HALF],
                                   ACT.Silu).then_inc(s_y, 1)
            expert_tiles(1)

        @block.vector
        def _(dve):
            count = [0]

            def link(ins):
                count[0] += 1
                ins.then_inc(s_dve, 1)
                dve.wait_ge(s_dve, count[0])

            tt, ts, stt, copy = dve.tensor_tensor, dve.tensor_scalar, dve.scalar_tensor_tensor, dve.tensor_copy

            dve.wait_ge(s_silu, 1)
            copy(silu_cb[:, :, :], silu_c[:, :].unsqueeze(2).to_broadcast([P, 2 * B, P])).then_inc(s_scb, 1)
            dve.wait_ge(s_modmm, 1)
            link(copy(modc[:, :, :, :], B4[:, 0:2 * 6 * B].rearrange("p (l c b) -> p l c b", l=2, c=6)))
            link(ts(modc[:, :, 1, :], modc[:, :, 1, :], 1.0, None, ALU.add))
            gm = gmod[:, :, 0:2].rearrange("p l k b d -> p l (k b d)")
            gsrc = SAB[0][:, :].rearrange("p (l w) -> p l w", l=2)
            gs = gsign.rearrange("p (l w) -> p l w", l=2)
            for kind in (2, 3):
                last = copy(gmod[:, :, kind].rearrange("p l b d -> p l (b d)"),
                            SAB[1][:, :].rearrange("p (l k w) -> p l k w", l=2, k=2)[:, :, kind - 2, :])
            link(last)
            link(ts(gmod[:, :, 2].rearrange("p l b d -> p l (b d)"), gmod[:, :, 2].rearrange("p l b d -> p l (b d)"),
                    1.0, None, ALU.add))
            link(ts(gs, gsrc, 0.0, None, ALU.is_ge))
            link(ts(gs, gs, 2.0, -1.0, ALU.mult, ALU.add))
            link(copy(gm, gsrc))
            link(stt(out=gm, in0=gm, scalar=-1.0, in1=gm, op0=ALU.mult, op1=ALU.max))
            stt(out=gm, in0=gm, scalar=0.25, in1=gs, op0=ALU.max, op1=ALU.mult).then_inc(s_mod, 1)
            dve.wait_ge(s_mod, 1)
            dve.wait_ge(s_wts, 16 * WTS)
            for b in range(B):
                tt(wo0g[:, b], wo0[:, :, :], gmod[:, 0, 0, b, :].unsqueeze(1).to_broadcast([P, GB, P]), ALU.mult).then_inc(s_wog, 1)
                tt(wo1g[:, b], attnw[:, A_WO1:A_WO1 + P], gmod[:, 1, 0, b, :], ALU.mult).then_inc(s_wog, 1)
                link(tt(bo1g[:, b], rows[:, R_BO1:R_BO1 + P], gmod[:, 1, 0, b, :], ALU.mult))

            def layer_norm(v):
                step, b = divmod(v, B)
                if step == 0:
                    dve.wait_ge(s_x, 16 * (b + 1))
                xb = [X[:, b * BT + i, :] for i in range(BT)]
                for i in range(BT):
                    last = dve.bn_stats(stats[:, i, :], xb[i])
                link(last)
                for i in range(BT):
                    last = dve.bn_aggr(mv[:, i, :], stats[:, i, :])
                last.then_inc(s_var, 1)
                dve.wait_ge(s_sd, v + 1)
                link(dve.reciprocal(rstd[:, :], sd[:, :]))
                layer, c = divmod(step, 2)
                if step >= 1:
                    dve.wait_ge(s_tr, v - 1)
                if step == 2:
                    dve.wait_ge(s_hst, 16 * (b + 1))
                for i in range(BT):
                    last = ts(XN[:, b, i, :], xb[i], mv[:, i, 0:1], rstd[:, i:i + 1], ALU.subtract, ALU.mult)
                if c:
                    link(last)
                    for op, kind in ((ALU.mult, 2), (ALU.add, 3)):
                        last = tt(XN[:, b], XN[:, b], gmod[:, layer, kind, b, :].unsqueeze(1).to_broadcast([P, BT, P]), op)
                        if kind == 2:
                            link(last)
                last.then_inc(s_xn, 1)
                dve.wait_ge(s_tr, v + 1)
                for half in range(2):
                    dst_h, src_h = hT[:, b * S + half * HALF:b * S + (half + 1) * HALF], (B6, B7)[half][:, :]
                    if c:
                        last = copy(dst_h, src_h)
                    else:
                        last = ts(dst_h, src_h, modc[:, layer, 1, b:b + 1], modc[:, layer, 0, b:b + 1], ALU.mult, ALU.add)
                last.then_inc(s_ht, 1)

            for b in range(B):
                layer_norm(b)
                dve.wait_ge(s_qmm, b + 1)
                ts(qk32[:, b, 0, :], SAB[0][:, :], vecs[:, V_BQ0:V_BQ0 + 1], None, ALU.add).then_inc(s_qk, 1)
                dve.wait_ge(s_kmm, b + 1)
                ts(qk32[:, b, 1, :], SAB[1][:, :], vecs[:, V_BK0:V_BK0 + 1], None, ALU.add).then_inc(s_qk, 1)
                for half in range(2):
                    dve.wait_ge(s_vmm, 2 * b + half + 1)
                    for i in range(BT // 2):
                        last = tt(V_all[:, b * GB:(b + 1) * GB, half * BT // 2 + i, :, :],
                                  (B4, B5)[half][:, i * P:(i + 1) * P].rearrange("p (g h d) -> p g h d", g=GB, h=HG),
                                  rows[:, R_BV0:R_BV0 + P].rearrange("p (g h d) -> p g h d", g=GB, h=HG), ALU.add)
                    last.then_inc(s_v, 1)
                for n in range(2):
                    dve.wait_ge(s_qk, 2 * b + n + 1)
                    z = qk32[:, b, n, :]
                    link(copy(pieces[:, b, n, 0, :], z))
                    link(tt(z, z, pieces[:, b, n, 0, :], ALU.subtract))
                    link(copy(pieces[:, b, n, 1, :], z))
                    link(tt(z, z, pieces[:, b, n, 1, :], ALU.subtract))
                    copy(pieces[:, b, n, 2, :], z).then_inc(s_pc, 1)
                for n in range(2):
                    for half in range(2):
                        dve.wait_ge(s_nb, (2 * b + n) * 2 + half + 1)
                        dve.tensor_reduce(norms[:, b, n, half:half + 1], (B6, B7)[half][0:HEADS, :], AX.X,
                                          ALU.max).then_inc(s_nr, 1)
            dve.wait_ge(s_nr, 4 * B)
            link(dve.tensor_reduce(norm_s[:, :], norms[:, :, :, :].rearrange("p b n h -> p (b n) h"), AX.X, ALU.max))
            for b in range(B):
                last = tt(norms[:, b, 0, 0:1], norm_s[:, 2 * b:2 * b + 1], norm_s[:, 2 * b + 1:2 * b + 2], ALU.mult)
            link(last)
            tt(norm_s[:, 0:1], norms[:, 0, 0, 0:1], norms[:, 1, 0, 0:1], ALU.max).then_inc(s_nt, 1)
            dve.wait_ge(s_ntr, 1)
            link(dve.tensor_reduce(worst[:, 0:1], B6[0:1, 0:HEADS], AX.X, ALU.max))
            link(ts(worst[:, 1:2], worst[:, 0:1], (SAFE_SCORE / SCALE) ** 2, None, ALU.is_le))
            ts(need_max[:, :], worst[:, 1:2], -1.0, 1.0, ALU.mult, ALU.add).then_inc(s_flag, 1)

            dve.wait_ge(s_flag, 1)
            flag = dve.value_load(need_max[0:1, 0:1], min_val=0, max_val=1)
            with dve.If(flag != 0):
                dve.sem_inc(s_mred, 2)
                with dve.Fori(0, NG // 2) as i:
                    for k in range(2):
                        g = i * 2 + k
                        for item in range(HG * BT):
                            dve.wait_ge(s_mm, g * (HG * BT) + (item + 1))
                            dve.tensor_reduce(mx[:, k, item:item + 1], SAB[item % 2][:, :], AX.X, ALU.max).then_inc(s_mred, 1)
                        dve.wait_ge(s_mtr, g + 1)
                        ts(mneg[:, :], B4[0:HG * BT, 0:P], -1.0, None, ALU.mult).then_inc(s_m3c, 1)
                        dve.wait_ge(s_m3c, g * 5 + 1)
                        dve.wait_ge(s_scr2[k], i * 16 + 16)
                        copy(m3[:, k, 0, :], mneg[:, :]).then_inc(s_m3c, 1)
                        dve.wait_ge(s_m3c, g * 5 + 2)
                        tt(mneg[:, :], mneg[:, :], m3[:, k, 0, :], ALU.subtract).then_inc(s_m3c, 1)
                        dve.wait_ge(s_m3c, g * 5 + 3)
                        copy(m3[:, k, 1, :], mneg[:, :]).then_inc(s_m3c, 1)
                        dve.wait_ge(s_m3c, g * 5 + 4)
                        tt(mneg[:, :], mneg[:, :], m3[:, k, 1, :], ALU.subtract).then_inc(s_m3c, 1)
                        dve.wait_ge(s_m3c, g * 5 + 5)
                        copy(m3[:, k, 2, :], mneg[:, :]).then_inc(s_m3, 1)

            dve.wait_ge(s_hbs, 16)
            dve.sem_inc(s_pve, 2)
            dve.sem_inc(s_denr, 1)
            with dve.Fori(0, NG // 2) as i:
                for k in range(2):
                    g = i * 2 + k
                    for qh in range(2):
                        r = g * 2 + qh
                        dve.wait_ge(s_pv, r * BT + (BT + 4))
                        copy(PV_sb[:, qh, :], (B4, B5)[qh][:, :]).then_inc(s_pve, 1)
                        dve.wait_ge(s_den, r + 1)
                        dve.reciprocal(den_r[:, :], B6[:, :]).then_inc(s_denr, 1)
                        dve.wait_ge(s_denr, r + 2)
                        tt(At[:, bass.ds(g, 1), qh * HALF:(qh + 1) * HALF].rearrange("p g t -> p (g t)"),
                           PV_sb[:, qh, :], den_r[:, :], ALU.mult).then_inc(s_at, 1)

            def residual(j, banks, bias=None):
                b = j % B
                dve.wait_ge(s_wo, j + 1)
                for half in range(2):
                    x = X[:, b * BT + half * BT // 2:b * BT + (half + 1) * BT // 2, :]
                    last = tt(x, x, banks[half].rearrange("p (i d) -> p i d", d=P), ALU.add)
                if bias is not None:
                    link(last)
                    x = X[:, b * BT:(b + 1) * BT, :]
                    last = tt(x, x, bias.unsqueeze(1).to_broadcast([P, BT, P]), ALU.add)
                link(last)

            residual(0, (B4[:, :], B5[:, :]))
            residual(1, (SAB[1][:, 0:HALF], SAB[1][:, HALF:2 * HALF]))

            def wide(col, n=E):
                return col.unsqueeze(2).to_broadcast([P, col.shape[1], n])

            def gates(layer):
                w = [gate_w[:, i] for i in range(12)]
                s = [gate_s[:, i] for i in range(8)]
                dve.wait_ge(s_lg, layer + 1)
                logits = SAB[0][:, 0:NT * E].rearrange("p (t e) -> p t e", e=E)
                if layer == 0:
                    link(dve.tensor_reduce(s[0], logits, AX.X, ALU.max))
                    tt(w[0], logits, wide(s[0]), ALU.subtract).then_inc(s_gx, 1)
                    dve.wait_ge(s_ge, 1)
                    link(dve.tensor_reduce(s[1], w[1], AX.X, ALU.add))
                    link(dve.reciprocal(s[2], s[1]))
                    link(tt(w[3], w[1], wide(s[2]), ALU.mult))
                else:
                    link(copy(w[3], logits))
                link(dve.tensor_reduce(s[3], w[3], AX.X, ALU.max))
                link(tt(w[4], w[3], wide(s[3]), ALU.not_equal))
                link(stt(out=w[4], in0=w[4], scalar=100.0, in1=iota, op0=ALU.mult, op1=ALU.add))
                link(dve.tensor_reduce(s[6], w[4], AX.X, ALU.min))
                link(tt(w[5], iota, wide(s[6]), ALU.is_equal))
                link(stt(out=w[6], in0=w[5], scalar=-BIG, in1=w[3], op0=ALU.mult, op1=ALU.add))
                link(dve.tensor_reduce(s[7], w[6], AX.X, ALU.max))
                link(tt(w[7], w[6], wide(s[7]), ALU.not_equal))
                link(stt(out=w[7], in0=w[7], scalar=100.0, in1=iota, op0=ALU.mult, op1=ALU.add))
                link(dve.tensor_reduce(s[6], w[7], AX.X, ALU.min))
                link(tt(w[8], iota, wide(s[6]), ALU.is_equal))
                tt(w[9], w[5], w[8], ALU.add).then_inc(s_ch, 1)
                if layer == 0:
                    copy(gsel[:, 0, :], s[3])
                    link(copy(gsel[:, 1, :], s[7]))
                    link(tt(w[10], w[5], wide(s[3]), ALU.mult))
                    link(tt(w[11], w[8], wide(s[7]), ALU.mult))
                    tt(GT[:, :, :].rearrange("p e t -> p t e"), w[10], w[11], ALU.add).then_inc(s_gate, 1)
                else:
                    tt(s[4], s[7], s[3], ALU.subtract).then_inc(s_gx, 1)
                    dve.wait_ge(s_ge, 2)
                    link(ts(s[0], s[5], 1.0, None, ALU.add))
                    link(dve.reciprocal(gsel[:, 0, :], s[0]))
                    link(tt(gsel[:, 1, :], s[5], gsel[:, 0, :], ALU.mult))

            def slots(layer):
                w = [gate_w[:, i] for i in range(12)]
                dve.wait_ge(s_cnt, layer + 1)
                before, totals = (B6[:, i * P:(i + 1) * P].rearrange("p (t e) -> p t e", e=E) for i in range(2))
                link(dve.memset(seen[:, 0, :], 0.0))
                for t in range(NT):
                    link(tt(seen[:, t + 1, :], seen[:, t, :], totals[:, t, :], ALU.add))
                cmp = w[10][:, :, :].rearrange("p t e -> p (t e)").rearrange("p (e j) -> p e j", e=E)
                link(tt(cmp, seen[:, NT, :].unsqueeze(2).to_broadcast([P, E, NT]),
                        consts[:, C_STEP:C_STEP + NT].unsqueeze(1).to_broadcast([P, E, NT]), ALU.is_gt))
                link(dve.tensor_reduce(exp_s[:, 0, :], cmp, AX.X, ALU.add))
                pre = w[11][:, 0:E, :]
                link(tt(pre, exp_s[:, 0, :].unsqueeze(1).to_broadcast([P, E, E]),
                        consts[:, C_BEFORE:C_BEFORE + E * E].rearrange("p (e f) -> p e f", e=E), ALU.mult))
                link(dve.tensor_reduce(exp_s[:, 1, :], pre, AX.X, ALU.add))
                link(tt(exp_s[:, 2, :], exp_s[:, 1, :], exp_s[:, 0, :], ALU.add))
                link(stt(out=w[9], in0=exp_s[:, 1, :].unsqueeze(1).to_broadcast([P, NT, E]), scalar=float(P),
                         in1=seen[:, 0:NT, :], op0=ALU.mult, op1=ALU.add))
                link(tt(w[9], w[9], before, ALU.add))
                for c, chosen in enumerate((w[5], w[8])):
                    link(tt(w[10], w[9], chosen, ALU.mult))
                    link(dve.tensor_reduce(slot[:, 0, c, :], w[10], AX.X, ALU.add))
                link(copy(slot_i[:, 0], slot[:, 0]))
                ts(slot_i[:, 1], slot_i[:, 0], 7, None, ALU.logical_shift_right)
                link(ts(slot_i[:, 2], slot_i[:, 0], P - 1, None, ALU.bitwise_and))
                link(copy(slot[:, 1:3], slot_i[:, 1:3]))
                tile = slot[:, 1].rearrange("p c t -> p (c t)")
                lane = slot[:, 2].rearrange("p c t -> p (c t)")
                n = TOP * NT
                tt(is_lane, consts[:, C_ROW:C_ROW + P].unsqueeze(1).to_broadcast([P, n, P]), wide(lane, P), ALU.is_equal)
                link(tt(is_tile, consts[:, C_ROW:C_ROW + MT].unsqueeze(1).to_broadcast([P, n, MT]), wide(tile, MT),
                        ALU.is_equal))
                ts(in_tile[:, :, 0, :], is_tile, consts[:, C_PART:C_PART + 1], None, ALU.mult)
                tt(in_tile[:, :, 1, :], is_tile, wide(consts[:, C_PAIR:C_PAIR + n], MT), ALU.mult).then_inc(s_oh, 1)
                link(tt(tile_w[:, :, :], consts[0:1, C_ROW:C_ROW + MT].unsqueeze(2).to_broadcast([1, MT, E]),
                        exp_s[0:1, 2, :].unsqueeze(1).to_broadcast([1, MT, E]), ALU.is_ge))
                link(dve.tensor_reduce(tile_e[:, :], tile_w[:, :, :], AX.X, ALU.add))
                link(ts(tile_i[:, :], tile_e[:, :], float(E - 1), None, ALU.min))

            def indices(layer):
                dve.wait_ge(s_im, layer + 1)
                lane, pair = B7[:, 0:MT], B7[:, MT:2 * MT]
                link(copy(dst[:, 0, :], pair))
                link(stt(out=dst[:, 1, :], in0=dst[:, 0, :], scalar=float(P), in1=lane, op0=ALU.mult, op1=ALU.add))
                link(ts(dst[:, 0, :], dst[:, 0, :], 0.0, None, ALU.is_equal))
                link(tt(dst[:, 0, :], dst[:, 0, :], consts[:, C_SPARE:C_SPARE + MT], ALU.mult))
                link(stt(out=dst[:, 1, :], in0=dst[:, 1, :], scalar=-float(P), in1=dst[:, 0, :], op0=ALU.add, op1=ALU.add))
                link(copy(dst_i[:, :], dst[:, 1, :]))
                ts(tok_i[:, :], dst_i[:, :], T - 1, None, ALU.bitwise_and).then_inc(s_idx, 1)

            def expert_tiles(layer):
                def turned(j, v):
                    dve.wait_ge(s_xt[layer], j + 1)
                    copy(XgT[:, v, :], B6[:, 0:P]).then_inc(s_xte[layer], 1)

                def taken(rnd, v):
                    dve.wait_ge(s_dn[layer], rnd * RING + (v + 1))
                    if not isinstance(rnd, int) or rnd > 0:
                        dve.wait_ge(s_sc[layer][v], rnd * 16)
                    copy(Yg[:, v, :], SAB[1][:, HALF:HALF + P]).then_inc(s_ys[layer], 1)

                def round_(i, first, last):
                    for v in range(RING):
                        j = i * RING + v
                        if layer == 0:
                            dve.wait_ge(s_u[0], j + 1)
                            dve.wait_ge(s_ga[0], j + 1)
                            tt(hid, SAB[0][:, HALF:2 * HALF], act_out, ALU.mult).then_inc(s_hh[0], 1)
                        if not (first and v == 0):
                            taken(i if v else i - 1, (v - 1) % RING)
                        if not (last and v == RING - 1):
                            turned(i * RING + (v + 1), (v + 1) % RING)

                dve.sem_inc(s_xte[layer], 1)
                dve.sem_inc(s_ys[layer], 1)
                turned(0, 0)
                round_(0, True, False)
                round_(1, False, False)
                with dve.Fori(2, MT // RING - 1) as i:
                    round_(i, False, False)
                round_(MT // RING - 1, False, True)
                taken(MT // RING - 1, RING - 1)

            def add_mixture(layer):
                for b in range(B):
                    dve.wait_ge(s_yt[b], 16 * TOP * (layer + 1))
                    for c in range(TOP):
                        for i in range(b * BT, (b + 1) * BT):
                            last = stt(out=ACC[:, i, :], in0=Yt[:, c, i, :], scalar=gsel[:, c, i:i + 1], in1=ACC[:, i, :],
                                       op0=ALU.mult, op1=ALU.add)
                        link(last)
                    a, x = ACC[:, b * BT:(b + 1) * BT, :], X[:, b * BT:(b + 1) * BT, :]
                    link(tt(a, a, gmod[:, layer, 1, b, :].unsqueeze(1).to_broadcast([P, BT, P]), ALU.mult))
                    tt(x, x, a, ALU.add).then_inc(s_res, 1)
                    dve.wait_ge(s_res, layer * B + b + 1)

            for b in range(B):
                layer_norm(B + b)
            gates(0)
            slots(0)
            for b in range(B):
                dve.wait_ge(s_gtr, b + 1)
                copy(gT[:, :], SAB[1][0:E, :]).then_inc(s_gts, 1)
                if b == 0:
                    indices(0)
                dve.wait_ge(s_b2, b + 1)
                for half in range(2):
                    last = copy(ACC[:, b * BT + half * BT // 2:b * BT + (half + 1) * BT // 2, :],
                                (B4, B5)[half][:, :].rearrange("p (i d) -> p i d", d=P))
                last.then_inc(s_acc0, 1)
            dve.wait_ge(s_acc0, B)
            expert_tiles(0)
            add_mixture(0)

            link(dve.memset(KVt[:, :, 2 * P:2 * P + 1], 1.0))
            for b in range(B):
                layer_norm(2 * B + b)
                if b:
                    dve.wait_ge(s_wo, B + b)
                dve.wait_ge(s_q1, b + 1)
                link(ts(ZQ, SAB[0][:, :], vecs[:, V_BQ1:V_BQ1 + 1], None, ALU.add))
                ts(TQ, ZQ, 0.0, None, ALU.min).then_inc(s_tq, 1)
                dve.wait_ge(s_kv1, b + 1)
                for src, i0, ni in ((SAB[1], 0, 4), (B4, 4, 2), (B5, 6, 2)):
                    last = tt(KVt[:, i0:i0 + ni, 0:2 * P], src[:, :].rearrange("p (i d) -> p i d", d=2 * P),
                              rows[:, R_BKV1:R_BKV1 + 2 * P].unsqueeze(1).to_broadcast([P, ni, 2 * P]), ALU.add)
                link(last)
                ts(TK, KVt[:, :, 0:P], 0.0, None, ALU.min).then_inc(s_tq, 1)
                dve.wait_ge(s_eq, 2 * b + 1)
                stt(out=QF, in0=ZQ, scalar=0.0, in1=TQ, op0=ALU.max, op1=ALU.add).then_inc(s_qf, 1)
                dve.wait_ge(s_eq, 2 * b + 2)
                stt(out=KF, in0=KVt[:, :, 0:P], scalar=0.0, in1=TK, op0=ALU.max, op1=ALU.add).then_inc(s_kf, 1)
                dve.wait_ge(s_kvm, b + 1)
                tt(KVB[:, 0:P], B6[:, 0:P], block_mask, ALU.mult)
                ts(KVB[:, P:2 * P], block_mask, B6[:, P:P + 1], None, ALU.mult).then_inc(s_kvb, 1)
                dve.wait_ge(s_nn, b + 1)
                link(ts(NRM, SAB[1][:, :], EPS_NORM, None, ALU.max))
                link(dve.reciprocal(NRM, NRM))
                tt(OT, SAB[0][:, :], NRM, ALU.mult).then_inc(s_ot, 1)
                residual(B + b, (B4[:, :], B5[:, :]), bo1g[:, b, :])

            def shared_out(v):
                dve.wait_ge(s_o, v + 1)
                copy(ACC[:, v * (HALF // P):(v + 1) * (HALF // P), :],
                     (B4, B5)[v % 2][:, :].rearrange("p (i d) -> p i d", d=P)).then_inc(s_ac, 1)

            for b in range(B):
                layer_norm(3 * B + b)
            gates(1)
            slots(1)
            for v in range(2):
                shared_out(v)
            indices(1)
            for v in range(2, NH):
                shared_out(v)
            dve.wait_ge(s_ac, NH)
            expert_tiles(1)
            add_mixture(1)

        @block.tensor
        def _(pe):
            mm = pe.matmul
            pe.wait_ge(s_small, 16 * SMALL)
            pe.wait_ge(s_silu, 1)
            for l in range(2):
                for c in range(6):
                    o = (l * 6 + c) * B
                    mm(B4[:, o:o + B], wmod[:, l, c * P:(c + 1) * P], silu_c[:, l * B:(l + 1) * B], start=True, stop=True)
            pe.wait_ge(s_scb, 1)
            for l in range(2):
                for kind, c in enumerate((2, 5, 4, 3)):
                    for b in range(B):
                        o = ((l * 2 + kind % 2) * B + b) * P
                        last = mm(SAB[kind // 2][:, o:o + P], silu_cb[:, l * B + b, :], wmod[:, l, c * P:(c + 1) * P],
                                  start=True, stop=True)
            last.then_inc(s_modmm, 1)

            def turn(v):
                pe.wait_ge(s_xn, v + 1)
                if v == 1:
                    pe.wait_ge(s_nr, 4)
                if v:
                    pe.wait_ge(s_ht, v)
                for i in range(BT):
                    last = pe.transpose((B6, B7)[i // 4][:, (i % 4) * P:(i % 4 + 1) * P], XN[:, v % B, i, :], ident)
                last.then_inc(s_tr, 1)
                pe.wait_ge(s_ht, v + 1)

            pe.wait_ge(s_wts, 16 * WTS)
            pe.wait_ge(s_mod, 1)
            for b in range(B):
                turn(b)
                if b:
                    pe.wait_ge(s_v, 2 * b)
                    pe.wait_ge(s_nr, 4 * b)
                for half in range(2):
                    h = hT[:, b * S + half * HALF:b * S + (half + 1) * HALF]
                    mm((B4, B5)[half][0:LAT, :], attnw[:, A_WL0:A_WL0 + LAT], h, start=True, stop=True).then_inc(s_lat, 1)
                if b:
                    pe.wait_ge(s_qk, 2 * b)
                    pe.wait_ge(s_sq, 2 * b)
                for half in range(2):
                    h = hT[:, b * S + half * HALF:b * S + (half + 1) * HALF]
                    last = mm(SAB[0][:, half * HALF:(half + 1) * HALF], attnw[:, A_WQ0:A_WQ0 + P], h, start=True, stop=True)
                last.then_inc(s_qmm, 1)
                pe.wait_ge(s_latsb, 2 * b + 2)
                for half in range(2):
                    last = mm(SAB[1][:, half * HALF:(half + 1) * HALF], lowrank[:, 0:P],
                              latT[:, half * HALF:(half + 1) * HALF], start=True, stop=True)
                last.then_inc(s_kmm, 1)
                for half in range(2):
                    for i in range(BT // 2):
                        t = half * BT // 2 + i
                        last = mm((B4, B5)[half][:, i * P:(i + 1) * P], latT[:, t * P:(t + 1) * P], lowrank[:, P:2 * P],
                                  start=True, stop=True)
                    last.then_inc(s_vmm, 1)
                for n in range(2):
                    pe.wait_ge(s_sq, 2 * b + n + 1)
                    for half in range(2):
                        if n:
                            pe.wait_ge(s_nr, 4 * b + half + 1)
                        mm((B6, B7)[half][0:HEADS, :], consts[:, C_HEAD:C_HEAD + HEADS], SQ[:, n, half * HALF:(half + 1) * HALF],
                           start=True, stop=True).then_inc(s_nb, 1)
            pe.wait_ge(s_nt, 1)
            pe.transpose(B6[0:1, 0:HEADS], norm_s[:, 0:1], ident[0:HEADS, 0:HEADS]).then_inc(s_ntr, 1)

            pe.wait_ge(s_qk, 2 * B)
            pe.wait_ge(s_sq, 2 * B)
            pe.wait_ge(s_v, 2 * B)
            pe.wait_ge(s_flag, 1)
            flag = pe.value_load(need_max[0:1, 0:1], min_val=0, max_val=1)
            with pe.If(flag != 0):
                with pe.Fori(0, NG // 2) as i:
                    for k in range(2):
                        g = i * 2 + k
                        pe.wait_ge(s_kqm[k], i * 32 + 32)
                        for item in range(HG * BT):
                            h, qt = divmod(item, BT)
                            pe.wait_ge(s_mred, g * (HG * BT) + (item + 1))
                            for half in range(2):
                                last = mm(SAB[item % 2][:, half * HALF:(half + 1) * HALF],
                                          Qb[0:KR, k, h * S + qt * P:h * S + (qt + 1) * P],
                                          Kb[0:KR, k, h * S + half * HALF:h * S + (half + 1) * HALF], start=True, stop=True)
                            last.then_inc(s_mm, 1)
                        pe.wait_ge(s_mred, g * (HG * BT) + (HG * BT + 2))
                        pe.transpose(B4[0:HG * BT, 0:P], mx[:, k, :], ident).then_inc(s_mtr, 1)

            with pe.Fori(0, NG // 2) as i:
                def spread_den(r):
                    pe.wait_ge(s_pve, i * 4 + (r + 3))
                    pe.wait_ge(s_denr, i * 4 + (r + 1))
                    mm(B6[:, :], den_sel, PV_sb[:, r % 2, :], start=True, stop=True).then_inc(s_den, 1)

                for v in range(2 * ATT_UNITS + 1):
                    if v < 2 * ATT_UNITS:
                        k, qh, kt = v // ATT_UNITS, v // BT % 2, v % BT
                        if v % ATT_UNITS == 0:
                            pe.wait_ge(s_kq[k], i * 32 + 32)
                        for pair in range(2):
                            pe.wait_ge(s_ex, i * (4 * ATT_UNITS) + (2 * v + pair + 1))
                            for h in (2 * pair, 2 * pair + 1):
                                last = mm(SAB[pair][:, (h % 2) * HALF:(h % 2 + 1) * HALF],
                                          Kb[0:KM, k, h * S + kt * P:h * S + (kt + 1) * P],
                                          Qb[0:KM, k, h * S + qh * HALF:h * S + (qh + 1) * HALF], start=True, stop=True)
                            last.then_inc(s_st, 1)
                    if v:
                        u = v - 1
                        k, qh, kt = u // ATT_UNITS, u // BT % 2, u % BT
                        if u % ATT_UNITS == 0:
                            pe.wait_ge(s_vg, i * 2 + (k + 1))
                        if kt == 0:
                            pe.wait_ge(s_pve, i * 4 + (u // BT + 1))
                        pe.wait_ge(s_ex, i * (4 * ATT_UNITS) + (2 * u + 4))
                        for h in range(HG):
                            last = mm((B4, B5)[qh][32 * h:32 * h + 32, :], Vg[:, k, kt, h, :], PR[:, u % 4, h, :],
                                      start=(kt == 0), stop=(kt == BT - 1))
                        last.then_inc(s_pv, 1)
                        if kt == 1 and u >= BT:
                            spread_den(u // BT - 1)
                spread_den(2 * ATT_UNITS // BT - 1)

            pe.wait_ge(s_wog, 2 * B)
            for b in range(B):
                pe.wait_ge(s_at, 2 * GB * (b + 1))
                for t in range(BT):
                    bank = ((B4, B5) if b == 0 else (SAB[1][:, 0:HALF], SAB[1][:, HALF:2 * HALF]))[t // 4]
                    for g in range(GB):
                        last = mm(bank[:, (t % 4) * P:(t % 4 + 1) * P], At[:, b * GB + g, t * P:(t + 1) * P],
                                  wo0g[:, b, g, :], start=(g == 0), stop=(g == GB - 1))
                last.then_inc(s_wo, 1)

            def router(layer, b):
                for t in range(b * BT, (b + 1) * BT):
                    c = (A_RT0, A_RT1)[layer]
                    last = mm(SAB[0][:, t * E:(t + 1) * E], hT[:, t * P:(t + 1) * P], attnw[:, c:c + E],
                              start=True, stop=True)
                if b == B - 1:
                    last.then_inc(s_lg, 1)

            def count_pairs(layer):
                pe.wait_ge(s_ch, layer + 1)
                pe.wait_ge(s_ht, (2 * layer + 2) * B)
                for n, c in enumerate((C_TRI, C_ONES)):
                    last = mm(B6[:, n * P:(n + 1) * P], consts[:, c:c + P], gate_w[:, 9].rearrange("p t e -> p (t e)"),
                              start=True, stop=True)
                last.then_inc(s_cnt, 1)

            def invert_slots(layer):
                pe.wait_ge(s_oh, layer + 1)
                for n in range(TOP * NT):
                    last = mm(B7[:, 0:2 * MT], is_lane[:, n, :], in_tile[:, n, :, :].rearrange("p w j -> p (w j)"),
                              start=(n == 0), stop=(n == TOP * NT - 1))
                last.then_inc(s_im, 1)

            def expert_tiles(layer):
                up, down0 = ((W0up, W0dn), (W1, W1))[layer]
                o = (0, FF)[layer]
                expert = [None, None]

                def turn_in(j, v):
                    pe.wait_ge(s_xg[layer][v], (j // RING if isinstance(j, int) else round_of[0]) * 16 + 16)
                    pe.wait_ge(s_xte[layer], j + 1)
                    pe.transpose(B6[:, 0:P], Xg[:, v, :], ident).then_inc(s_xt[layer], 1)

                round_of = [None]

                def up_products(j, v):
                    expert[1] = expert[0]
                    e = expert[0] = pe.value_load(tile_i[0:1, bass.ds(j, 1)], min_val=0, max_val=E - 1)
                    pe.wait_ge(s_xte[layer], j + 2)
                    for n, s_ in enumerate((s_g, s_u)[:2 - layer]):
                        bank = SAB[0][:, n * HALF:(n + 1) * HALF]
                        if layer == 0:
                            mm(bank, ones3, BR[:, bass.ds(e, 1), n * FF:(n + 1) * FF].rearrange("p e w -> p (e w)"),
                               start=True, stop=False)
                        mm(bank, XgT[:, v, :], up[:, bass.ds(e, 1), n * FF:(n + 1) * FF].rearrange("p e w -> p (e w)"),
                           start=(layer == 1), stop=True).then_inc(s_[layer], 1)

                def turn_hidden(j):
                    pe.wait_ge(s_hh[layer], j + 1)
                    for f in range(FC):
                        last = pe.transpose(SAB[1][:, f * P:(f + 1) * P], hid[:, f * P:(f + 1) * P], ident)
                    last.then_inc(s_hr[layer], 1)

                def down_product(j, e):
                    pe.wait_ge(s_hre[layer], j + 1)
                    pe.wait_ge(s_ys[layer], j + 1)
                    for f in range(FC):
                        last = mm(SAB[1][:, HALF:HALF + P], hidT[:, f * P:(f + 1) * P],
                                  down0[:, bass.ds(e, 1), o + f * P:o + (f + 1) * P].rearrange("p e w -> p (e w)"),
                                  start=(f == 0), stop=(f == FC - 1))
                    last.then_inc(s_dn[layer], 1)

                def round_(i, first, last):
                    if first:
                        round_of[0] = 0
                    for v in range(RING):
                        j = i * RING + v
                        if v == 0 and not first:
                            expert[0] = pe.value_load(tile_i[0:1, bass.ds(i * RING - 1, 1)], min_val=0, max_val=E - 1)
                        up_products(j, v)
                        if not (first and v == 0):
                            down_product(i * RING + (v - 1), expert[1])
                        if not (last and v == RING - 1):
                            round_of[0] = i if v < RING - 1 else i + 1
                            turn_in(i * RING + (v + 1), (v + 1) % RING)
                        turn_hidden(j)

                pe.wait_ge(s_idx, layer + 1)
                turn_in(0, 0)
                round_(0, True, False)
                with pe.Fori(1, MT // RING - 1) as i:
                    round_(i, False, False)
                round_(MT // RING - 1, False, True)
                down_product(MT - 1, expert[0])

            for b in range(B):
                turn(B + b)
                router(0, b)
            count_pairs(0)
            pe.wait_ge(s_gate, 1)
            for b in range(B):
                if b:
                    pe.wait_ge(s_gts, b)
                for t in range(BT):
                    last = pe.transpose(SAB[1][0:E, t * P:(t + 1) * P], GT[:, :, b * BT + t], ident)
                last.then_inc(s_gtr, 1)
                if b == 0:
                    invert_slots(0)
                pe.wait_ge(s_gts, b + 1)
                if b:
                    pe.wait_ge(s_acc0, b)
                for t in range(BT):
                    last = mm((B4, B5)[t // 4][:, (t % 4) * P:(t % 4 + 1) * P], gT[:, t * P:(t + 1) * P], w2b[:, :],
                              start=True, stop=True)
                last.then_inc(s_b2, 1)
            pe.wait_ge(s_ones, 1)
            pe.wait_ge(s_br, 16)
            pe.wait_ge(s_w0u, 16 * (E // 2))
            pe.wait_ge(s_w0d, 16)
            expert_tiles(0)

            for b in range(B):
                if b:
                    pe.wait_ge(s_kvb, b)
                turn(2 * B + b)
                if b:
                    pe.wait_ge(s_ot, b)
                for half in range(2):
                    last = mm(SAB[0][:, half * HALF:(half + 1) * HALF], attnw[:, A_WQ1:A_WQ1 + P],
                              hT[:, b * S + half * HALF:b * S + (half + 1) * HALF], start=True, stop=True)
                last.then_inc(s_q1, 1)
                for t in range(BT):
                    dst = SAB[1][:, t * 2 * P:(t + 1) * 2 * P] if t < 4 else (B4, B5)[(t - 4) // 2][:, (t % 2) * 2 * P:(t % 2 + 1) * 2 * P]
                    last = mm(dst, hT[:, b * S + t * P:b * S + (t + 1) * P], attnw[:, A_WKV1:A_WKV1 + 2 * P],
                              start=True, stop=True)
                last.then_inc(s_kv1, 1)
                pe.wait_ge(s_kf, b + 1)
                for t in range(BT):
                    last = mm(B6[:, 0:P + 1], KF[:, t, :], KVt[:, t, P:2 * P + 1], start=(t == 0), stop=(t == BT - 1))
                last.then_inc(s_kvm, 1)
                pe.wait_ge(s_kvb, b + 1)
                pe.wait_ge(s_qf, b + 1)
                for n in range(2):
                    for half in range(2):
                        last = mm(SAB[n][:, half * HALF:(half + 1) * HALF], KVB[:, n * P:(n + 1) * P],
                                  QF[:, half * HALF:(half + 1) * HALF], start=True, stop=True)
                last.then_inc(s_nn, 1)
                pe.wait_ge(s_ot, b + 1)
                for t in range(BT):
                    last = mm((B4, B5)[t // 4][:, (t % 4) * P:(t % 4 + 1) * P], OT[:, t * P:(t + 1) * P], wo1g[:, b, :],
                              start=True, stop=True)
                last.then_inc(s_wo, 1)

            for b in range(B):
                turn(3 * B + b)
                router(1, b)

            def shared_up(v, f):
                pe.wait_ge(s_y, v * FC + f + 1)
                mm(SAB[0][:, (f % 2) * HALF:(f % 2 + 1) * HALF], Wsh[:, f * P:(f + 1) * P], hT[:, v * HALF:(v + 1) * HALF],
                   start=True, stop=True).then_inc(s_gm, 1)

            def shared_down(v, t):
                if t == 0:
                    pe.wait_ge(s_y, v * FC + FC + 2)
                    if v >= 2:
                        pe.wait_ge(s_ac, v - 1)
                for f in range(FC):
                    last = mm((B4, B5)[v % 2][:, t * P:(t + 1) * P], H[:, v % 2, f, t * P:(t + 1) * P],
                              Wsh[:, FF + f * P:FF + (f + 1) * P], start=(f == 0), stop=(f == FC - 1))
                if t == HALF // P - 1:
                    last.then_inc(s_o, 1)

            pe.wait_ge(s_wsh, 16)
            pe.wait_ge(s_gx, 2)
            for v in range(NH + 1):
                for j in range(FC):
                    if v < NH:
                        shared_up(v, j)
                    if v:
                        shared_down(v - 1, j)
                if v == 0:
                    count_pairs(1)
                if v == 2:
                    invert_slots(1)
            pe.wait_ge(s_w1, 16 * (E // 2))
            expert_tiles(1)


def kernel(**inputs):
    import concourse.bacc as bacc
    from concourse.bass_utils import run_bass_kernel_spmd

    a = {k: np.asarray(v) for k, v in inputs.items()}
    f32 = np.float32

    consts = np.zeros((P, C_END), f32)
    consts[:, C_ID:C_ID + P] = np.eye(P)
    consts[:, C_BLOCK:C_BLOCK + P] = np.kron(np.eye(HEADS), np.ones((DH, DH)))
    for h in range(HG):
        consts[32 * h + DH, C_SEL + 32 * h:C_SEL + 32 * h + 32] = 1
    consts[:, C_IOTA:C_HEAD] = np.tile(np.arange(E), NT)
    consts[:, C_TRI:C_TRI + P] = np.triu(np.ones((P, P)), 1)
    consts[:, C_ONES:C_ONES + P] = 1
    consts[:, C_ROW:C_ROW + P] = np.arange(P)
    consts[:, C_STEP:C_STEP + NT] = np.arange(NT) * P
    consts[:, C_BEFORE:C_BEFORE + E * E] = np.tril(np.ones((E, E)), -1).reshape(-1)
    consts[:, C_PAIR:C_PAIR + TOP * NT] = np.arange(TOP * NT) + 1
    consts[:, C_SPARE:C_SPARE + MT] = P + TOP * T + np.arange(MT) * P + np.arange(P)[:, None]
    consts[:, C_PART] = np.arange(P)

    consts[np.arange(P), C_HEAD + np.arange(P) // (HG * DH) * HG + np.arange(P) % HG] = 1
    def turned(w):
        return w.reshape(w.shape[:-1] + (GB, HG, DH)).swapaxes(-1, -2).reshape(w.shape)

    vecs = np.zeros((P, V_END), f32)
    vecs[:, V_BQ0] = turned(a["L0_attn_bq"])
    vecs[:, V_BK0] = turned(a["L0_attn_bk"])
    vecs[0:LAT, V_BL0] = a["L0_attn_bl"]
    vecs[:, V_BQ1] = a["L1_attn_bq"]
    vecs[:, V_CT:V_CT + B] = a["L0_c"].T
    vecs[:, V_CT + B:V_CT + 2 * B] = a["L1_c"].T
    vecs[:, V_EPS] = EPS_LN
    rows = np.concatenate([a["L0_attn_bv"], a["L1_attn_bk"], a["L1_attn_bv"], a["L1_attn_bo"]])
    rows = np.ascontiguousarray(np.broadcast_to(rows, (P, R_END)))
    attnw = np.concatenate([turned(a["L0_attn_Wq"]), a["L0_attn_Wl"], a["L0_ffn_router_w"].T, a["L1_attn_Wq"],
                            a["L1_attn_Wk"], a["L1_attn_Wv"], a["L1_attn_Wo"], a["L1_ffn_gate_w"].T], axis=1)
    lowrank = np.concatenate([turned(a["L0_attn_Wk"]), a["L0_attn_Wv"]], axis=1)
    wo0 = np.zeros((P, GB, P), f32)
    wo = a["L0_attn_Wo"].reshape(GB, HG, DH, P)
    for h in range(HG):
        wo0[32 * h:32 * h + DH] = wo[:, h].transpose(1, 0, 2)
    wo0[DH, 0] = a["L0_attn_bo"]
    wmod = np.stack([a["L0_wmod"], a["L1_wmod"]], axis=1)

    def up(w):
        return w.transpose(0, 2, 1)

    def down(w):
        return w.transpose(0, 2, 1).reshape(-1, FC, P, P).transpose(0, 2, 1, 3).reshape(-1, P, FF)

    def by_lane(w):
        return w.transpose(1, 0, 2)

    up0 = by_lane(np.concatenate([up(a["L0_ffn_wg_w"]), up(a["L0_ffn_w1_w"])], axis=2))
    down0 = by_lane(down(a["L0_ffn_w2_w"]))
    hb = np.concatenate([a["L0_ffn_wg_b"], a["L0_ffn_w1_b"]], axis=1)
    exp1 = by_lane(np.concatenate([up(a["L1_ffn_experts_w1"]), down(a["L1_ffn_experts_w2"])], axis=2))
    shared1 = np.concatenate([up(a["L1_ffn_shared_w1"][None]), down(a["L1_ffn_shared_w2"][None])], axis=2)[0]

    arrays, args = {}, []
    nc = bacc.Bacc("TRN2", target_bir_lowering=False, num_devices=1)
    for name, x in (("x", a["L0_attn_x"]), ("consts", consts), ("vecs", vecs), ("rows", rows), ("attnw", attnw),
                    ("lowrank", lowrank), ("wo0", wo0), ("wmod", wmod), ("w2b", a["L0_ffn_w2_b"]), ("hb", hb),
                    ("up0", up0), ("down0", down0),
                    ("shared1", shared1), ("exp1", exp1)):
        arrays[name + "_dram"] = np.ascontiguousarray(x)
        args.append(nc.dram_tensor(name + "_dram", x.shape, mybir.dt.from_np(x.dtype), kind="ExternalInput").ap())
    out = nc.dram_tensor("out_dram", (B, S, P), F32, kind="ExternalOutput").ap()
    build(nc, *args, out)
    r = run_bass_kernel_spmd(nc, [arrays], core_ids=[0])
    return r.results[0]["out_dram"]
```

```python
from contextlib import ExitStack

import numpy as np

import concourse.bass as bass
from concourse import mybir

F32 = mybir.dt.float32
BF16 = mybir.dt.bfloat16
F32R = mybir.dt.float32r
I32 = mybir.dt.int32
ALU = mybir.AluOpType
ACT = mybir.ActivationFunctionType
AX = mybir.AxisListType

P = 128
B, S = 2, 1024
T = B * S
NT = T // P
BT = S // P
HEADS, DH = 16, 8
HG = 4
GB = HEADS // HG
NG = B * GB
LAT = 32
E, FF = 8, 512
FC = FF // P
HALF = 512
NH = T // HALF
PIECES = 3
KR = PIECES * PIECES * DH
KM = KR + PIECES
KD = PIECES * DH
KX = (2 * PIECES - 1) * DH
SCALE = float(DH) ** -0.5
EPS_LN = 1e-5
EPS_NORM = 1e-6
BIG = 1e30
TOP = 2
MT = (TOP * T + E * (P - 1)) // P
RING = 3
AHEAD = 6
ROUND = 12
SAFE_SCORE = 60.0

C_ID, C_BLOCK, C_SEL, C_IOTA = 0, 128, 256, 384
C_HEAD = C_IOTA + NT * E
C_TRI = C_HEAD + HEADS
C_ONES = C_TRI + P
C_ROW = C_ONES + P
C_STEP = C_ROW + P
C_BEFORE = C_STEP + NT
C_PAIR = C_BEFORE + E * E
C_SPARE = C_PAIR + 2 * NT
C_PART = C_SPARE + MT
C_END = C_PART + 1
(V_BQ0, V_BK0, V_BL0, V_BQ1, V_CT) = (0, 1, 2, 3, 4)
V_EPS = V_CT + 2 * B
V_END = V_EPS + 1
R_BV0, R_BKV1, R_BO1 = 0, 128, 384
R_END = 512
(A_WQ0, A_WL0, A_RT0, A_WQ1, A_WKV1, A_WO1, A_RT1) = (0, 128, 160, 168, 296, 552, 680)
A_END = 688
W1_W = 2 * FF


def build(nc, x_in, consts_in, vecs_in, rows_in, attnw_in, lowrank_in, wo0_in, wmod_in, w2b_in, hb_in, up0_in,
          down0_in, shared1_in, exp1_in, out):
    q_scr = nc.dram_tensor("q_pieces", [NG, KD + PIECES, HG * S], BF16, kind="Internal").ap()
    k_scr = nc.dram_tensor("k_pieces", [NG, KX + PIECES, HG * S], BF16, kind="Internal").ap()

    h_scr = nc.dram_tensor("mixture_in", [T, P], F32, kind="Internal").ap()
    y_scr = [nc.dram_tensor(f"mixture_out{l}", [TOP * T + MT * P, P], F32, kind="Internal").ap() for l in range(2)]

    with ExitStack() as ctx:
        def sb(name, shape, dt=F32):
            return ctx.enter_context(nc.sbuf_tensor(name, shape, dt))

        def ps(name, shape):
            return ctx.enter_context(nc.psum_tensor(name, shape, F32))

        def sem(name):
            return ctx.enter_context(nc.semaphore(name))

        SAB = [ps(f"bank{i}{i + 1}", [P, 2 * HALF]) for i in (0, 2, 6)]
        B4, B5 = (ps(f"bank{i}", [P, HALF]) for i in (4, 5))
        B6, B7 = (SAB[2][:, i * HALF:(i + 1) * HALF] for i in range(2))

        logit_bank = (SAB[0][:, 0:NT * E], SAB[1][:, HALF:HALF + NT * E])

        consts = sb("consts", [P, C_END])
        ident = consts[:, C_ID:C_ID + P]
        block_mask = consts[:, C_BLOCK:C_BLOCK + P]
        den_sel = consts[:, C_SEL:C_SEL + P]
        iota = consts[:, C_IOTA:C_HEAD].rearrange("p (t e) -> p t e", e=E)
        vecs = sb("vecs", [P, V_END])
        rows = sb("rows", [P, R_END])
        attnw = sb("attnw", [P, A_END])
        lowrank = sb("lowrank", [LAT, 2 * P])
        wo0 = sb("wo0", [P, GB, P])
        wo0g = sb("wo0g", [P, B, GB, P])
        wo1g = sb("wo1g", [P, B, P])
        bo1g = sb("bo1g", [P, B, P])
        w2b = sb("w2b", [E, P])
        silu_c = sb("silu_c", [P, 2 * B])
        modc = sb("modc", [P, 2, 6, B])
        gmod = sb("gmod", [P, 2, 4, B, P])

        norms = sb("norms", [HEADS, B, 2, 2])
        norm_s = sb("norm_s", [HEADS, 4])
        worst = sb("worst", [1, 2])
        need_max = sb("need_max", [1, 1], mybir.dt.int32)

        X = sb("X", [P, NT, P])
        hT = sb("hT", [P, T])
        XN = sb("XN", [P, B, BT, P])
        GT = sb("GT", [P, E, NT])
        stats = sb("stats", [P, BT, 6])
        mv = sb("mv", [P, BT, 2])
        sd = sb("sd", [P, BT])
        rstd = sb("rstd", [P, BT])
        latT = sb("latT", [LAT, S])
        R5 = sb("R5", [P, E * FF])
        V_all = R5[:, 0:NG * BT * HG * DH].rearrange("p (g i h d) -> p g i h d", g=NG, i=BT, h=HG)
        Vg = R5[:, E * FF // 2:E * FF].rearrange("p (n i h d) -> p n i h d", n=2, i=BT, h=HG)
        W0dn = R5[:, :].rearrange("p (e w) -> p e w", e=E)
        R3 = sb("R3", [P, E * 2 * FF])
        Kb = R3[:, 0:HG * S].bitcast(BF16).rearrange("p (n t) -> p n t", n=2)
        Qb = R3[:, HG * S:2 * HG * S].bitcast(BF16).rearrange("p (n t) -> p n t", n=2)
        W0up = R3[:, :].rearrange("p (e w) -> p e w", e=E)
        mx = sb("mx", [P, 2, HG * BT])
        mneg = sb("mneg", [HG * BT, P])
        m3 = sb("m3", [HG * BT, 2, PIECES, P], BF16)
        gate_w = sb("gate_w", [P, 12, NT, E])
        gate_s = sb("gate_s", [P, 10, NT])
        gsel = sb("gsel", [P, TOP, NT])
        seen = sb("seen", [P, NT + 1, E])
        exp_s = sb("exp_s", [P, 3, E])
        slot = sb("slot", [P, 4, TOP, NT])
        slot_i = sb("slot_i", [P, 3, TOP, NT], I32)
        dst = sb("dst", [P, 3, MT])
        dst_i = sb("dst_i", [P, MT], I32)
        tok_i = sb("tok_i", [P, MT], I32)
        tile_w = sb("tile_w", [1, MT, E])
        tile_e = sb("tile_e", [1, MT])
        tile_i = sb("tile_i", [1, MT], I32)
        Wsh = sb("Wsh", [P, W1_W])

        R1 = sb("R1", [P, 10240])
        ACC = R1[:, E * W1_W:E * W1_W + T].rearrange("p (i d) -> p i d", d=P)
        qk32 = R1[:, 0:4 * S].rearrange("p (b n t) -> p b n t", b=B, n=2)
        pieces = R1[:, 4 * S:10 * S].bitcast(BF16).rearrange("p (b n j t) -> p b n j t", b=B, n=2, j=PIECES)
        At = R1[:, 0:NG * S].rearrange("p (g t) -> p g t", g=NG)
        W1 = R1[:, 0:E * W1_W].rearrange("p (e w) -> p e w", e=E)
        BR = R1[:, 0:E * 2 * FF].rearrange("p (e w) -> p e w", e=E)
        R2 = sb("R2", [P, 8192])
        wmod = R2[:, 4096:4096 + 12 * P].rearrange("p (l w) -> p l w", l=2)
        silu_cb = R2[:, 4096 + 12 * P:4096 + (12 + 2 * B) * P].rearrange("p (n d) -> p n d", d=P)
        PR = R2[:, :].rearrange("p (n h t) -> p n h t", n=4, h=HG)
        ZG, ZU = (R2[:, 2 * i * FF:2 * (i + 1) * FF].rearrange("p (n w) -> p n w", n=2) for i in range(2))
        H = R2[:, 0:2 * FC * HALF].rearrange("p (n f t) -> p n f t", n=2, f=FC)
        is_lane = R2[:, 4096:6144].bitcast(BF16).rearrange("p (n m) -> p n m", m=P)
        is_tile = R2[:, 6144:6144 + TOP * NT * MT // 2].bitcast(BF16).rearrange("p (n j) -> p n j", j=MT)
        in_tile = R2[:, 6144 + TOP * NT * MT // 2:6144 + 3 * TOP * NT * MT // 2].bitcast(BF16)\
            .rearrange("p (n w j) -> p n w j", w=2, j=MT)
        Yt = R2[:, 4096:8192].rearrange("p (c i d) -> p c i d", c=TOP, i=NT)
        KVW = 2 * P + 4
        attn1 = []
        for R in (R3, R2):
            ZQ, TQ, QF = (R[:, i * S:(i + 1) * S] for i in range(3))
            TK, KF = (R[:, i * S:(i + 1) * S].rearrange("p (i d) -> p i d", i=BT) for i in (3, 4))
            KVt = R[:, 5 * S:5 * S + BT * KVW].rearrange("p (i d) -> p i d", i=BT)
            KVB = R[:, 5 * S + BT * KVW:5 * S + BT * KVW + P + HEADS]
            NRM = R[:, 3 * S:3 * S + BT * HEADS].rearrange("p (i h) -> p i h", h=HEADS)
            attn1.append((ZQ, TQ, QF, TK, KF, KVt, KVB, NRM))
        gate_scratch = gate_w[:, :, :, :].rearrange("p n t e -> p (n t e)")
        gsign = gate_scratch[:, 0:2 * 2 * B * P]
        R4 = sb("R4", [P, 3 * HALF])
        PV_sb = R4[:, 0:2 * HALF].rearrange("p (n t) -> p n t", n=2)
        den_r = R4[:, 2 * HALF:3 * HALF]
        PV_hi, PV_lo = (sb(f"sums_part{i}", [P, HALF], F32R)[:, :] for i in range(2))
        sel_r = sb("den_selector", [P, P], F32R)[:, :]
        XgT = R4[:, 0:RING * P].rearrange("p (n d) -> p n d", n=RING)
        Yg = R4[:, RING * P:2 * RING * P].rearrange("p (n d) -> p n d", n=RING)
        act_out, hid, hidT = (R2[:, 4096 + 2 * i * FF:4096 + 2 * (i + 1) * FF].rearrange("p (n w) -> p n w", n=2) for i in range(3))
        Xg = R2[:, 4096 + 6 * FF:4096 + 6 * FF + AHEAD * P].rearrange("p (n d) -> p n d", n=AHEAD)
        lat = [latT[:, :], gate_scratch[0:LAT, 0:S]]
        gT = latT[0:E, :]
        SQ = R2[:, 6144:8192].rearrange("p (n t) -> p n t", n=2)
        zero_one = R2[:, 0:4096].bitcast(BF16).rearrange("p (n t) -> p n t", n=2)

        s_vecs, s_wm, s_small, s_wts = (sem(n) for n in ("vecs_loaded", "wmod_loaded", "small_loaded", "wts_loaded"))
        s_x = [sem(f"x_loaded_{b}") for b in range(B)]
        s_w0d, s_w0u, s_w1, s_br = (sem(n) for n in ("down0_loaded", "up0_loaded", "experts1_loaded", "bias_rows_loaded"))
        s_wo0 = sem("wo0_loaded")
        s_xm, s_hst = sem("mixture_in_ready"), sem("mixture_in_stored")
        s_wsh = sem("shared_loaded")
        s_dve, s_pool = sem("dve_chain"), sem("pool_chain")
        s_silu, s_scb, s_modmm, s_mod = sem("silu_c_ready"), sem("silu_cb_ready"), sem("mod_products"), sem("mod_ready")
        s_rowmm, s_row, s_rows = sem("mod_row_products"), sem("mod_rows_evacuated"), sem("mod_rows_ready")
        s_var, s_sd, s_xn, s_tr, s_ht = (sem(n) for n in ("var_ready", "sd_ready", "xn_ready", "xn_turned", "ht_ready"))
        s_lat, s_latsb, s_qmm, s_kmm, s_vmm = (sem(n) for n in ("lat_mm", "lat_ready", "q_mm", "k_mm", "v_mm"))
        s_qk, s_v, s_pc = sem("qk_evacuated"), sem("v_ready"), sem("pieces_ready")
        s_sq, s_nb, s_nr, s_nt, s_ntr, s_flag = (sem(n) for n in (
            "squares_ready", "norms_summed", "norms_taken", "norm_bound", "norm_bound_turned", "need_max_ready"))
        s_zo, s_scr = sem("zero_one_ready"), [sem(f"pieces_stored_{b}") for b in range(B)]
        s_scr2 = [sem("max_rows_even_stored"), sem("max_rows_odd_stored")]
        s_kq = [sem("kq_even_loaded"), sem("kq_odd_loaded")]
        s_kqx = [sem("first_max_rows_even_loaded"), sem("first_max_rows_odd_loaded")]
        s_mm, s_mred, s_mtr, s_m3, s_m3c = (sem(n) for n in ("max_scores", "max_taken", "max_turned", "max_split", "max_split_chain"))
        s_kqm = [sem("max_kq_even_loaded"), sem("max_kq_odd_loaded")]
        s_vz, s_vg = sem("vg_padding_ready"), sem("vg_ready")
        s_st, s_ex, s_pv, s_pve, s_den, s_denr, s_at = (sem(n) for n in (
            "scores_ready", "probs_ready", "pv_done", "pv_evacuated", "den_spread", "den_recip", "attn_normed"))
        s_wog, s_wo = sem("wo_scaled"), sem("wo_done")
        s_res = [sem(f"mixture_added_{b}") for b in range(B)]
        s_res2, s_xa = sem("mixture_added_1_by_dve"), sem("mixture_start_added")
        s_y0 = [sem(f"first_choice_weighted_{b}") for b in range(B)]
        s_lg, s_gx, s_ge, s_gate, s_gtr, s_gts, s_b2 = (sem(n) for n in (
            "logits_ready", "gate_exp_in", "gate_exp_out", "gates_ready", "gates_turned", "gates_t_ready", "bias2_ready"))
        s_acc0 = sem("acc_started")
        s_gm, s_y, s_o, s_ac = (sem(n) for n in ("shared_up", "shared_silu", "shared_down", "shared_taken"))
        s_ch, s_cnt, s_tile, s_oh, s_ohp, s_im, s_idx = (sem(n) for n in (
            "choices_ready", "pairs_counted", "tile_table_ready", "lane_table_ready", "tile_products_ready",
            "slots_inverted", "indices_ready"))

        def both(name):
            return [sem(f"{name}{l}") for l in range(2)]

        s_xg = [[sem(f"gathered{l}_{v}") for v in range(AHEAD)] for l in range(2)]
        s_sc = [[sem(f"scattered{l}_{v}") for v in range(RING)] for l in range(2)]
        s_xt, s_xte, s_g, s_u, s_ga, s_hh, s_hr, s_hre, s_dn, s_ys = (both(n) for n in (
            "tile_turned", "tile_t_ready", "tile_gate_mm", "tile_up_mm", "tile_act", "tile_hidden", "tile_hidden_turned",
            "tile_hidden_t", "tile_down_mm", "tile_out"))
        s_zg, s_zu = sem("tile_gate_with_bias"), sem("tile_up_with_bias")
        s_yt = [sem(f"mixture_out_loaded_{b}") for b in range(B)]
        s_q1, s_kv1, s_kvt, s_qe, s_ke, s_qf, s_kf, s_kvm, s_kvb, s_nn, s_ot, s_ott, s_oe = (sem(n) for n in (
            "q1_mm", "kv1_mm", "kv1_ready", "q_exp_ready", "k_exp_ready", "qf_ready", "kf_ready", "kv_sum", "kv_masked",
            "num_norm", "o_ready", "o_turned", "o_t_ready"))
        s_sel, s_ph, s_pl = sem("selector_ready"), sem("sums_first_part"), sem("sums_rest")
        s_r1 = sem("block1_attention_added")
        s_out = sem("out_stored")

        SMALL = 3
        WTS = 2
        LAST = NT - 4
        GI = GB
        ATT_UNITS = 2 * BT

        block = ctx.enter_context(nc.Block())

        @block.sync
        def _(sp):
            def load_x(b):
                sp.dma_start(X[:, b * BT:(b + 1) * BT, :], x_in[b].rearrange("(i p) d -> p i d", p=P)).then_inc(s_x[b], 16)

            sp.dma_start(vecs[:, :], vecs_in).then_inc(s_vecs, 16)
            load_x(0)
            sp.dma_start(wmod[:, :, :], wmod_in).then_inc(s_wm, 16)
            sp.dma_start(consts[:, :], consts_in).then_inc(s_small, 16)
            sp.dma_start(attnw[:, :], attnw_in).then_inc(s_wts, 16)
            load_x(1)
            sp.dma_start(lowrank[:, :], lowrank_in).then_inc(s_wts, 16)
            sp.dma_start(rows[:, :], rows_in).then_inc(s_small, 16)
            sp.dma_start(w2b[:, :], w2b_in).then_inc(s_small, 16)
            sp.dma_start(wo0[:, :, :], wo0_in).then_inc(s_wo0, 16)
            sp.dma_start(Wsh[:, :], shared1_in).then_inc(s_wsh, 16)
            sp.wait_ge(s_zo, 2)
            sp.dma_start(q_scr[:, KD:KD + PIECES, :], zero_one[0:NG * PIECES, 0, :]).then_inc(s_scr[0], 16)
            sp.dma_start(k_scr[:, KX:KX + PIECES, :], zero_one[0:NG * PIECES, 1, :]).then_inc(s_scr[0], 16)

            def load_products(g, k, signal):
                for turn in range(PIECES):
                    at = slice(turn * KD, (turn + 1) * KD)
                    sp.dma_start(Kb[at, k, :], k_scr[g, turn * DH:turn * DH + KD, :].rearrange("g r t -> (g r) t"))\
                      .then_inc(signal, 16)
                    sp.dma_start(Qb[at, k, :], q_scr[g, 0:KD, :].rearrange("g r t -> (g r) t")).then_inc(signal, 16)

            def load_max_rows(g, k, signal):
                sp.dma_start(Kb[KR:KM, k, :], k_scr[g, KX:KX + PIECES, :].rearrange("g r t -> (g r) t")).then_inc(signal, 16)
                sp.dma_start(Qb[KR:KM, k, :], q_scr[g, KD:KD + PIECES, :].rearrange("g r t -> (g r) t")).then_inc(signal, 16)

            for b in range(B):
                for n, scr in enumerate((q_scr, k_scr)):
                    sp.wait_ge(s_pc, 2 * b + n + 1)
                    for at in range((PIECES, 2 * PIECES - 1)[n]):
                        sp.dma_start(scr[b * GB:(b + 1) * GB, at * DH:(at + 1) * DH, :]
                                     .rearrange("g d (h t) -> g (d h) t", h=HG),
                                     pieces[:, b, n, at % PIECES, :]).then_inc(s_scr[b], 16)
                sp.wait_ge(s_scr[b], 16 * (2 * (b == 0) + 3 * PIECES - 1))
                if b == 0:
                    for k in range(2):
                        load_products(slice(k, k + 1), k, s_kqm[k])
                        load_max_rows(slice(k, k + 1), k, s_kqx[k])

            for k in range(2):
                sp.wait_ge(s_kqm[k], 32 * PIECES)
                sp.wait_ge(s_kqx[k], 32)
            sp.wait_ge(s_flag, 1)
            flag = sp.value_load(need_max[0:1, 0:1], min_val=0, max_val=1)
            with sp.If(flag != 0):
                with sp.Fori(1, NG // 2) as i:
                    for k in range(2):
                        sp.wait_ge(s_mm, (i * 2 + (k - 1)) * (HG * BT))
                        load_products(bass.ds(i * 2 + k, 1), k, s_kqm[k])
                for k in range(2):
                    sp.wait_ge(s_scr2[k], 16 * (NG // 2 + 1))
                sp.wait_ge(s_mm, NG * HG * BT)
                for k in range(2):
                    load_products(slice(k, k + 1), k, s_kq[k])
                    load_max_rows(slice(k, k + 1), k, s_kq[k])
            with sp.If(flag == 0):
                for k in range(2):
                    sp.sem_inc(s_kq[k], 32 * (PIECES + 1))
            with sp.Fori(1, NG // 2) as i:
                for k in range(2):
                    sp.wait_ge(s_st, (i * 2 + (k - 1)) * (2 * ATT_UNITS))
                    load_products(bass.ds(i * 2 + k, 1), k, s_kq[k])
                    load_max_rows(bass.ds(i * 2 + k, 1), k, s_kq[k])
            sp.wait_ge(s_st, NG * 2 * ATT_UNITS)
            for e in range(0, E, 2):
                sp.dma_start(W0up[:, e:e + 2, :], up0_in[:, e:e + 2, :]).then_inc(s_w0u, 16)
            sp.wait_ge(s_pv, NG * ATT_UNITS + 4)
            sp.dma_start(W0dn, down0_in).then_inc(s_w0d, 16)
            sp.wait_ge(s_wo, B)
            for e in range(0, E, 2):
                sp.dma_start(BR[:, e:e + 2, :], hb_in[e:e + 2, :].unsqueeze(0).to_broadcast([P, 2, 2 * FF])).then_inc(s_br, 16)

            def mixture_io(layer):
                for b in range(B):
                    sp.wait_ge(s_xm, layer * B + b + 1)
                    sp.dma_start(h_scr[b * S:(b + 1) * S, :].rearrange("(i p) d -> p i d", p=P),
                                 XN[:, b]).then_inc(s_hst, 16)
                for v in range(RING):
                    sp.wait_ge(s_sc[layer][v], 16 * len(range(v, MT, RING)))
                for b in range(B):
                    for c in range(TOP):
                        sp.dma_start(Yt[:, c, b * BT:(b + 1) * BT, :],
                                     y_scr[layer][c * T + b * S:c * T + (b + 1) * S, :].rearrange("(i p) d -> p i d", p=P))\
                          .then_inc(s_yt[b], 16)
                if layer == 0:
                    for e in range(0, E, 2):
                        sp.dma_start(W1[:, e:e + 2, :], exp1_in[:, e:e + 2, :]).then_inc(s_w1, 16)

            mixture_io(0)
            mixture_io(1)
            for b in range(B):
                sp.wait_ge(s_res[b], 2)
                if b:
                    sp.wait_ge(s_res2, 1)
                sp.dma_start(out[b].rearrange("(i p) d -> p i d", p=P), X[:, b * BT:(b + 1) * BT, :]).then_inc(s_out, 16)
            sp.wait_ge(s_out, 16 * B)

        def add_mixture(eng, link, layer, tiles, done):
            b, n = tiles.start // BT, len(tiles)
            at = slice(tiles.start, tiles.stop)
            eng.wait_ge(s_yt[b], 16 * TOP * (layer + 1))
            y0, y1 = (Yt[:, c, at, :] for c in range(TOP))
            link(eng.tensor_tensor(y1, y1, gsel[:, 1, at].unsqueeze(2).to_broadcast([P, n, P]), ALU.mult))
            eng.wait_ge(s_y0[b], layer + 1)
            link(eng.tensor_tensor(y0, y0, y1, ALU.add))
            link(eng.tensor_tensor(y0, y0, gmod[:, layer, 1, b, :].unsqueeze(1).to_broadcast([P, n, P]), ALU.mult))
            eng.tensor_tensor(X[:, at, :], X[:, at, :], y0, ALU.add).then_inc(done, 1)

        @block.gpsimd
        def _(pool):
            count = [0]

            def link(ins):
                count[0] += 1
                ins.then_inc(s_pool, 1)
                pool.wait_ge(s_pool, count[0])

            pool.memset(zero_one[0:NG * PIECES, 0, :], 0.0).then_inc(s_zo, 1)
            pool.memset(zero_one[0:NG * PIECES, 1, :], 1.0).then_inc(s_zo, 1)
            pool.memset(Vg[:, :, :, :, :], 0.0).then_inc(s_vz, 1)
            pool.wait_ge(s_vz, 1)
            pool.memset(Vg[:, :, :, :, DH:DH + 1], 1.0).then_inc(s_vz, 1)
            pool.wait_ge(s_vz, 2)
            pool.wait_ge(s_v, B * 2)
            pool.sem_inc(s_pv, 4)
            for k in range(2):
                pool.tensor_copy(Vg[:, k, :, :, 0:DH], V_all[:, k, :, :, :]).then_inc(s_vg, 1)
            with pool.Fori(1, NG // 2) as i:
                for k in range(2):
                    pool.wait_ge(s_pv, (i * 2 + (k - 1)) * ATT_UNITS + 4)
                    pool.tensor_copy(Vg[:, k, :, :, 0:DH],
                                     V_all[:, bass.ds(i * 2 + k, 1), :, :, :].rearrange("p g i h d -> p (g i) h d")).then_inc(s_vg, 1)

            for layer in range(2):
                def gather(j):
                    pool.indirect_dma_start(Xg[:, j % AHEAD, :], None, h_scr,
                                            bass.IndirectOffsetOnAxis(tok_i[:, j:j + 1], 0)).then_inc(s_xg[layer][j % AHEAD], 16)

                for b in range(B):
                    pool.wait_ge(s_tr, (2 * layer + 1) * B + b + 1)
                    scale, shift = (gmod[:, layer, kind, b, :].unsqueeze(1).to_broadcast([P, BT, P]) for kind in (2, 3))
                    link(pool.tensor_tensor(XN[:, b], XN[:, b], scale, ALU.mult))
                    pool.tensor_tensor(XN[:, b], XN[:, b], shift, ALU.add).then_inc(s_xm, 1)
                pool.wait_ge(s_tile, layer + 1)
                n = TOP * NT
                pool.tensor_tensor(in_tile[:, :, 1, :], is_tile,
                                   consts[:, C_PAIR:C_PAIR + n].unsqueeze(2).to_broadcast([P, n, MT]),
                                   ALU.mult).then_inc(s_ohp, 1)
                pool.wait_ge(s_idx, layer + 1)
                pool.wait_ge(s_hst, 16 * B * (layer + 1))
                for j in range(AHEAD):
                    gather(j)
                for j in range(MT):
                    if j + AHEAD < MT:
                        pool.wait_ge(s_xt[layer], j + 1)
                        gather(j + AHEAD)
                    pool.wait_ge(s_ys[layer], j + 1)
                    pool.indirect_dma_start(y_scr[layer], bass.IndirectOffsetOnAxis(dst_i[:, j:j + 1], 0),
                                            Yg[:, j % RING, :], None).then_inc(s_sc[layer][j % RING], 16)
                pool.wait_ge(s_xa, B * (layer + 1))
                add_mixture(pool, link, layer, range((BT, LAST)[layer], NT), s_res[1])

        @block.scalar
        def _(act):
            act.wait_ge(s_vecs, 16)
            act.activation(silu_c[:, :], vecs[:, V_CT:V_EPS], ACT.Silu).then_inc(s_silu, 1)

            def spread(v):
                act.wait_ge(s_var, v + 1)
                act.activation(sd[:, :], mv[:, :, 1], ACT.Sqrt, bias=vecs[:, V_EPS:V_END]).then_inc(s_sd, 1)

            def modulate(v):
                step, b = divmod(v, B)
                layer, c = divmod(step, 2)
                act.wait_ge(s_tr, v + 1)
                for half in range(2):
                    last = act.activation(hT[:, b * S + half * HALF:b * S + (half + 1) * HALF], (B6, B7)[half][:, :],
                                          ACT.Identity, scale=modc[:, layer, 3 * c + 1, b:b + 1],
                                          bias=modc[:, layer, 3 * c, b:b + 1])
                last.then_inc(s_ht, 1)

            def latent(b):
                for half in range(2):
                    act.wait_ge(s_lat, 2 * b + half + 1)
                    act.activation(lat[b][:, half * HALF:(half + 1) * HALF], (B4, B5)[half][0:LAT, :], ACT.Identity,
                                   bias=vecs[0:LAT, V_BL0:V_BL0 + 1]).then_inc(s_latsb, 1)

            def first_piece(b, n):
                act.wait_ge((s_qmm, s_kmm)[n], b + 1)
                bias = vecs[:, V_BQ0 + n:V_BQ0 + n + 1]
                act.activation(pieces[:, b, n, 0, :], SAB[n][:, :], ACT.Identity, bias=bias)
                if b:
                    act.wait_ge(s_nb, 2 * n + 2)
                act.activation(SQ[:, n, :], SAB[n][:, :], ACT.Square, bias=bias).then_inc(s_sq, 1)

            spread(0)
            modulate(0)
            latent(0)
            spread(1)
            first_piece(0, 0)
            modulate(1)
            first_piece(0, 1)
            latent(1)
            first_piece(1, 0)
            first_piece(1, 1)
            act.wait_ge(s_rowmm, 1)
            act.activation(gmod[:, :, 0:2].rearrange("p l k b d -> p l (k b d)"),
                           SAB[0][:, :].rearrange("p (l w) -> p l w", l=2), ACT.Copy).then_inc(s_row, 1)

            act.wait_ge(s_flag, 1)
            flag = act.value_load(need_max[0:1, 0:1], min_val=0, max_val=1)
            with act.If(flag != 0):
                for k in range(2):
                    act.wait_ge(s_kqx[k], 32)
                    act.sem_inc(s_scr2[k], 16)
                with act.Fori(0, NG // 2) as i:
                    for k in range(2):
                        act.wait_ge(s_m3, i * 2 + k + 1)
                        act.dma_start(q_scr[bass.ds(i * 2 + k, 1), KD:KD + PIECES, :].rearrange("g r (x t) -> (g x) r t", t=P),
                                      m3[:, k, :, :]).then_inc(s_scr2[k], 16)

            act.sem_inc(s_ex, 3)
            with act.Fori(0, NG // GI) as i:
                for v in range(GI * ATT_UNITS):
                    n = i * (GI * ATT_UNITS) + v
                    for pair in range(2):
                        act.wait_ge(s_st, n * 2 + (pair + 1))
                        act.wait_ge(s_pv, n + 1)
                        act.activation(PR[:, v % 4, 2 * pair:2 * pair + 2, :], SAB[(2 * v + pair) % 3][:, :].rearrange("p (h t) -> p h t", h=2),
                                       ACT.Exp, scale=SCALE).then_inc(s_ex, 1)

            def gate_exp(layer):
                act.wait_ge(s_gx, layer + 1)
                if layer == 0:
                    act.activation(gate_w[:, 1], gate_w[:, 0], ACT.Exp).then_inc(s_ge, 1)
                else:
                    act.activation(gate_s[:, 5], gate_s[:, 4], ACT.Exp).then_inc(s_ge, 1)

            def expert_tiles(layer):
                def activate(i, k):
                    if layer == 0:
                        act.wait_ge(s_zg, i * 2 + (k + 1))
                        act.activation(act_out[:, k % 2, :], ZG[:, k % 2, :], ACT.Gelu).then_inc(s_ga[0], 1)
                    else:
                        act.wait_ge(s_g[1], i * 2 + (k + 1))
                        act.activation(hid[:, k % 2, :], SAB[0][:, (k % 2) * HALF:(k % 2 + 1) * HALF], ACT.Silu)\
                           .then_inc(s_hh[1], 1)

                def turned_hidden(i, k):
                    act.wait_ge(s_hr[layer], i * 2 + (k + 1))
                    act.activation(hidT[:, k % 2, :], SAB[1][:, 0:HALF], ACT.Copy).then_inc(s_hre[layer], 1)

                activate(0, 0)
                with act.Fori(0, (MT - 1) // 2) as i:
                    for k in range(2):
                        activate(i, k + 1)
                        turned_hidden(i, k)
                turned_hidden(0, MT - 1)
                for b in range(B):
                    act.wait_ge(s_yt[b], 16 * TOP * (layer + 1))
                    for t in range(b * BT, (b + 1) * BT):
                        last = act.activation(Yt[:, 0, t, :], Yt[:, 0, t, :], ACT.Copy, scale=gsel[:, 0, t:t + 1])
                    last.then_inc(s_y0[b], 1)

            for b in range(B):
                spread(B + b)
                modulate(B + b)
            gate_exp(0)
            for b in range(B):
                act.wait_ge(s_gtr, b + 1)
                act.activation(gT[:, :], SAB[1][0:E, :], ACT.Copy).then_inc(s_gts, 1)
                act.wait_ge(s_b2, b + 1)
                for half in range(2):
                    last = act.activation(ACC[:, b * BT + half * BT // 2:b * BT + (half + 1) * BT // 2, :],
                                          (B4, B5)[half][:, :].rearrange("p (i d) -> p i d", d=P), ACT.Copy)
                last.then_inc(s_acc0, 1)
            expert_tiles(0)

            def q_features(b):
                ZQ, TQ = attn1[b][:2]
                act.wait_ge(s_q1, b + 1)
                act.activation(ZQ, SAB[0][:, :], ACT.Relu, bias=vecs[:, V_BQ1:V_BQ1 + 1])
                act.activation(TQ, SAB[0][:, :], ACT.Exp, bias=vecs[:, V_BQ1:V_BQ1 + 1]).then_inc(s_qe, 1)

            def k_features(b):
                TK, KF, KVt = attn1[b][3:6]
                act.wait_ge(s_kvt, b + 1)
                act.activation(TK, KVt[:, :, 0:P], ACT.Exp)
                act.activation(KF, KVt[:, :, 0:P], ACT.Relu).then_inc(s_ke, 1)

            def attention_out(b):
                act.wait_ge(s_ott, b + 1)
                for half in range(2):
                    last = act.activation(attn1[b][1][:, half * HALF:(half + 1) * HALF], ((B6, B7), (B4, B5))[b][half][:, :], ACT.Copy)
                last.then_inc(s_oe, 1)

            spread(2 * B)
            modulate(2 * B)
            spread(2 * B + 1)
            q_features(0)
            modulate(2 * B + 1)
            k_features(0)
            q_features(1)
            k_features(1)
            attention_out(0)
            attention_out(1)
            def shared_silu(v, f):
                act.wait_ge(s_gm, v * FC + f + 1)
                if f == 0 and v >= 2:
                    act.wait_ge(s_o, v - 1)
                act.activation(H[:, v % 2, f, :], SAB[0][:, (f % 2) * HALF:(f % 2 + 1) * HALF],
                               ACT.Silu).then_inc(s_y, 1)

            def shared_out(v):
                act.wait_ge(s_o, v + 1)
                act.activation(ACC[:, v * (HALF // P):(v + 1) * (HALF // P), :],
                               (B4, B5)[v % 2][:, :].rearrange("p (i d) -> p i d", d=P), ACT.Copy).then_inc(s_ac, 1)

            spread(3 * B)
            modulate(3 * B)
            act.sem_inc(s_y, 2)
            spread(3 * B + 1)
            shared_silu(0, 0)
            shared_silu(0, 1)
            modulate(3 * B + 1)
            shared_silu(0, 2)
            shared_silu(0, 3)
            for v in range(1, NH):
                for f in range(FC):
                    shared_silu(v, f)
                shared_out(v - 1)
            shared_out(NH - 1)
            gate_exp(1)
            expert_tiles(1)

        @block.vector
        def _(dve):
            count = [0]

            def link(ins):
                count[0] += 1
                ins.then_inc(s_dve, 1)
                dve.wait_ge(s_dve, count[0])

            tt, ts, stt, copy = dve.tensor_tensor, dve.tensor_scalar, dve.scalar_tensor_tensor, dve.tensor_copy

            def layer_norm(v):
                step, b = divmod(v, B)
                if step == 0:
                    dve.wait_ge(s_x[b], 16)
                xb = [X[:, b * BT + i, :] for i in range(BT)]
                for i in range(BT):
                    last = dve.bn_stats(stats[:, i, :], xb[i])
                link(last)
                for i in range(BT):
                    last = dve.bn_aggr(mv[:, i, :], stats[:, i, :])
                last.then_inc(s_var, 1)
                dve.wait_ge(s_sd, v + 1)
                link(dve.reciprocal(rstd[:, :], sd[:, :]))
                if step >= 1:
                    dve.wait_ge(s_tr, v - 1)
                if step == 2:
                    dve.wait_ge(s_hst, 16 * (b + 1))
                for i in range(BT):
                    last = ts(XN[:, b, i, :], xb[i], mv[:, i, 0:1], rstd[:, i:i + 1], ALU.subtract, ALU.mult)
                last.then_inc(s_xn, 1)

            dve.wait_ge(s_silu, 1)
            copy(silu_cb[:, :, :], silu_c[:, :].unsqueeze(2).to_broadcast([P, 2 * B, P])).then_inc(s_scb, 1)
            layer_norm(0)
            dve.wait_ge(s_modmm, 1)
            link(copy(modc[:, :, :, :], B4[:, 0:2 * 6 * B].rearrange("p (l c b) -> p l c b", l=2, c=6)))
            for c in (1, 4):
                last = ts(modc[:, :, c, :], modc[:, :, c, :], 1.0, None, ALU.add)
            last.then_inc(s_mod, 1)
            layer_norm(1)

            def later_pieces(b, n):
                dve.wait_ge(s_sq, 2 * b + n + 1)
                z = qk32[:, b, n, :]
                stt(out=z, in0=SAB[n][:, :], scalar=vecs[:, V_BQ0 + n:V_BQ0 + n + 1], in1=pieces[:, b, n, 0, :],
                    op0=ALU.add, op1=ALU.subtract).then_inc(s_qk, 1)
                dve.wait_ge(s_qk, 2 * b + n + 1)
                link(copy(pieces[:, b, n, 1, :], z))
                tt(pieces[:, b, n, 2, :], z, pieces[:, b, n, 1, :], ALU.subtract).then_inc(s_pc, 1)

            def values(b):
                for half in range(2):
                    dve.wait_ge(s_vmm, 2 * b + half + 1)
                    for i in range(BT // 2):
                        last = tt(V_all[:, b * GB:(b + 1) * GB, half * BT // 2 + i, :, :],
                                  (B4, B5)[half][:, i * P:(i + 1) * P].rearrange("p (g h d) -> p g h d", g=GB, h=HG),
                                  rows[:, R_BV0:R_BV0 + P].rearrange("p (g h d) -> p g h d", g=GB, h=HG), ALU.add)
                    last.then_inc(s_v, 1)

            dve.wait_ge(s_small, 16 * SMALL)
            for b in range(B):
                later_pieces(b, 0)
                later_pieces(b, 1)
                values(b)
                for n in range(2):
                    for half in range(2):
                        dve.wait_ge(s_nb, (2 * b + n) * 2 + half + 1)
                        dve.tensor_reduce(norms[:, b, n, half:half + 1], (B6, B7)[half][0:HEADS, :], AX.X,
                                          ALU.max).then_inc(s_nr, 1)
            copy(sel_r, den_sel).then_inc(s_sel, 1)
            dve.wait_ge(s_nr, 4 * B)
            link(dve.tensor_reduce(norm_s[:, :], norms[:, :, :, :].rearrange("p b n h -> p (b n) h"), AX.X, ALU.max))
            for b in range(B):
                last = tt(norms[:, b, 0, 0:1], norm_s[:, 2 * b:2 * b + 1], norm_s[:, 2 * b + 1:2 * b + 2], ALU.mult)
            link(last)
            tt(norm_s[:, 0:1], norms[:, 0, 0, 0:1], norms[:, 1, 0, 0:1], ALU.max).then_inc(s_nt, 1)
            dve.wait_ge(s_rowmm, 1)
            for kind in (2, 3):
                last = copy(gmod[:, :, kind].rearrange("p l b d -> p l (b d)"),
                            SAB[1][:, :].rearrange("p (l k w) -> p l k w", l=2, k=2)[:, :, kind - 2, :])
            last.then_inc(s_row, 1)
            dve.wait_ge(s_ntr, 1)
            link(dve.tensor_reduce(worst[:, 0:1], B6[0:1, 0:HEADS], AX.X, ALU.max))
            link(ts(worst[:, 1:2], worst[:, 0:1], (SAFE_SCORE / SCALE) ** 2, None, ALU.is_le))
            ts(need_max[:, :], worst[:, 1:2], -1.0, 1.0, ALU.mult, ALU.add).then_inc(s_flag, 1)

            dve.wait_ge(s_flag, 1)
            flag = dve.value_load(need_max[0:1, 0:1], min_val=0, max_val=1)
            with dve.If(flag != 0):
                dve.sem_inc(s_mred, 2)
                with dve.Fori(0, NG // 2) as i:
                    for k in range(2):
                        g = i * 2 + k
                        for item in range(HG * BT):
                            dve.wait_ge(s_mm, g * (HG * BT) + (item + 1))
                            dve.tensor_reduce(mx[:, k, item:item + 1], SAB[item % 2][:, :], AX.X, ALU.max).then_inc(s_mred, 1)
                        dve.wait_ge(s_mtr, g + 1)
                        ts(mneg[:, :], B4[0:HG * BT, 0:P], -1.0, None, ALU.mult).then_inc(s_m3c, 1)
                        dve.wait_ge(s_m3c, g * 5 + 1)
                        dve.wait_ge(s_scr2[k], i * 16 + 16)
                        copy(m3[:, k, 0, :], mneg[:, :]).then_inc(s_m3c, 1)
                        dve.wait_ge(s_m3c, g * 5 + 2)
                        tt(mneg[:, :], mneg[:, :], m3[:, k, 0, :], ALU.subtract).then_inc(s_m3c, 1)
                        dve.wait_ge(s_m3c, g * 5 + 3)
                        copy(m3[:, k, 1, :], mneg[:, :]).then_inc(s_m3c, 1)
                        dve.wait_ge(s_m3c, g * 5 + 4)
                        tt(mneg[:, :], mneg[:, :], m3[:, k, 1, :], ALU.subtract).then_inc(s_m3c, 1)
                        dve.wait_ge(s_m3c, g * 5 + 5)
                        copy(m3[:, k, 2, :], mneg[:, :]).then_inc(s_m3, 1)

            dve.wait_ge(s_row, 2)
            link(ts(gmod[:, :, 2].rearrange("p l b d -> p l (b d)"), gmod[:, :, 2].rearrange("p l b d -> p l (b d)"),
                    1.0, None, ALU.add))
            gm = gmod[:, :, 0:2].rearrange("p l k b d -> p l (k b d)")
            gs = gsign.rearrange("p (l w) -> p l w", l=2)
            link(ts(gs, gm, 0.0, None, ALU.is_ge))
            link(ts(gs, gs, 2.0, -1.0, ALU.mult, ALU.add))
            link(stt(out=gm, in0=gm, scalar=-1.0, in1=gm, op0=ALU.mult, op1=ALU.max))
            stt(out=gm, in0=gm, scalar=0.25, in1=gs, op0=ALU.max, op1=ALU.mult).then_inc(s_rows, 1)
            dve.wait_ge(s_rows, 1)
            dve.wait_ge(s_wo0, 16)
            for b in range(B):
                tt(wo0g[:, b], wo0[:, :, :], gmod[:, 0, 0, b, :].unsqueeze(1).to_broadcast([P, GB, P]), ALU.mult).then_inc(s_wog, 1)
                tt(wo1g[:, b], attnw[:, A_WO1:A_WO1 + P], gmod[:, 1, 0, b, :], ALU.mult).then_inc(s_wog, 1)
                link(tt(bo1g[:, b], rows[:, R_BO1:R_BO1 + P], gmod[:, 1, 0, b, :], ALU.mult))

            dve.sem_inc(s_denr, 2)
            with dve.Fori(0, NG // GI) as i:
                for k in range(GI):
                    g = i * GI + k
                    for qh in range(2):
                        r = g * 2 + qh
                        dve.wait_ge(s_pv, r * BT + (BT + 4))
                        copy(PV_sb[:, qh, :], (B4, B5)[qh][:, :]).then_inc(s_pve, 1)
                        dve.wait_ge(s_pve, r + 1)
                        copy(PV_hi, PV_sb[:, qh, :]).then_inc(s_ph, 1)
                        dve.wait_ge(s_ph, r + 1)
                        tt(PV_lo, PV_sb[:, qh, :], PV_hi.bitcast(F32), ALU.subtract).then_inc(s_pl, 1)
                        dve.wait_ge(s_den, r + 1)
                        dve.reciprocal(den_r[:, :], (B4, B5)[qh][:, :]).then_inc(s_denr, 1)
                        dve.wait_ge(s_denr, r + 3)
                        tt(At[:, bass.ds(g, 1), qh * HALF:(qh + 1) * HALF].rearrange("p g t -> p (g t)"),
                           PV_sb[:, qh, :], den_r[:, :], ALU.mult).then_inc(s_at, 1)

            def residual(j, banks, bias=None):
                b = j % B
                dve.wait_ge(s_wo, j + 1)
                for half in range(2):
                    x = X[:, b * BT + half * BT // 2:b * BT + (half + 1) * BT // 2, :]
                    last = tt(x, x, banks[half].rearrange("p (i d) -> p i d", d=P), ALU.add)
                if bias is not None:
                    link(last)
                    x = X[:, b * BT:(b + 1) * BT, :]
                    tt(x, x, bias.unsqueeze(1).to_broadcast([P, BT, P]), ALU.add).then_inc(s_r1, 1)
                    dve.wait_ge(s_r1, b + 1)
                else:
                    link(last)


            def wide(col, n=E):
                return col.unsqueeze(2).to_broadcast([P, col.shape[1], n])

            def gates(layer):
                w = [gate_w[:, i] for i in range(12)]
                s = [gate_s[:, i] for i in range(8)]
                dve.wait_ge(s_lg, layer + 1)
                logits = logit_bank[layer].rearrange("p (t e) -> p t e", e=E)
                if layer == 0:
                    link(dve.tensor_reduce(s[0], logits, AX.X, ALU.max))
                    tt(w[0], logits, wide(s[0]), ALU.subtract).then_inc(s_gx, 1)
                    dve.wait_ge(s_ge, 1)
                    link(dve.tensor_reduce(s[1], w[1], AX.X, ALU.add))
                    link(dve.reciprocal(s[2], s[1]))
                    link(tt(w[3], w[1], wide(s[2]), ALU.mult))
                else:
                    link(copy(w[3], logits))
                link(dve.tensor_reduce(s[3], w[3], AX.X, ALU.max))
                link(tt(w[4], w[3], wide(s[3]), ALU.not_equal))
                link(stt(out=w[4], in0=w[4], scalar=100.0, in1=iota, op0=ALU.mult, op1=ALU.add))
                link(dve.tensor_reduce(s[6], w[4], AX.X, ALU.min))
                link(tt(w[5], iota, wide(s[6]), ALU.is_equal))
                link(stt(out=w[6], in0=w[5], scalar=-BIG, in1=w[3], op0=ALU.mult, op1=ALU.add))
                link(dve.tensor_reduce(s[7], w[6], AX.X, ALU.max))
                link(tt(w[7], w[6], wide(s[7]), ALU.not_equal))
                link(stt(out=w[7], in0=w[7], scalar=100.0, in1=iota, op0=ALU.mult, op1=ALU.add))
                link(dve.tensor_reduce(s[6], w[7], AX.X, ALU.min))
                link(tt(w[8], iota, wide(s[6]), ALU.is_equal))
                tt(w[9], w[5], w[8], ALU.add).then_inc(s_ch, 1)
                if layer == 0:
                    copy(gsel[:, 0, :], s[3])
                    link(copy(gsel[:, 1, :], s[7]))
                    link(tt(w[10], w[5], wide(s[3]), ALU.mult))
                    link(tt(w[11], w[8], wide(s[7]), ALU.mult))
                    tt(GT[:, :, :].rearrange("p e t -> p t e"), w[10], w[11], ALU.add).then_inc(s_gate, 1)
                else:
                    tt(s[4], s[7], s[3], ALU.subtract).then_inc(s_gx, 1)

            def second_gates():
                s = [gate_s[:, i] for i in range(8)]
                dve.wait_ge(s_ge, 2)
                link(ts(s[0], s[5], 1.0, None, ALU.add))
                link(dve.reciprocal(gsel[:, 0, :], s[0]))
                link(tt(gsel[:, 1, :], s[5], gsel[:, 0, :], ALU.mult))

            def slots(layer):
                w = [gate_w[:, i] for i in range(12)]
                dve.wait_ge(s_cnt, layer + 1)
                before, totals = (B6[:, i * P:(i + 1) * P].rearrange("p (t e) -> p t e", e=E) for i in range(2))
                dve.memset(seen[:, 0, :], 0.0)
                dve.wait_ge(s_gate, 1)
                sums = w[11]
                link(copy(sums, totals))
                for step in range(4):
                    n = 1 << step
                    wider = seen[:, 1:NT + 1, :] if 2 * n == NT else w[10 + step % 2]
                    copy(wider[:, 0:n, :], sums[:, 0:n, :])
                    link(tt(wider[:, n:NT, :], sums[:, n:NT, :], sums[:, 0:NT - n, :], ALU.add))
                    sums = wider
                cmp = w[10][:, :, :].rearrange("p t e -> p (t e)").rearrange("p (e j) -> p e j", e=E)
                link(tt(cmp, seen[:, NT, :].unsqueeze(2).to_broadcast([P, E, NT]),
                        consts[:, C_STEP:C_STEP + NT].unsqueeze(1).to_broadcast([P, E, NT]), ALU.is_gt))
                link(dve.tensor_reduce(exp_s[:, 0, :], cmp, AX.X, ALU.add))
                pre = w[11][:, 0:E, :]
                link(tt(pre, exp_s[:, 0, :].unsqueeze(1).to_broadcast([P, E, E]),
                        consts[:, C_BEFORE:C_BEFORE + E * E].rearrange("p (e f) -> p e f", e=E), ALU.mult))
                link(dve.tensor_reduce(exp_s[:, 1, :], pre, AX.X, ALU.add))
                link(tt(exp_s[:, 2, :], exp_s[:, 1, :], exp_s[:, 0, :], ALU.add))
                link(stt(out=w[9], in0=exp_s[:, 1, :].unsqueeze(1).to_broadcast([P, NT, E]), scalar=float(P),
                         in1=seen[:, 0:NT, :], op0=ALU.mult, op1=ALU.add))
                link(tt(w[9], w[9], before, ALU.add))
                for c, chosen in enumerate((w[5], w[8])):
                    link(tt(w[10], w[9], chosen, ALU.mult))
                    link(dve.tensor_reduce(slot[:, 0, c, :], w[10], AX.X, ALU.add))
                link(copy(slot_i[:, 0], slot[:, 0]))
                ts(slot_i[:, 1], slot_i[:, 0], 7, None, ALU.logical_shift_right)
                link(ts(slot_i[:, 2], slot_i[:, 0], P - 1, None, ALU.bitwise_and))
                link(copy(slot[:, 1:3], slot_i[:, 1:3]))
                tile = slot[:, 1].rearrange("p c t -> p (c t)")
                lane = slot[:, 2].rearrange("p c t -> p (c t)")
                n = TOP * NT
                tt(is_tile, consts[:, C_ROW:C_ROW + MT].unsqueeze(1).to_broadcast([P, n, MT]), wide(tile, MT),
                   ALU.is_equal).then_inc(s_tile, 1)
                tt(is_lane, consts[:, C_ROW:C_ROW + P].unsqueeze(1).to_broadcast([P, n, P]), wide(lane, P), ALU.is_equal)
                dve.wait_ge(s_tile, layer + 1)
                ts(in_tile[:, :, 0, :], is_tile, consts[:, C_PART:C_PART + 1], None, ALU.mult).then_inc(s_oh, 1)
                link(tt(tile_w[:, :, :], consts[0:1, C_ROW:C_ROW + MT].unsqueeze(2).to_broadcast([1, MT, E]),
                        exp_s[0:1, 2, :].unsqueeze(1).to_broadcast([1, MT, E]), ALU.is_ge))
                link(dve.tensor_reduce(tile_e[:, :], tile_w[:, :, :], AX.X, ALU.add))
                link(ts(tile_i[:, :], tile_e[:, :], float(E - 1), None, ALU.min))

            def indices(layer):
                dve.wait_ge(s_im, layer + 1)
                lane, pair = B7[:, 0:MT], B7[:, MT:2 * MT]
                link(copy(dst[:, 0, :], pair))
                link(stt(out=dst[:, 1, :], in0=dst[:, 0, :], scalar=float(P), in1=lane, op0=ALU.mult, op1=ALU.add))
                link(ts(dst[:, 0, :], dst[:, 0, :], 0.0, None, ALU.is_equal))
                link(tt(dst[:, 0, :], dst[:, 0, :], consts[:, C_SPARE:C_SPARE + MT], ALU.mult))
                link(stt(out=dst[:, 1, :], in0=dst[:, 1, :], scalar=-float(P), in1=dst[:, 0, :], op0=ALU.add, op1=ALU.add))
                link(copy(dst_i[:, :], dst[:, 1, :]))
                ts(tok_i[:, :], dst_i[:, :], T - 1, None, ALU.bitwise_and).then_inc(s_idx, 1)

            def expert_tiles(layer):
                def turned_in(i, k):
                    dve.wait_ge(s_xt[layer], i * ROUND + (k + 1))
                    copy(XgT[:, k % RING, :], B6[:, 0:P]).then_inc(s_xte[layer], 1)

                def add_biases(i, k):
                    e = dve.value_load(tile_i[0:1, bass.ds(i * ROUND + k, 1)], min_val=0, max_val=E - 1)
                    for n, (z, bank, done, ready) in enumerate(((ZG, (SAB[0][:, 0:HALF], B4[:, :]), s_g[0], s_zg),
                                                                (ZU, (SAB[0][:, HALF:2 * HALF], B5[:, :]), s_u[0], s_zu))):
                        dve.wait_ge(done, i * ROUND + (k + 1))
                        tt(z[:, k % 2, :], bank[k % 2], BR[:, bass.ds(e, 1), n * FF:(n + 1) * FF].rearrange("p e w -> p (e w)"),
                           ALU.add).then_inc(ready, 1)

                def multiply(i, k):
                    dve.wait_ge(s_zu, i * ROUND + (k + 1))
                    dve.wait_ge(s_ga[0], i * ROUND + (k + 1))
                    tt(hid[:, k % 2, :], ZU[:, k % 2, :], act_out[:, k % 2, :], ALU.mult).then_inc(s_hh[0], 1)

                def out(i, k):
                    dve.wait_ge(s_dn[layer], i * ROUND + (k + 1))
                    if not isinstance(i, int) or i * ROUND + k >= RING:
                        dve.wait_ge(s_sc[layer][k % RING], i * (ROUND // RING * 16) + k // RING * 16)
                    copy(Yg[:, k % RING, :], SAB[1][:, HALF:HALF + P]).then_inc(s_ys[layer], 1)

                def unit(i, k):
                    j = i * ROUND + k if isinstance(i, int) else ROUND
                    if layer == 0 and j < MT:
                        add_biases(i, k)
                        multiply(i, k)
                    if j >= 2:
                        out(i, k - 2)
                    if j + 2 < MT:
                        turned_in(i, k + 2)

                def add_start(b):
                    a, x = ACC[:, b * BT:(b + 1) * BT, :], X[:, b * BT:(b + 1) * BT, :]
                    dve.wait_ge((s_acc0, s_ac)[layer], (B, NH)[layer])
                    link(tt(a, a, gmod[:, layer, 1, b, :].unsqueeze(1).to_broadcast([P, BT, P]), ALU.mult))
                    tt(x, x, a, ALU.add).then_inc(s_xa, 1)

                for k in range(2):
                    turned_in(0, k)
                for k in range(ROUND):
                    unit(0, k)
                    if layer == 1 and k == ROUND // 2 - 2:
                        second_gates()
                    if k in (ROUND // 2, ROUND - 2):
                        add_start(k // (ROUND - 2))
                with dve.Fori(1, MT // ROUND) as i:
                    for k in range(ROUND):
                        unit(i, k)
                for k in range(MT % ROUND + 2):
                    unit(MT // ROUND, k)

            residual(0, (SAB[1][:, 0:HALF], SAB[1][:, HALF:2 * HALF]))
            layer_norm(B)
            residual(1, (B4[:, :], B5[:, :]))
            layer_norm(B + 1)
            gates(0)
            slots(0)
            indices(0)
            dve.wait_ge(s_br, 16 * (E // 2))
            expert_tiles(0)
            add_mixture(dve, link, 0, range(0, BT), s_res[0])
            dve.wait_ge(s_res[0], 1)

            def keys_values(b):
                KVt = attn1[b][5]
                dve.wait_ge(s_kv1, b + 1)
                for src, i0, ni in ((SAB[1], 0, 4), (B4, 4, 2), (B5, 6, 2)):
                    last = tt(KVt[:, i0:i0 + ni, 0:2 * P], src[:, :].rearrange("p (i d) -> p i d", d=2 * P),
                              rows[:, R_BKV1:R_BKV1 + 2 * P].unsqueeze(1).to_broadcast([P, ni, 2 * P]), ALU.add)
                last.then_inc(s_kvt, 1)

            def features(b):
                ZQ, TQ, QF = attn1[b][:3]
                dve.wait_ge(s_qe, b + 1)
                stt(out=QF, in0=TQ, scalar=1.0, in1=ZQ, op0=ALU.min, op1=ALU.add).then_inc(s_qf, 1)

            def key_features(b):
                TK, KF = attn1[b][3:5]
                dve.wait_ge(s_ke, b + 1)
                stt(out=KF, in0=TK, scalar=1.0, in1=KF, op0=ALU.min, op1=ALU.add).then_inc(s_kf, 1)

            def own_head(b):
                KVB = attn1[b][6]
                dve.wait_ge(s_kvm, b + 1)
                tt(KVB[:, 0:P], B6[:, 0:P], block_mask, ALU.mult)
                ts(KVB[:, P:P + HEADS], block_mask.rearrange("p (h d) -> p h d", h=HEADS)[:, :, 0], B6[:, P:P + 1], None,
                   ALU.mult).then_inc(s_kvb, 1)

            def normalise(b):
                ZQ, NRM = attn1[b][0], attn1[b][7]
                dve.wait_ge(s_nn, b + 1)
                link(ts(NRM, B7[:, 0:BT * HEADS].rearrange("p (i h) -> p i h", h=HEADS), EPS_NORM, None, ALU.max))
                link(dve.reciprocal(NRM, NRM))
                tt(ZQ.rearrange("p (i h d) -> p i h d", i=BT, h=HEADS),
                   SAB[b][:, :].rearrange("p (i h d) -> p i h d", i=BT, h=HEADS),
                   NRM.unsqueeze(3).to_broadcast([P, BT, HEADS, DH]), ALU.mult).then_inc(s_ot, 1)

            for b in range(B):
                if b:
                    dve.wait_ge(s_res[b], 1)
                layer_norm(2 * B + b)
            for b in range(B):
                dve.memset(attn1[b][5][:, :, 2 * P:2 * P + 1], 1.0)
            keys_values(0)
            features(0)
            key_features(0)
            own_head(0)
            keys_values(1)
            features(1)
            normalise(0)
            key_features(1)
            own_head(1)
            residual(B, (SAB[0][:, 0:HALF], SAB[0][:, HALF:2 * HALF]), bo1g[:, 0, :])
            normalise(1)
            layer_norm(3 * B)
            residual(B + 1, (SAB[1][:, 0:HALF], SAB[1][:, HALF:2 * HALF]), bo1g[:, 1, :])
            layer_norm(3 * B + 1)

            gates(1)
            slots(1)
            indices(1)
            expert_tiles(1)
            add_mixture(dve, link, 1, range(0, BT), s_res[0])
            add_mixture(dve, link, 1, range(BT, LAST), s_res2)

        @block.tensor
        def _(pe):
            mm = pe.matmul

            def keep_warm(n):
                for _ in range(n):
                    mm(B4[:, 0:P], ident, ident, start=True, stop=True)

            pe.wait_ge(s_wm, 16)
            pe.wait_ge(s_silu, 1)
            for l in range(2):
                for c in range(6):
                    o = (l * 6 + c) * B
                    last = mm(B4[:, o:o + B], wmod[:, l, c * P:(c + 1) * P], silu_c[:, l * B:(l + 1) * B], start=True, stop=True)
            last.then_inc(s_modmm, 1)

            def turn(v):
                pe.wait_ge(s_xn, v + 1)
                if v:
                    pe.wait_ge(s_ht, v)
                for i in range(BT):
                    last = pe.transpose((B6, B7)[i // 4][:, (i % 4) * P:(i % 4 + 1) * P], XN[:, v % B, i, :], ident)
                last.then_inc(s_tr, 1)

            def latent(b):
                pe.wait_ge(s_ht, b + 1)
                if b:
                    pe.wait_ge(s_v, 2 * b)
                for half in range(2):
                    h = hT[:, b * S + half * HALF:b * S + (half + 1) * HALF]
                    mm((B4, B5)[half][0:LAT, :], attnw[:, A_WL0:A_WL0 + LAT], h, start=True, stop=True).then_inc(s_lat, 1)

            def queries(b):
                if b:
                    pe.wait_ge(s_qk, 2 * b - 1)
                for half in range(2):
                    h = hT[:, b * S + half * HALF:b * S + (half + 1) * HALF]
                    last = mm(SAB[0][:, half * HALF:(half + 1) * HALF], attnw[:, A_WQ0:A_WQ0 + P], h, start=True, stop=True)
                last.then_inc(s_qmm, 1)

            def keys_values(b):
                pe.wait_ge(s_latsb, 2 * b + 2)
                if b:
                    pe.wait_ge(s_qk, 2 * b)
                for half in range(2):
                    last = mm(SAB[1][:, half * HALF:(half + 1) * HALF], lowrank[:, 0:P],
                              lat[b][:, half * HALF:(half + 1) * HALF], start=True, stop=True)
                last.then_inc(s_kmm, 1)
                for half in range(2):
                    for i in range(BT // 2):
                        t = half * BT // 2 + i
                        last = mm((B4, B5)[half][:, i * P:(i + 1) * P], lat[b][:, t * P:(t + 1) * P], lowrank[:, P:2 * P],
                                  start=True, stop=True)
                    last.then_inc(s_vmm, 1)

            def norms_of(b):
                for n in range(2):
                    pe.wait_ge(s_sq, 2 * b + n + 1)
                    for half in range(2):
                        if b or n:
                            pe.wait_ge(s_nr, (2 * b + n - 1) * 2 + half + 1)
                        mm((B6, B7)[half][0:HEADS, :], consts[:, C_HEAD:C_HEAD + HEADS], SQ[:, n, half * HALF:(half + 1) * HALF],
                           start=True, stop=True).then_inc(s_nb, 1)

            pe.wait_ge(s_small, 16 * SMALL)
            pe.wait_ge(s_wts, 16 * WTS)
            pe.wait_ge(s_mod, 1)
            turn(0)
            latent(0)
            queries(0)
            turn(1)
            keys_values(0)
            pe.wait_ge(s_ht, 2)
            norms_of(0)
            latent(1)
            queries(1)
            keys_values(1)
            norms_of(1)
            pe.wait_ge(s_scb, 1)
            pe.wait_ge(s_qk, 2 * B)
            for l in range(2):
                for kind, c in enumerate((2, 5, 4, 3)):
                    for b in range(B):
                        o = ((l * 2 + kind % 2) * B + b) * P
                        last = mm(SAB[kind // 2][:, o:o + P], silu_cb[:, l * B + b, :], wmod[:, l, c * P:(c + 1) * P],
                                  start=True, stop=True)
            last.then_inc(s_rowmm, 1)
            pe.wait_ge(s_nt, 1)
            pe.transpose(B6[0:1, 0:HEADS], norm_s[:, 0:1], ident[0:HEADS, 0:HEADS]).then_inc(s_ntr, 1)

            pe.wait_ge(s_row, 2)
            pe.wait_ge(s_v, 2 * B)
            pe.wait_ge(s_flag, 1)
            flag = pe.value_load(need_max[0:1, 0:1], min_val=0, max_val=1)
            with pe.If(flag != 0):
                with pe.Fori(0, NG // 2) as i:
                    for k in range(2):
                        g = i * 2 + k
                        pe.wait_ge(s_kqm[k], (i + 1) * (32 * PIECES))
                        for item in range(HG * BT):
                            h, qt = divmod(item, BT)
                            pe.wait_ge(s_mred, g * (HG * BT) + (item + 1))
                            for half in range(2):
                                last = mm(SAB[item % 2][:, half * HALF:(half + 1) * HALF],
                                          Qb[0:KR, k, h * S + qt * P:h * S + (qt + 1) * P],
                                          Kb[0:KR, k, h * S + half * HALF:h * S + (half + 1) * HALF], start=True, stop=True)
                            last.then_inc(s_mm, 1)
                        pe.wait_ge(s_mred, g * (HG * BT) + (HG * BT + 2))
                        pe.transpose(B4[0:HG * BT, 0:P], mx[:, k, :], ident).then_inc(s_mtr, 1)

            pe.wait_ge(s_sel, 1)
            with pe.Fori(0, NG // GI) as i:
                def spread_den(r):
                    pe.wait_ge(s_pl, i * (2 * GI) + (r + 1))
                    mm((B4, B5)[r % 2][:, :], sel_r, PV_hi, start=True, stop=False)
                    mm((B4, B5)[r % 2][:, :], sel_r, PV_lo, start=False, stop=True).then_inc(s_den, 1)

                for v in range(GI * ATT_UNITS + 1):
                    if v < GI * ATT_UNITS:
                        k, qh, kt = v // ATT_UNITS, v // BT % 2, v % BT
                        if v % ATT_UNITS == 0:
                            pe.wait_ge(s_kq[k % 2], (i * (GI // 2) + (k // 2 + 1)) * (32 * (PIECES + 1)))
                        for pair in range(2):
                            n = 2 * v + pair
                            pe.wait_ge(s_ex, i * (2 * GI * ATT_UNITS) + ((2, 3, 1)[n] if n < 3 else n + 1))
                            for h in (2 * pair, 2 * pair + 1):
                                last = mm(SAB[n % 3][:, (h % 2) * HALF:(h % 2 + 1) * HALF],
                                          Kb[0:KM, k % 2, h * S + kt * P:h * S + (kt + 1) * P],
                                          Qb[0:KM, k % 2, h * S + qh * HALF:h * S + (qh + 1) * HALF], start=True, stop=True)
                            last.then_inc(s_st, 1)
                    if v:
                        u = v - 1
                        k, qh, kt = u // ATT_UNITS, u // BT % 2, u % BT
                        if u % ATT_UNITS == 0:
                            pe.wait_ge(s_vg, i * GI + (k + 1))
                        if kt == 0:
                            pe.wait_ge(s_denr, i * (2 * GI) + (u // BT + 1))
                        pe.wait_ge(s_ex, i * (2 * GI * ATT_UNITS) + (2 * u + 5))
                        for h in range(HG):
                            last = mm((B4, B5)[qh][32 * h:32 * h + 32, :], Vg[:, k % 2, kt, h, :], PR[:, u % 4, h, :],
                                      start=(kt == 0), stop=(kt == BT - 1))
                        last.then_inc(s_pv, 1)
                        if kt == 3 and u >= BT:
                            spread_den(u // BT - 1)
                spread_den(GI * ATT_UNITS // BT - 1)

            pe.wait_ge(s_wog, 2 * B)
            for b in range(B):
                pe.wait_ge(s_at, 2 * GB * (b + 1))
                for t in range(BT):
                    bank = ((B4, B5) if b else (SAB[1][:, 0:HALF], SAB[1][:, HALF:2 * HALF]))[t // 4]
                    for g in range(GB):
                        last = mm(bank[:, (t % 4) * P:(t % 4 + 1) * P], At[:, b * GB + g, t * P:(t + 1) * P],
                                  wo0g[:, b, g, :], start=(g == 0), stop=(g == GB - 1))
                last.then_inc(s_wo, 1)

            def router(layer, b):
                pe.wait_ge(s_ht, (2 * layer + 1) * B + b + 1)
                for t in range(b * BT, (b + 1) * BT):
                    c = (A_RT0, A_RT1)[layer]
                    last = mm(logit_bank[layer][:, t * E:(t + 1) * E], hT[:, t * P:(t + 1) * P], attnw[:, c:c + E],
                              start=True, stop=True)
                if b == B - 1:
                    last.then_inc(s_lg, 1)

            def count_pairs(layer):
                pe.wait_ge(s_ch, layer + 1)
                pe.wait_ge(s_ht, (2 * layer + 2) * B)
                for n, c in enumerate((C_TRI, C_ONES)):
                    last = mm(B6[:, n * P:(n + 1) * P], consts[:, c:c + P], gate_w[:, 9].rearrange("p t e -> p (t e)"),
                              start=True, stop=True)
                last.then_inc(s_cnt, 1)

            def invert_slots(layer):
                pe.wait_ge(s_oh, layer + 1)
                pe.wait_ge(s_ohp, layer + 1)
                for n in range(TOP * NT):
                    last = mm(B7[:, 0:2 * MT], is_lane[:, n, :], in_tile[:, n, :, :].rearrange("p w j -> p (w j)"),
                              start=(n == 0), stop=(n == TOP * NT - 1))
                last.then_inc(s_im, 1)

            def expert_tiles(layer):
                up, down = ((W0up, W0dn), (W1, W1))[layer]
                o = (0, FF)[layer]
                expert = {}

                def load_expert(i, k):
                    return pe.value_load(tile_i[0:1, bass.ds(i * ROUND + k, 1)], min_val=0, max_val=E - 1)

                def turn_in(i, k):
                    pe.wait_ge(s_xg[layer][k % AHEAD], i * (ROUND // AHEAD * 16) + (k // AHEAD + 1) * 16)
                    if not isinstance(i, int) or i * ROUND + k:
                        pe.wait_ge(s_xte[layer], i * ROUND + k)
                    pe.transpose(B6[:, 0:P], Xg[:, k % AHEAD, :], ident).then_inc(s_xt[layer], 1)

                def up_products(i, k):
                    e = expert[k % ROUND] = load_expert(i, k)
                    pe.wait_ge(s_xte[layer], i * ROUND + (k + 1))
                    if not isinstance(i, int) or i * ROUND + k >= 2:
                        pe.wait_ge(s_hh[layer], i * ROUND + (k - 1))
                    if layer == 0:
                        banks = ((SAB[0][:, 0:HALF], SAB[0][:, HALF:2 * HALF]), (B4[:, :], B5[:, :]))[k % 2]
                    else:
                        banks = (SAB[0][:, (k % 2) * HALF:(k % 2 + 1) * HALF],)
                    for n, bank in enumerate(banks):
                        mm(bank, XgT[:, k % RING, :], up[:, bass.ds(e, 1), n * FF:(n + 1) * FF].rearrange("p e w -> p (e w)"),
                           start=True, stop=True).then_inc((s_g, s_u)[n][layer], 1)

                def down_product(i, k):
                    pe.wait_ge(s_hre[layer], i * ROUND + (k + 1))
                    if not isinstance(i, int) or i * ROUND + k:
                        pe.wait_ge(s_ys[layer], i * ROUND + k)
                    for f in range(FC):
                        last = mm(SAB[1][:, HALF:HALF + P], hidT[:, k % 2, f * P:(f + 1) * P],
                                  down[:, bass.ds(expert[k % ROUND], 1), o + f * P:o + (f + 1) * P].rearrange("p e w -> p (e w)"),
                                  start=(f == 0), stop=(f == FC - 1))
                    last.then_inc(s_dn[layer], 1)

                def turn_hidden(i, k):
                    pe.wait_ge(s_hh[layer], i * ROUND + (k + 1))
                    for f in range(FC):
                        last = pe.transpose(SAB[1][:, f * P:(f + 1) * P], hid[:, k % 2, f * P:(f + 1) * P], ident)
                    last.then_inc(s_hr[layer], 1)

                def unit(i, k):
                    j = i * ROUND + k if isinstance(i, int) else ROUND
                    if j < MT:
                        up_products(i, k)
                    if j >= 2:
                        down_product(i, k - 2)
                    if 1 <= j < MT + 1:
                        turn_hidden(i, k - 1)
                    if j + 2 < MT:
                        turn_in(i, k + 2)

                pe.wait_ge(s_idx, layer + 1)
                for k in range(2):
                    turn_in(0, k)
                for k in range(ROUND):
                    unit(0, k)
                with pe.Fori(1, MT // ROUND) as i:
                    for k in (ROUND - 2, ROUND - 1):
                        expert[k] = load_expert(i, k - ROUND)
                    for k in range(ROUND):
                        unit(i, k)
                for k in (ROUND - 2, ROUND - 1):
                    expert[k] = load_expert(MT // ROUND, k - ROUND)
                for k in range(MT % ROUND + 2):
                    unit(MT // ROUND, k)

            for b in range(B):
                turn(B + b)
                router(0, b)
            count_pairs(0)
            pe.wait_ge(s_gate, 1)
            for b in range(B):
                if b:
                    pe.wait_ge(s_gts, b)
                for t in range(BT):
                    last = pe.transpose(SAB[1][0:E, t * P:(t + 1) * P], GT[:, :, b * BT + t], ident)
                last.then_inc(s_gtr, 1)
                pe.wait_ge(s_gts, b + 1)
                if b:
                    pe.wait_ge(s_acc0, b)
                for t in range(BT):
                    last = mm((B4, B5)[t // 4][:, (t % 4) * P:(t % 4 + 1) * P], gT[:, t * P:(t + 1) * P], w2b[:, :],
                              start=True, stop=True)
                last.then_inc(s_b2, 1)
            invert_slots(0)
            pe.wait_ge(s_w0u, 16 * (E // 2))
            pe.wait_ge(s_w0d, 16)
            pe.wait_ge(s_acc0, B)
            keep_warm(9)
            expert_tiles(0)

            def queries(b):
                pe.wait_ge(s_ht, 2 * B + b + 1)
                if b:
                    pe.wait_ge(s_qe, b)
                for half in range(2):
                    last = mm(SAB[0][:, half * HALF:(half + 1) * HALF], attnw[:, A_WQ1:A_WQ1 + P],
                              hT[:, b * S + half * HALF:b * S + (half + 1) * HALF], start=True, stop=True)
                last.then_inc(s_q1, 1)

            def keys_values(b):
                if b:
                    pe.wait_ge(s_kvt, b)
                for t in range(BT):
                    dst = SAB[1][:, t * 2 * P:(t + 1) * 2 * P] if t < 4 else (B4, B5)[(t - 4) // 2][:, (t % 2) * 2 * P:(t % 2 + 1) * 2 * P]
                    last = mm(dst, hT[:, b * S + t * P:b * S + (t + 1) * P], attnw[:, A_WKV1:A_WKV1 + 2 * P],
                              start=True, stop=True)
                last.then_inc(s_kv1, 1)

            def sum_keys_values(b):
                KF, KVt = attn1[b][4:6]
                pe.wait_ge(s_kf, b + 1)
                if b:
                    pe.wait_ge(s_oe, b)
                for t in range(BT):
                    last = mm(B6[:, 0:P + 1], KF[:, t, :], KVt[:, t, P:2 * P + 1], start=(t == 0), stop=(t == BT - 1))
                last.then_inc(s_kvm, 1)

            def outputs(b):
                QF, KVB = attn1[b][2], attn1[b][6]
                pe.wait_ge(s_kvb, b + 1)
                pe.wait_ge(s_qf, b + 1)
                pe.wait_ge(s_qe, B)
                for t in range(BT):
                    mm(SAB[b][:, t * P:(t + 1) * P], QF[:, t * P:(t + 1) * P], KVB[:, 0:P], start=True, stop=True)
                    last = mm(B7[:, t * HEADS:(t + 1) * HEADS], QF[:, t * P:(t + 1) * P], KVB[:, P:P + HEADS],
                              start=True, stop=True)
                last.then_inc(s_nn, 1)

            def turn_outputs(b):
                pe.wait_ge(s_ot, b + 1)
                for t in range(BT):
                    last = pe.transpose(((B6, B7), (B4, B5))[b][t // 4][:, (t % 4) * P:(t % 4 + 1) * P], attn1[b][0][:, t * P:(t + 1) * P],
                                        ident)
                last.then_inc(s_ott, 1)

            def project(b):
                pe.wait_ge(s_oe, b + 1)
                for t in range(BT):
                    last = mm(SAB[b][:, t * P:(t + 1) * P], attn1[b][1][:, t * P:(t + 1) * P], wo1g[:, b, :],
                              start=True, stop=True)
                last.then_inc(s_wo, 1)

            pe.wait_ge(s_res[0], 1)
            keep_warm(11)
            turn(2 * B)
            queries(0)
            keys_values(0)
            turn(2 * B + 1)
            queries(1)
            keys_values(1)
            sum_keys_values(0)
            outputs(0)
            turn_outputs(0)
            sum_keys_values(1)
            project(0)
            outputs(1)
            keep_warm(8)
            turn_outputs(1)
            project(1)
            def shared_up(v, f):
                pe.wait_ge(s_y, v * FC + f + 1)
                mm(SAB[0][:, (f % 2) * HALF:(f % 2 + 1) * HALF], Wsh[:, f * P:(f + 1) * P], hT[:, v * HALF:(v + 1) * HALF],
                   start=True, stop=True).then_inc(s_gm, 1)

            def shared_down(v, t):
                if t == 0:
                    pe.wait_ge(s_y, v * FC + FC + 2)
                    if v >= 2:
                        pe.wait_ge(s_ac, v - 1)
                for f in range(FC):
                    last = mm((B4, B5)[v % 2][:, t * P:(t + 1) * P], H[:, v % 2, f, t * P:(t + 1) * P],
                              Wsh[:, FF + f * P:FF + (f + 1) * P], start=(f == 0), stop=(f == FC - 1))
                if t == HALF // P - 1:
                    last.then_inc(s_o, 1)

            pe.wait_ge(s_wsh, 16)
            keep_warm(5)
            turn(3 * B)
            pe.wait_ge(s_r1, B)
            router(1, 0)
            shared_up(0, 0)
            shared_up(0, 1)
            turn(3 * B + 1)
            router(1, 1)
            shared_up(0, 2)
            shared_up(0, 3)
            count_pairs(1)
            for t in range(HALF // P):
                shared_down(0, t)
            for v in range(1, NH + 1):
                for j in range(FC):
                    if v < NH:
                        shared_up(v, j)
                    if v > 1:
                        shared_down(v - 1, j)
                if v == 2:
                    invert_slots(1)
            pe.wait_ge(s_w1, 16 * (E // 2))
            expert_tiles(1)


def kernel(**inputs):
    import concourse.bacc as bacc
    from concourse.bass_utils import run_bass_kernel_spmd

    a = {k: np.asarray(v) for k, v in inputs.items()}
    f32 = np.float32

    consts = np.zeros((P, C_END), f32)
    consts[:, C_ID:C_ID + P] = np.eye(P)
    consts[:, C_BLOCK:C_BLOCK + P] = np.kron(np.eye(HEADS), np.ones((DH, DH)))
    for h in range(HG):
        consts[32 * h + DH, C_SEL + 32 * h:C_SEL + 32 * h + 32] = 1
    consts[:, C_IOTA:C_HEAD] = np.tile(np.arange(E), NT)
    consts[:, C_TRI:C_TRI + P] = np.triu(np.ones((P, P)), 1)
    consts[:, C_ONES:C_ONES + P] = 1
    consts[:, C_ROW:C_ROW + P] = np.arange(P)
    consts[:, C_STEP:C_STEP + NT] = np.arange(NT) * P
    consts[:, C_BEFORE:C_BEFORE + E * E] = np.tril(np.ones((E, E)), -1).reshape(-1)
    consts[:, C_PAIR:C_PAIR + TOP * NT] = np.arange(TOP * NT) + 1
    consts[:, C_SPARE:C_SPARE + MT] = P + TOP * T + np.arange(MT) * P + np.arange(P)[:, None]
    consts[:, C_PART] = np.arange(P)

    consts[np.arange(P), C_HEAD + np.arange(P) // (HG * DH) * HG + np.arange(P) % HG] = 1
    def turned(w):
        return w.reshape(w.shape[:-1] + (GB, HG, DH)).swapaxes(-1, -2).reshape(w.shape)

    vecs = np.zeros((P, V_END), f32)
    vecs[:, V_BQ0] = turned(a["L0_attn_bq"])
    vecs[:, V_BK0] = turned(a["L0_attn_bk"])
    vecs[0:LAT, V_BL0] = a["L0_attn_bl"]
    vecs[:, V_BQ1] = a["L1_attn_bq"]
    vecs[:, V_CT:V_CT + B] = a["L0_c"].T
    vecs[:, V_CT + B:V_CT + 2 * B] = a["L1_c"].T
    vecs[:, V_EPS] = EPS_LN
    rows = np.concatenate([a["L0_attn_bv"], a["L1_attn_bk"], a["L1_attn_bv"], a["L1_attn_bo"]])
    rows = np.ascontiguousarray(np.broadcast_to(rows, (P, R_END)))
    attnw = np.concatenate([turned(a["L0_attn_Wq"]), a["L0_attn_Wl"], a["L0_ffn_router_w"].T, a["L1_attn_Wq"],
                            a["L1_attn_Wk"], a["L1_attn_Wv"], a["L1_attn_Wo"], a["L1_ffn_gate_w"].T], axis=1)
    lowrank = np.concatenate([turned(a["L0_attn_Wk"]), a["L0_attn_Wv"]], axis=1)
    wo0 = np.zeros((P, GB, P), f32)
    wo = a["L0_attn_Wo"].reshape(GB, HG, DH, P)
    for h in range(HG):
        wo0[32 * h:32 * h + DH] = wo[:, h].transpose(1, 0, 2)
    wo0[DH, 0] = a["L0_attn_bo"]
    wmod = np.stack([a["L0_wmod"], a["L1_wmod"]], axis=1)

    def up(w):
        return w.transpose(0, 2, 1)

    def down(w):
        return w.transpose(0, 2, 1).reshape(-1, FC, P, P).transpose(0, 2, 1, 3).reshape(-1, P, FF)

    def by_lane(w):
        return w.transpose(1, 0, 2)

    up0 = by_lane(np.concatenate([up(a["L0_ffn_wg_w"]), up(a["L0_ffn_w1_w"])], axis=2))
    down0 = by_lane(down(a["L0_ffn_w2_w"]))
    hb = np.concatenate([a["L0_ffn_wg_b"], a["L0_ffn_w1_b"]], axis=1)
    exp1 = by_lane(np.concatenate([up(a["L1_ffn_experts_w1"]), down(a["L1_ffn_experts_w2"])], axis=2))
    shared1 = np.concatenate([up(a["L1_ffn_shared_w1"][None]), down(a["L1_ffn_shared_w2"][None])], axis=2)[0]

    arrays, args = {}, []
    nc = bacc.Bacc("TRN2", target_bir_lowering=False, num_devices=1)
    for name, x in (("x", a["L0_attn_x"]), ("consts", consts), ("vecs", vecs), ("rows", rows), ("attnw", attnw),
                    ("lowrank", lowrank), ("wo0", wo0), ("wmod", wmod), ("w2b", a["L0_ffn_w2_b"]), ("hb", hb),
                    ("up0", up0), ("down0", down0),
                    ("shared1", shared1), ("exp1", exp1)):
        arrays[name + "_dram"] = np.ascontiguousarray(x)
        args.append(nc.dram_tensor(name + "_dram", x.shape, mybir.dt.from_np(x.dtype), kind="ExternalInput").ap())
    out = nc.dram_tensor("out_dram", (B, S, P), F32, kind="ExternalOutput").ap()
    build(nc, *args, out)
    r = run_bass_kernel_spmd(nc, [arrays], core_ids=[0])
    return r.results[0]["out_dram"]
```
